# Optimizing a Trainium2 kernel written in Bass

```python
import numpy as np
import jax
import jax.numpy as jnp

def _softmax(x, axis=-1):
    return jax.nn.softmax(x, axis=axis)

def _gelu(x):
    return jax.nn.gelu(x, approximate=True)

def _silu(x):
    return jax.nn.silu(x)

def _sigmoid(x):
    return jax.nn.sigmoid(x)

def _layernorm(x, axis=-1, eps=1e-05):
    m = jnp.mean(x, axis=axis, keepdims=True)
    v = jnp.var(x, axis=axis, keepdims=True)
    return (x - m) / jnp.sqrt(v + eps)

def _scatter_add(tgt, idx, src, axis=0):
    return tgt.at[idx].add(src)

def _segment_sum(src, seg, n):
    return jax.ops.segment_sum(src, seg, n)
kernel_name = 'mk_sandwich_d2_jaxref_r8_1e046e'

def setup_inputs(seed: int=0):
    np.random.seed(seed)
    _w = jnp.asarray

    def _L0_attn_setup():
        import jax, jax.numpy as jnp
        import numpy as np
        D_MODEL = 256
        NHEAD = 32
        N_KV = 8
        HEAD_DIM = D_MODEL // NHEAD
        EPS = 1e-05

        def weight_quant(w):
            scale = jnp.maximum(jnp.mean(jnp.abs(w)), EPS)
            return jax.lax.stop_gradient(jnp.sign(w) * scale - w) + w

        def bitlinear(x, w):
            return x @ weight_quant(w).T
        key = jax.random.key(seed)
        k1, k2, k3, k4, k5 = jax.random.split(key, 5)
        B, S = (2, 256)
        return {'x': jax.random.normal(k1, (B, S, D_MODEL), dtype=jnp.float32), 'wq': jax.random.normal(k2, (D_MODEL, D_MODEL), dtype=jnp.float32) * 0.02, 'wk': jax.random.normal(k3, (N_KV * HEAD_DIM, D_MODEL), dtype=jnp.float32) * 0.02, 'wv': jax.random.normal(k4, (N_KV * HEAD_DIM, D_MODEL), dtype=jnp.float32) * 0.02, 'wo': jax.random.normal(k5, (D_MODEL, D_MODEL), dtype=jnp.float32) * 0.02}
    _L0_attn_in = _L0_attn_setup()

    def _L0_ffn_setup():
        import jax, jax.numpy as jnp
        import numpy as np
        B, S, D, H = (4, 256, 256, 1024)

        def fwht(x):
            orig_shape = x.shape
            n = orig_shape[-1]
            x = x.reshape(-1, n)
            h = 1
            while h < n:
                xb = x.reshape(-1, n // (2 * h), 2, h)
                a = xb[:, :, 0, :]
                b = xb[:, :, 1, :]
                x = jnp.stack([a + b, a - b], axis=2).reshape(-1, n)
                h *= 2
            scale = jnp.asarray(1.0 / np.sqrt(n), dtype=x.dtype)
            return (x * scale).reshape(orig_shape)
        key = jax.random.key(seed)
        kx, k1, k2, k3 = jax.random.split(key, 4)
        x = jax.random.normal(kx, (B, S, D), dtype=jnp.float32)
        W1 = jax.random.normal(k1, (H, D), dtype=jnp.float32) * (1.0 / np.sqrt(D))
        W2 = jax.random.normal(k2, (D, H), dtype=jnp.float32) * (1.0 / np.sqrt(H))
        W3 = jax.random.normal(k3, (H, D), dtype=jnp.float32) * (1.0 / np.sqrt(D))
        return {'x': x, 'W1': W1, 'W2': W2, 'W3': W3}
    _L0_ffn_in = _L0_ffn_setup()

    def _L1_attn_setup():
        import jax, jax.numpy as jnp
        import numpy as np
        B, T, D = (4, 512, 256)
        W_SCALE = 0.02
        key = jax.random.key(seed)
        ks = jax.random.split(key, 10)
        x = jax.random.normal(ks[0], (B, T, D), dtype=jnp.float32)
        Wk = jax.random.normal(ks[1], (D, D), dtype=jnp.float32) * W_SCALE
        Wv = jax.random.normal(ks[2], (D, D), dtype=jnp.float32) * W_SCALE
        Wr = jax.random.normal(ks[3], (D, D), dtype=jnp.float32) * W_SCALE
        Wo = jax.random.normal(ks[4], (D, D), dtype=jnp.float32) * W_SCALE
        bk = jnp.zeros((D,), jnp.float32)
        bv = jnp.zeros((D,), jnp.float32)
        br = jnp.zeros((D,), jnp.float32)
        bo = jnp.zeros((D,), jnp.float32)
        tmk = jax.random.uniform(ks[5], (D,), dtype=jnp.float32)
        tmv = jax.random.uniform(ks[6], (D,), dtype=jnp.float32)
        tmr = jax.random.uniform(ks[7], (D,), dtype=jnp.float32)
        u = jax.random.normal(ks[8], (D,), dtype=jnp.float32) * 0.1
        w = jax.random.uniform(ks[9], (D,), dtype=jnp.float32)
        return {'x': x, 'Wk': Wk, 'bk': bk, 'Wv': Wv, 'bv': bv, 'Wr': Wr, 'br': br, 'Wo': Wo, 'bo': bo, 'tmk': tmk, 'tmv': tmv, 'tmr': tmr, 'u': u, 'w': w}
    _L1_attn_in = _L1_attn_setup()

    def _L1_ffn_setup():
        import jax, jax.numpy as jnp
        import numpy as np
        H = 256
        F = 96
        E = 32
        K = 4
        SF = 704
        B, S = (1, 256)

        def _moe_forward(x, gate_w, wg, wu, wd, sg, su, sd, seg):
            T = x.shape[0]
            logits = x @ gate_w
            probs = jax.nn.softmax(logits, axis=-1)
            topw, topi = jax.lax.top_k(probs, K)
            topw = topw / jnp.sum(topw, axis=-1, keepdims=True)
            combine = jnp.zeros((T, E), x.dtype).at[jnp.arange(T)[:, None], topi].set(topw)

            def body(acc, ew):
                wg_e, wu_e, wd_e, c_e = ew
                h = jax.nn.silu(x @ wg_e) * (x @ wu_e)
                return (acc + c_e[:, None] * (h @ wd_e), None)
            out, _ = jax.lax.scan(body, jnp.zeros_like(x), (wg, wu, wd, combine.T))
            shared = jax.nn.silu(x @ sg) * (x @ su) @ sd
            out = out + jax.nn.sigmoid(x @ seg) * shared
            return out
        key = jax.random.key(seed)
        ks = jax.random.split(key, 9)
        rn = lambda k, sh, sc: jax.random.normal(k, sh, jnp.float32) * sc
        return {'hidden_states': rn(ks[0], (B, S, H), 1.0), 'gate_w': rn(ks[1], (H, E), 0.02), 'wg': rn(ks[2], (E, H, F), H ** (-0.5)), 'wu': rn(ks[3], (E, H, F), H ** (-0.5)), 'wd': rn(ks[4], (E, F, H), F ** (-0.5)), 'sg': rn(ks[5], (H, SF), H ** (-0.5)), 'su': rn(ks[6], (H, SF), H ** (-0.5)), 'sd': rn(ks[7], (SF, H), SF ** (-0.5)), 'seg': rn(ks[8], (H, 1), H ** (-0.5))}
    _L1_ffn_in = _L1_ffn_setup()
    _d = {'L0_attn_x': _L0_attn_in['x'], 'L0_attn_wq': _L0_attn_in['wq'], 'L0_attn_wk': _L0_attn_in['wk'], 'L0_attn_wv': _L0_attn_in['wv'], 'L0_attn_wo': _L0_attn_in['wo'], 'L0_ffn_W1': _L0_ffn_in['W1'], 'L0_ffn_W2': _L0_ffn_in['W2'], 'L0_ffn_W3': _L0_ffn_in['W3'], 'L1_attn_Wk': _L1_attn_in['Wk'], 'L1_attn_bk': _L1_attn_in['bk'], 'L1_attn_Wv': _L1_attn_in['Wv'], 'L1_attn_bv': _L1_attn_in['bv'], 'L1_attn_Wr': _L1_attn_in['Wr'], 'L1_attn_br': _L1_attn_in['br'], 'L1_attn_Wo': _L1_attn_in['Wo'], 'L1_attn_bo': _L1_attn_in['bo'], 'L1_attn_tmk': _L1_attn_in['tmk'], 'L1_attn_tmv': _L1_attn_in['tmv'], 'L1_attn_tmr': _L1_attn_in['tmr'], 'L1_attn_u': _L1_attn_in['u'], 'L1_attn_w': _L1_attn_in['w'], 'L1_ffn_gate_w': _L1_ffn_in['gate_w'], 'L1_ffn_wg': _L1_ffn_in['wg'], 'L1_ffn_wu': _L1_ffn_in['wu'], 'L1_ffn_wd': _L1_ffn_in['wd'], 'L1_ffn_sg': _L1_ffn_in['sg'], 'L1_ffn_su': _L1_ffn_in['su'], 'L1_ffn_sd': _L1_ffn_in['sd'], 'L1_ffn_seg': _L1_ffn_in['seg']}
    _x0 = _d['L0_attn_x']
    _d['L0_attn_x'] = jax.random.normal(jax.random.fold_in(jax.random.key(seed), 1), (2, 512, 256), dtype=_x0.dtype)
    del _x0
    return _d

def reference(L0_attn_x, L0_attn_wq, L0_attn_wk, L0_attn_wv, L0_attn_wo, L0_ffn_W1, L0_ffn_W2, L0_ffn_W3, L1_attn_Wk, L1_attn_bk, L1_attn_Wv, L1_attn_bv, L1_attn_Wr, L1_attn_br, L1_attn_Wo, L1_attn_bo, L1_attn_tmk, L1_attn_tmv, L1_attn_tmr, L1_attn_u, L1_attn_w, L1_ffn_gate_w, L1_ffn_wg, L1_ffn_wu, L1_ffn_wd, L1_ffn_sg, L1_ffn_su, L1_ffn_sd, L1_ffn_seg):

    def _L0_attn_ref(x, wq, wk, wv, wo):
        import jax, jax.numpy as jnp
        import numpy as np
        D_MODEL = 256
        NHEAD = 32
        N_KV = 8
        HEAD_DIM = D_MODEL // NHEAD
        EPS = 1e-05

        def weight_quant(w):
            scale = jnp.maximum(jnp.mean(jnp.abs(w)), EPS)
            return jax.lax.stop_gradient(jnp.sign(w) * scale - w) + w

        def bitlinear(x, w):
            return x @ weight_quant(w).T
        B, S, _ = x.shape
        G = NHEAD // N_KV
        q = bitlinear(x, wq).reshape(B, S, N_KV, G, HEAD_DIM)
        k = bitlinear(x, wk).reshape(B, S, N_KV, HEAD_DIM)
        v = bitlinear(x, wv).reshape(B, S, N_KV, HEAD_DIM)
        sm_scale = 1.0 / jnp.sqrt(jnp.asarray(HEAD_DIM, dtype=x.dtype))
        scores = jnp.einsum('bskgd,btkd->bkgst', q, k) * sm_scale
        causal = jnp.tril(jnp.ones((S, S), dtype=bool))
        scores = jnp.where(causal, scores, jnp.asarray(-jnp.inf, dtype=scores.dtype))
        probs = jax.nn.softmax(scores, axis=-1)
        out = jnp.einsum('bkgst,btkd->bskgd', probs, v)
        out = out.reshape(B, S, D_MODEL)
        return bitlinear(out, wo)

    def _L0_ffn_ref(x, W1, W2, W3):
        import jax, jax.numpy as jnp
        import numpy as np
        B, S, D, H = (4, 256, 256, 1024)

        def fwht(x):
            orig_shape = x.shape
            n = orig_shape[-1]
            x = x.reshape(-1, n)
            h = 1
            while h < n:
                xb = x.reshape(-1, n // (2 * h), 2, h)
                a = xb[:, :, 0, :]
                b = xb[:, :, 1, :]
                x = jnp.stack([a + b, a - b], axis=2).reshape(-1, n)
                h *= 2
            scale = jnp.asarray(1.0 / np.sqrt(n), dtype=x.dtype)
            return (x * scale).reshape(orig_shape)
        up_gate = jnp.einsum('bsd,hd->bsh', x, W1)
        up_lin = jnp.einsum('bsd,hd->bsh', x, W3)
        hidden = jax.nn.silu(up_gate) * up_lin
        hidden = fwht(hidden)
        out = jnp.einsum('bsh,dh->bsd', hidden, W2)
        return out

    def _L1_attn_ref(x, Wk, bk, Wv, bv, Wr, br, Wo, bo, tmk, tmv, tmr, u, w):
        import jax, jax.numpy as jnp
        import numpy as np
        B, T, D = (4, 512, 256)
        W_SCALE = 0.02
        xs = jnp.pad(x, ((0, 0), (1, 0), (0, 0)))[:, :-1]
        k = x * tmk + xs * (1.0 - tmk)
        v = x * tmv + xs * (1.0 - tmv)
        r = jax.nn.silu(x * tmr + xs * (1.0 - tmr))
        k = jnp.einsum('btd,ed->bte', k, Wk) + bk
        v = jnp.einsum('btd,ed->bte', v, Wv) + bv
        r = jnp.einsum('btd,ed->bte', r, Wr) + br

        def step(carry, kv_t):
            a, b = carry
            k_t, v_t = kv_t
            t = jnp.maximum(u + k_t, w)
            e1 = jnp.exp(-w - t)
            e2 = jnp.exp(u + k_t - t)
            a = e1 * a + e2 * v_t
            b = e1 * b + e2
            return ((a, b), a / b)
        a0 = jnp.zeros((x.shape[0], x.shape[2]), x.dtype)
        b0 = jnp.zeros_like(a0)
        _, wkv = jax.lax.scan(step, (a0, b0), (k.transpose(1, 0, 2), v.transpose(1, 0, 2)))
        wkv = wkv.transpose(1, 0, 2)
        return jnp.einsum('btd,ed->bte', wkv * r, Wo) + bo

    def _L1_ffn_ref(hidden_states, gate_w, wg, wu, wd, sg, su, sd, seg):
        import jax, jax.numpy as jnp
        import numpy as np
        H = 256
        F = 96
        E = 32
        K = 4
        SF = 704
        B, S = (1, 256)

        def _moe_forward(x, gate_w, wg, wu, wd, sg, su, sd, seg):
            T = x.shape[0]
            logits = x @ gate_w
            probs = jax.nn.softmax(logits, axis=-1)
            topw, topi = jax.lax.top_k(probs, K)
            topw = topw / jnp.sum(topw, axis=-1, keepdims=True)
            combine = jnp.zeros((T, E), x.dtype).at[jnp.arange(T)[:, None], topi].set(topw)

            def body(acc, ew):
                wg_e, wu_e, wd_e, c_e = ew
                h = jax.nn.silu(x @ wg_e) * (x @ wu_e)
                return (acc + c_e[:, None] * (h @ wd_e), None)
            out, _ = jax.lax.scan(body, jnp.zeros_like(x), (wg, wu, wd, combine.T))
            shared = jax.nn.silu(x @ sg) * (x @ su) @ sd
            out = out + jax.nn.sigmoid(x @ seg) * shared
            return out
        b, s, h = hidden_states.shape
        x = hidden_states.reshape(-1, h)
        out = _moe_forward(x, gate_w, wg, wu, wd, sg, su, sd, seg)
        return out.reshape(b, s, h)
    x = L0_attn_x
    x = x + _layernorm(_L0_attn_ref(_layernorm(x, axis=-1), L0_attn_wq, L0_attn_wk, L0_attn_wv, L0_attn_wo), axis=-1)
    x = x + _layernorm(_L0_ffn_ref(_layernorm(x, axis=-1), L0_ffn_W1, L0_ffn_W2, L0_ffn_W3), axis=-1)
    x = x + _layernorm(_L1_attn_ref(_layernorm(x, axis=-1), L1_attn_Wk, L1_attn_bk, L1_attn_Wv, L1_attn_bv, L1_attn_Wr, L1_attn_br, L1_attn_Wo, L1_attn_bo, L1_attn_tmk, L1_attn_tmv, L1_attn_tmr, L1_attn_u, L1_attn_w), axis=-1)
    x = x + _layernorm(_L1_ffn_ref(_layernorm(x, axis=-1), L1_ffn_gate_w, L1_ffn_wg, L1_ffn_wu, L1_ffn_wd, L1_ffn_sg, L1_ffn_su, L1_ffn_sd, L1_ffn_seg), axis=-1)
    return x

_drawn_inputs = setup_inputs


def setup_inputs(seed=0):
    import zlib

    import numpy as np

    out = dict(_drawn_inputs(seed))
    spreads = {'L1_attn_bk': (0.0, 0.693),
     'L1_attn_bv': (0.0, 0.1),
     'L1_attn_br': (0.0, 0.1),
     'L1_attn_bo': (0.0, 0.1)}
    factors = {'L1_attn_tmk': 4.343, 'L1_attn_u': 6.038}
    for name, (base, spread) in spreads.items():
        noise = np.random.default_rng([zlib.crc32(name.encode()), seed]).standard_normal(out[name].shape)
        drawn = base * np.exp(spread * noise) if base else spread * noise
        out[name] = jnp.asarray(drawn.astype(out[name].dtype))
    for name, factor in factors.items():
        out[name] = (out[name] * factor).astype(out[name].dtype)
    return out
```

```python
from contextlib import ExitStack, contextmanager

import numpy as np

import concourse.bass as bass
from concourse import mybir

F32 = mybir.dt.float32
F32R = mybir.dt.float32r
BF16 = mybir.dt.bfloat16
U32 = mybir.dt.uint32
ALU = mybir.AluOpType
ACT = mybir.ActivationFunctionType
AX = mybir.AxisListType

P = 128
D = 256
DC = D // P
B, T = 2, 512
N = B * T
TILES = N // P
TPB = T // P
NKV, GQ, HD = 8, 4, 8
NG = B * NKV
HID = 1024
HC = HID // P
E, TOPK, F, SF = 32, 4, 96, 704
MC = -(-(E * F + SF) // P)
RW = 34
TMR, TMK, TMV, UK, WD, BK, BV, BR = range(8)
LN_EPS = 1e-5
QUANT_EPS = 1e-5
MASKED = -1e30


class Chain:

    def __init__(self, eng, sem):
        self.eng, self.sem, self.n, self.off = eng, sem, 0, 0

    def step(self, ins):
        ins.then_inc(self.sem, 1)
        self.n += 1
        return ins

    def settle(self):
        self.eng.wait_ge(self.sem, self.off + self.n)

    @contextmanager
    def loop(self, count, per):
        before = self.n
        with self.eng.Fori(0, count) as i:
            self.off = i * per
            yield i
            assert self.n - before == per, (self.n - before, per)
        self.off, self.n = 0, before + count * per


def need(eng, sem, value):
    if not isinstance(value, int) or value > 0:
        eng.wait_ge(sem, value)


def sandwich_kernel(nc, x, consts, wq, wk, wv, wo, w1, w3, w2, mix_w, vecs, bo, route_w, moe_w,
                    select, out):
    ctx = ExitStack()
    with ctx:
        def sem(name):
            return ctx.enter_context(nc.semaphore(name))

        at = [(nc.sbuf_base + 31) // 32 * 32]
        SIZE = {F32: 4, F32R: 4, BF16: 2, U32: 4}

        def sb(name, shape, dt):
            size = int(np.prod(shape[1:])) * SIZE[dt]
            t = nc.alloc_sbuf_tensor_at(name, shape, dt, offset=at[0])
            at[0] += (size + 31) // 32 * 32
            assert at[0] <= nc.sbuf_usable_end, (name, at[0])
            return t

        xa = sb("xa", [P, TILES, D], F32)
        xb = sb("xb", [P, TILES, D], F32)
        ident = sb("ident", [P, P], F32)
        identb = sb("identb", [P, P], BF16)
        had = sb("had", [P, P], F32)
        hadr = sb("hadr", [P, P], F32R)
        ones = sb("ones", [P, P], F32)
        zero = sb("zero", [P, 1, 1], F32)
        hide_cols = sb("hide_cols", [P, P], BF16)
        hide_rows = sb("hide_rows", [P, P], BF16)
        halfneg = sb("halfneg", [P, TILES], F32)
        st6 = sb("st6", [P, TILES, 6], F32)
        mv = sb("mv", [P, TILES, 2], F32)
        ve = sb("ve", [P, TILES], F32)
        rstd = sb("rstd", [P, TILES], F32)
        nmr = sb("nmr", [P, TILES], F32)
        asum = sb("asum", [P, 4], F32)
        wsc = sb("wsc", [P, 4], F32)
        qsc = sb("qsc", [P, 1], F32)
        wsg_at = at[0]
        wsg = sb("wsg", [P, 4, DC * D], F32R)
        w2hi = sb("w2hi", [P, HC, D], F32R)
        w2lo = sb("w2lo", [P, HC, D], F32R)
        att = sb("att", [P, NG * TPB * 32], F32)
        vec = sb("vec", [P, 8, DC], F32)
        omt = sb("omt", [P, 3, DC], F32)
        ubk = sb("ubk", [P, DC], F32)
        ubw = sb("ubw", [P, DC], F32)
        nwd = sb("nwd", [P, DC], F32)
        so2 = sb("so2", [P, 1], F32)

        def place(start, *wanted):
            at[0] = start
            made = [sb(*w) for w in wanted]
            return made, at[0]

        region = at[0]
        (q_all, k_all, v_all), stage = place(
            region, ("q_all", [P, NG * GQ * T], BF16), ("k_all", [P, NG * T], BF16),
            ("v_all", [P, NG * TPB * 32], F32))
        (probs, v_now, o_cols), end = place(
            stage, ("probs", [P, 2, 10, T], F32), ("v_now", [P, 2, TPB, 32], F32),
            ("o_cols", [P, 2, T], F32))
        (negm, negr, m3, mrow, rsum), region_end = place(
            end, ("negm", [P, 2, TPB, GQ], F32), ("negr", [P, 2, TPB, GQ], F32),
            ("m3", [P, 2, TPB, 3, GQ], BF16), ("mrow", [3 * GQ, 2, T], BF16),
            ("rsum", [P, 2, TPB, GQ], F32))
        (xn0, cols0_hi, cols0_lo, w2b, wraw, qf), end = place(
            stage, ("xn0", [P, TPB, D], F32), ("cols0_hi", [P, DC, N], F32R),
            ("cols0_lo", [P, DC, N], F32R), ("w2b", [P, HC, D], F32),
            ("wraw", [P, 4, DC * D], F32), ("qf", [P, DC, T], F32))
        assert end <= region_end
        (qparts, kf, kparts, w2a), _ = place(
            region_end, ("qparts", [P, 3, DC, T], BF16), ("kf", [64, T], F32),
            ("kparts", [64, 3, T], BF16), ("w2a", [P, HC, D], F32))
        (w1hi, w3hi, w1lo, w3lo), half_q = place(
            region, ("w1hi", [P, DC, HID], F32R), ("w3hi", [P, DC, HID], F32R),
            ("w1lo", [P, DC, HID], F32R), ("w3lo", [P, DC, HID], F32R))
        (w1raw, w3raw), _ = place(half_q - 2 * DC * HID * 4, ("w1raw", [P, DC, HID], F32),
                                  ("w3raw", [P, DC, HID], F32))
        (cols_hi, cols_lo, rows, rwhi, rwlo, sg, hf, select_sb), end = place(
            half_q, ("cols_hi", [P, DC, N], F32R), ("cols_lo", [P, DC, N], F32R),
            ("rows", [P, TILES, D], F32), ("rwhi", [P, 4, DC, D], F32R),
            ("rwlo", [P, 4, DC, D], F32R), ("sg", [P, 2, T], F32), ("hf", [P, 2, T], F32),
            ("select_sb", [P, MC * P], BF16))
        assert end <= stage
        (rwraw,), _ = place(half_q + 4 * DC * N * 4, ("rwraw", [P, 4, DC, D], F32))
        (h_hi, h_lo, xT, mix, mixed, m_hi, m_lo, ct, mslot_hi, mslot_lo, iota), end = place(
            stage, ("h_hi", [P, 2, T], F32R), ("h_lo", [P, 2, T], F32R),
            ("xT", [P, DC, B, T + 1], F32), ("mix", [P, DC, T], F32), ("mixed", [P, 2, DC, T], F32),
            ("m_hi", [P, 3, DC, T], F32R), ("m_lo", [P, 3, DC, T], F32R),
            ("ct", [P, N], BF16), ("mslot_hi", [P, 2, 3 * D], F32R),
            ("mslot_lo", [P, 2, 3 * D], F32R), ("iota", [P, E], F32))
        (gate_hi, gate_lo, bo_sb), end = place(
            end, ("gate_hi", [P, DC, RW], F32R), ("gate_lo", [P, DC, RW], F32R),
            ("bo_sb", [P, D], F32))
        (gate_raw,), end = place(end, ("gate_raw", [P, DC, RW], F32))
        (decay_in, decay, gain, gained, num, den), end = place(
            region, *[(n, [P, DC, T], F32)
                      for n in ("decay_in", "decay", "gain", "gained", "num", "den")])
        (logits, top8, topi, topf, wtop, wsum, comb, eq, cb), end = place(
            end, ("logits", [P, TILES, RW], F32), ("top8", [P, TILES, 8], F32),
            ("topi", [P, TILES, 8], U32), ("topf", [P, TILES, 8], F32),
            ("wtop", [P, TILES, TOPK + 1], F32), ("wsum", [P, TILES, 2], F32),
            ("comb", [P, TPB, E + 1], F32), ("eq", [P, TPB, E], F32), ("cb", [P, TPB, P], BF16))
        assert end <= half_q
        mraw_at = wsg_at
        (mraw,), _ = place(mraw_at, ("mraw", [P, 2, 3 * D], F32))

        ps = ctx.enter_context(nc.psum_tensor("ps", [P, 8, 512], F32))
        q_dram = nc.dram_tensor("q_parts_scratch", (3, D, N), BF16).ap()
        k_dram = nc.dram_tensor("k_parts_scratch", (3, NKV * HD, N), BF16).ap()

        x_rows = x.rearrange("(t p) d -> p t d", p=P)
        out_rows = out.rearrange("(t p) d -> p t d", p=P)

        s_x = [sem("x0_loaded"), sem("x1_loaded")]
        s_const = sem("consts_loaded")
        s_constb = sem("bf16_consts_loaded")
        s_w = sem("attn_weights_loaded")
        s_dve = sem("vector_order")
        s_act = sem("scalar_order")
        s_pool = sem("pool_order")
        s_ready = sem("pool_constants_ready")
        ln_var = sem("ln_variance_ready")
        ln_rstd = sem("ln_rstd_ready")
        ln_rows = sem("ln_rows_ready")
        tr_done = sem("rows_transposed")
        hi_done = sem("cols_hi_ready")
        lo_done = sem("cols_lo_ready")
        s_abs = sem("weight_abs_sums_ready")
        s_tot = sem("weight_totals_ready")
        s_sign = sem("weight_signs_ready")
        s_scale = sem("weight_scales_ready")
        q_mm = sem("q_product_done")
        kv_mm = sem("kv_product_done")
        q_scaled = sem("q_scaled")
        k_scaled = sem("k_scaled")
        v_stored = sem("v_stored")
        q_split0 = sem("q_chunk0_split")
        q_split1 = sem("q_chunk1_split")
        k_split = sem("k_split")
        q_spilled = sem("q_parts_in_dram")
        k_spilled = sem("k_parts_in_dram")
        q_in = [sem("q_even_group_loaded"), sem("q_odd_group_loaded")]
        k_in = [sem("k_batch0_loaded"), sem("k_batch1_loaded")]
        s1_full = sem("score_rows_full")
        s1_read = sem("score_rows_read")
        msplit = sem("max_split")
        mt_full = sem("max_rows_full")
        mrow_ready = sem("max_rows_ready")
        m_in = [sem("max_rows_even_loaded"), sem("max_rows_odd_loaded")]
        st_full = sem("score_cols_full")
        st_exp = sem("probs_ready")
        v_ready = sem("v_group_ready")
        pv_done = sem("pv_done")
        o_copied = sem("o_copied")
        ot_full = sem("o_rows_full")
        att_ready = sem("att_rows_ready")
        s_w2 = sem("w2_loaded")
        butterfly = sem("w2_butterfly_done")
        w2_split = sem("w2_split")
        w2_mm = sem("w2_hadamard_done")
        w2_hi_done = sem("w2_hi_ready")
        w2_lo_done = sem("w2_lo_ready")
        s_vec = sem("vectors_loaded")
        s_post = sem("post_attention_weights_loaded")
        s_rw = sem("mix_weights_loaded")
        s_tail = sem("routing_weights_and_vectors_loaded")
        s_select = sem("select_loaded")
        w13_hi = sem("w1_w3_hi_ready")
        w13_lo = sem("w1_w3_lo_ready")
        rw_hi = sem("mix_weights_hi_ready")
        rw_lo = sem("mix_weights_lo_ready")
        gate_split = sem("routing_weights_split")
        z_done = sem("z_done")
        z_ready = sem("z_scale_ready")
        z_norm = sem("z_normalised")
        x_new = sem("residual_ready")
        rows_ready = sem("rows_ready")
        cols_full = sem("cols_in_psum")
        cols_h = sem("cols_hi_done")
        cols_l = sem("cols_lo_done")
        up_g = sem("gate_product_done")
        up_u = sem("linear_product_done")
        silu_done = sem("silu_done")
        mul_done = sem("gated")
        h_hi_done = sem("hidden_hi_ready")
        h_lo_done = sem("hidden_lo_ready")
        down_done = sem("down_product_done")
        xt_ready = sem("xT_ready")
        xt_zero = sem("xT_start_zeroed")
        mix_tmp = sem("shifted_mix_ready")
        mix_done = sem("mix_ready")
        mix_silu = sem("receptance_silu_ready")
        mix_hi = sem("mix_hi_ready")
        mix_lo = sem("mix_lo_ready")
        proj_k = sem("key_projection_done")
        proj_v = sem("value_projection_done")
        proj_r = sem("receptance_projection_done")
        k_read = sem("key_projection_read")
        decay_done = sem("decay_ready")
        gain_done = sem("gain_ready")
        v_read = sem("value_projection_read")
        wkv_done = sem("wkv_ready")
        wkv_hi = sem("wkv_hi_ready")
        wkv_lo = sem("wkv_lo_ready")
        z_biased = sem("z_biased")
        route_mm = sem("routing_logits_done")
        route_ex = sem("routing_exponent_ready")
        route_exp = sem("routing_exp_done")
        route_rows = sem("routing_rows_ready")
        route_t = sem("routing_transposed")
        route_cols = sem("routing_cols_ready")
        m_loaded = [sem("expert_even_loaded"), sem("expert_odd_loaded")]
        m_hi_ready = sem("expert_hi_ready")
        m_lo_ready = sem("expert_lo_ready")
        bc_full = sem("routing_broadcast_done")
        t_done = sem("hidden_product_done")
        s_out = sem("out_stored")

        UNITS = ([(3, h, 1) for h in range(4)] + [(2, h, 1) for h in range(4)]
                 + [(1, 0, 2), (1, 2, 2), (0, 0, 2), (0, 2, 2)])
        PIECES = ([[(0, h, 0)] for h in range(4)] + [[(1, h, 0), (3, h, 384)] for h in range(4)]
                  + [[(2, 0, 0), (2, 1, 256)], [(2, 2, 0), (2, 3, 256)]])
        WHERE = {(t, h): (u, c) for u, pieces in enumerate(PIECES) for t, h, c in pieces}
        SLOTS = NG + 4
        FIRST, PAIRS = 4, 6

        def slots(eng, body, per=None):
            for n in range(FIRST):
                body(n, n % 2, n // 2)
            with (eng.Fori(0, PAIRS) if per is None else eng.loop(PAIRS, per)) as i:
                body(i * 2 + FIRST, 0, i + FIRST // 2)
                body(i * 2 + (FIRST + 1), 1, i + FIRST // 2)
            for n in range(FIRST + 2 * PAIRS, SLOTS):
                body(n, n % 2, n // 2)

        def has(n, lag):
            return not isinstance(n, int) or 0 <= n - lag < NG

        def z_tile(b, t):
            return ps[:, 4 + 2 * b + t // 2, (t % 2) * D:(t % 2 + 1) * D]

        block = ctx.enter_context(nc.Block())

        @block.sync
        def _(sp):
            for b in range(B):
                sp.dma_start(xa[:, b * TPB:(b + 1) * TPB, :],
                             x_rows[:, b * TPB:(b + 1) * TPB, :]).then_inc(s_x[b], 16)
                if b == 0:
                    sp.dma_start(ident[:], consts[:, 0:P]).then_inc(s_const, 16)
            for n, w in enumerate((wq, wk, wv, wo)):
                cols = w.shape[1]
                sp.dma_start(wraw[:, n, 0:DC * cols],
                             w.rearrange("(k p) o -> p k o", p=P)).then_inc(s_w, 16)
            sp.dma_start(w2a[:, :, :], w2.rearrange("(c p) d -> p c d", p=P)).then_inc(s_w2, 16)
            sp.dma_start(had[:, :], consts[:, 3 * P:4 * P]).then_inc(s_w2, 16)
            sp.dma_start(vec[:, :, :], vecs).then_inc(s_vec, 16)
            def load_q(g, b, kv, par):
                need(sp, q_in[par], (g // 2) * 48)
                for j in range(3):
                    sp.dma_start(
                        q_all[24 * j:24 * j + 24, bass.ds(g * (GQ * T), GQ * T)]
                        .rearrange("r (h t) -> r h t", h=GQ),
                        q_dram[:, :, b * T:(b + 1) * T]
                        .rearrange("i (d h) t -> (i d) h t", d=HD)
                        [:, kv * GQ:(kv + 1) * GQ, :]).then_inc(q_in[par], 16)

            for b in range(B):
                sp.wait_ge(k_split, b + 1)
                sp.dma_start(k_dram[:, :, b * T:(b + 1) * T].rearrange("j r t -> r j t"),
                             kparts[:, :, :]).then_inc(k_spilled, 16)
                sp.wait_ge(q_split0, b + 1)
                sp.wait_ge(q_split1, b + 1)
                for i in range(3):
                    sp.dma_start(
                        q_dram[i, :, b * T:(b + 1) * T].rearrange("(m p) t -> p m t", p=P),
                        qparts[:, i, :, :]).then_inc(q_spilled, 16)
                sp.wait_ge(k_spilled, 16 * (b + 1))
                if b == 0:
                    sp.wait_ge(s_ready, 3)
                for j in range(3):
                    for i in range(3):
                        r = 24 * j + 8 * i
                        sp.dma_start(
                            k_all[r:r + 8, b * NKV * T:(b + 1) * NKV * T]
                            .rearrange("d (k t) -> d k t", k=NKV),
                            k_dram[j, :, b * T:(b + 1) * T]
                            .rearrange("(d k) t -> d k t", d=HD)).then_inc(k_in[b], 16)
                sp.wait_ge(q_spilled, 48 * (b + 1))
                for kv in range(NKV):
                    load_q(b * NKV + kv, b, kv, kv % 2)
            sp.wait_ge(st_full, 10 * NKV)
            for w, dst in ((w1, w1raw), (w3, w3raw)):
                sp.dma_start(dst[:, :, :], w.rearrange("(k p) h -> p k h", p=P))\
                    .then_inc(s_post, 16)
            sp.dma_start(rwraw[:, :, :, :], mix_w.rearrange("w (k p) o -> p w k o", p=P))\
                .then_inc(s_rw, 16)
            sp.wait_ge(att_ready, NG)
            sp.dma_start(gate_raw[:, :, :], route_w.rearrange("(k p) o -> p k o", p=P))\
                .then_inc(s_tail, 16)
            sp.dma_start(iota[:, :], consts[:, 4 * P:4 * P + E]).then_inc(s_tail, 16)
            sp.dma_start(bo_sb[:, :], bo.to_broadcast((P, D))).then_inc(s_tail, 16)

            sp.wait_ge(z_done, 2)
            def load_chunk(c, par, turn):
                need(sp, m_lo_ready, c - 1)
                sp.dma_start(mraw[:, par, :], moe_w[c]).then_inc(m_loaded[par], 16)
            load_chunk(0, 0, 0)
            load_chunk(1, 1, 0)
            with sp.Fori(1, MC // 2) as i:
                for par in range(2):
                    sp.wait_ge(m_lo_ready, i * 2 + par - 1)
                    sp.dma_start(mraw[:, par, :],
                                 moe_w[bass.ds(i * 2 + par, 1)].rearrange("o p f -> p (o f)"))\
                        .then_inc(m_loaded[par], 16)
            for b in range(B):
                sp.wait_ge(x_new, 3 * B + b + 1)
                sp.dma_start(out_rows[:, b * TPB:(b + 1) * TPB, :],
                             xa[:, b * TPB:(b + 1) * TPB, :]).then_inc(s_out, 16)
            sp.wait_ge(s_out, 16 * B)

        @block.gpsimd
        def _(pool):
            chain = Chain(pool, s_pool)
            chain.step(pool.memset(zero[:], 0.0))
            chain.settle()
            none = zero[:, :, :].to_broadcast((P, TPB, GQ))
            pool.memset(ones[:], 1.0).then_inc(s_ready, 1)
            pool.memset(halfneg[:], -0.5).then_inc(s_ready, 1)
            pool.wait_ge(s_ready, 2)
            pool.memset(k_all[64:96, :].bitcast(U32), 0x3F803F80).then_inc(s_ready, 1)
            pool.wait_ge(s_ready, 3)
            chain.step(pool.memset(v_all[:, :], 0.0))
            pool.dma_start(identb[:], consts[:, 0:P]).then_inc(s_constb, 16)
            pool.dma_start(hide_cols[:], consts[:, P:2 * P]).then_inc(s_constb, 16)
            pool.dma_start(hide_rows[:], consts[:, 2 * P:3 * P]).then_inc(s_constb, 16)
            chain.settle()
            pool.memset(v_all[:, :].rearrange("p (a c) -> p a c", c=32)[:, :, HD:HD + 1],
                        1.0).then_inc(s_ready, 1)
            pool.wait_ge(s_ready, 4)

            def power(n):
                b = n if n < 2 else (n // 2 - 1) % 2 if n < 14 else n % 2
                h = slice(b * TPB, (b + 1) * TPB)
                pool.wait_ge(ln_var, n + 1)
                pool.tensor_tensor(rstd[:, h], ve[:, h], halfneg[:, h], ALU.pow)\
                    .then_inc(ln_rstd, 1)
            power(0)
            power(1)
            pool.wait_ge(s_w2, 32)
            src, dst = w2a, w2b
            for width in (1, 2, 4):
                a4 = src[:, :, :].rearrange("p (n two w) d -> p n two (w d)", two=2, w=width)
                b4 = dst[:, :, :].rearrange("p (n two w) d -> p n two (w d)", two=2, w=width)
                chain.step(pool.tensor_tensor(b4[:, :, 0], a4[:, :, 0], a4[:, :, 1], ALU.add))
                chain.step(pool.tensor_tensor(b4[:, :, 1], a4[:, :, 0], a4[:, :, 1],
                                              ALU.subtract))
                chain.settle()
                src, dst = dst, src
            pool.tensor_copy(w2hi[:, :, :], w2b[:, :, :]).then_inc(butterfly, 1)
            pool.wait_ge(butterfly, 1)
            pool.tensor_tensor(w2lo[:, :, :], w2b[:, :, :], w2hi[:, :, :].bitcast(F32),
                               ALU.subtract).then_inc(butterfly, 1)
            for b in range(B):
                pool.wait_ge(q_scaled, 2 * b + 2)
                if b >= 1:
                    pool.wait_ge(q_spilled, 48 * b)
                chain.step(pool.tensor_copy(qparts[:, 0, 1, :], qf[:, 1, :]))
                chain.settle()
                chain.step(pool.tensor_tensor(qf[:, 1, :], qf[:, 1, :], qparts[:, 0, 1, :],
                                              ALU.subtract))
                chain.settle()
                chain.step(pool.tensor_copy(qparts[:, 1, 1, :], qf[:, 1, :]))
                chain.settle()
                pool.tensor_tensor(qparts[:, 2, 1, :], qf[:, 1, :], qparts[:, 1, 1, :],
                                   ALU.subtract).then_inc(q_split1, 1)

            def slot(n, par, pair):
                if has(n, 1):
                    g = n - 1
                    need(pool, mrow_ready, g + 1)
                    for i in range(3):
                        pool.dma_start(
                            q_all[72 + i:73 + i, bass.ds(g * (GQ * T), GQ * T)]
                            .rearrange("o (h t) -> o h t", h=GQ),
                            mrow[GQ * i:GQ * i + GQ, par ^ 1, :]).then_inc(m_in[par ^ 1], 16)
                if has(n, 0):
                    g = n
                    need(pool, s1_read, g * 12 + 12)
                    need(pool, mt_full, g - 1)
                    chain.step(pool.tensor_tensor(m3[:, par, :, 0, :], negm[:, par, :, :], none, ALU.add))
                    chain.settle()
                    chain.step(pool.tensor_tensor(negr[:, par, :, :], negm[:, par, :, :],
                                                  m3[:, par, :, 0, :], ALU.subtract))
                    chain.settle()
                    chain.step(pool.tensor_tensor(m3[:, par, :, 1, :], negr[:, par, :, :], none, ALU.add))
                    chain.settle()
                    pool.tensor_tensor(m3[:, par, :, 2, :], negr[:, par, :, :],
                                       m3[:, par, :, 1, :], ALU.subtract).then_inc(msplit, 1)
            slots(chain, slot, 6)
            for n, (raw, hi, lo) in enumerate(((w1raw, w1hi, w1lo), (w3raw, w3hi, w3lo))):
                pool.wait_ge(w13_hi, n + 1)
                pool.tensor_tensor(lo[:, :, :], raw[:, :, :], hi[:, :, :].bitcast(F32),
                                   ALU.subtract).then_inc(w13_lo, 1)
                power(2 + n)
            power(4)
            power(5)
            pool.wait_ge(s_rw, 16)
            pool.wait_ge(pv_done, NG)
            pool.tensor_copy(rwhi[:, :, :, :], rwraw[:, :, :, :]).then_inc(rw_hi, 1)
            pool.wait_ge(rw_hi, 1)
            pool.tensor_tensor(rwlo[:, :, :, :], rwraw[:, :, :, :], rwhi[:, :, :, :].bitcast(F32),
                               ALU.subtract).then_inc(rw_lo, 1)
            pool.wait_ge(s_tail, 48)
            chain.step(pool.tensor_copy(gate_hi[:, :, :], gate_raw[:, :, :]))
            chain.settle()
            pool.tensor_tensor(gate_lo[:, :, :], gate_raw[:, :, :], gate_hi[:, :, :].bitcast(F32),
                               ALU.subtract).then_inc(gate_split, 1)
            pool.memset(xT[:, :, :, 0:1], 0.0).then_inc(xt_zero, 1)
            pool.dma_start(select_sb[:, :], select).then_inc(s_select, 16)

            def mix_low(b):
                for q in range(3):
                    pool.wait_ge(mix_hi, 3 * b + q + 1)
                    pool.tensor_tensor(m_lo[:, q, :, :], mixed[:, (3 * b + q) % 2, :, :],
                                       m_hi[:, q, :, :].bitcast(F32), ALU.subtract)\
                        .then_inc(mix_lo, 1)

            for b in range(B):
                power(6 + 2 * b)
                power(7 + 2 * b)
                if b == 0:
                    mix_low(0)
            mix_low(1)

            def split_chunk(par, turn, first):
                pool.wait_ge(m_loaded[par], turn * 16 + 16)
                if not first:
                    pool.wait_ge(down_done, turn * 4 + (HC * B - 2 + 2 * par))
                pool.tensor_tensor(mslot_hi[:, par, :], mraw[:, par, :],
                                   zero[:, 0, :].to_broadcast((P, 3 * D)), ALU.add)\
                    .then_inc(m_hi_ready, 1)
                pool.wait_ge(m_hi_ready, turn * 2 + (par + 1))
                pool.tensor_tensor(mslot_lo[:, par, :], mraw[:, par, :],
                                   mslot_hi[:, par, :].bitcast(F32), ALU.subtract)\
                    .then_inc(m_lo_ready, 1)
            for par in range(2):
                split_chunk(par, 0, True)
            for b in range(B):
                power(10 + 2 * b)
                power(11 + 2 * b)
            with pool.Fori(1, MC // 2) as i:
                for par in range(2):
                    split_chunk(par, i, False)
            power(14)
            power(15)

        @block.vector
        def _(dve):
            chain = Chain(dve, s_dve)
            dve.wait_ge(s_w, 64)
            for n in range(4):
                cols = DC * (64 if n in (1, 2) else D)
                dve.tensor_reduce(asum[:, n:n + 1], wraw[:, n, 0:cols], AX.X, ALU.add,
                                  apply_absolute_value=True).then_inc(s_abs, 1)
            for b in range(B):
                h = slice(b * TPB, (b + 1) * TPB)
                dve.wait_ge(s_x[b], 16)
                for t in range(b * TPB, (b + 1) * TPB):
                    chain.step(dve.bn_stats(st6[:, t, :], xa[:, t, :]))
                chain.settle()
                for t in range(b * TPB, (b + 1) * TPB):
                    chain.step(dve.bn_aggr(mv[:, t, :], st6[:, t, :]))
                chain.settle()
                dve.tensor_scalar(ve[:, h], mv[:, h, 1], LN_EPS, None, ALU.add).then_inc(ln_var, 1)
            dve.wait_ge(s_tot, 1)
            for n in range(4):
                count = D * (64 if n in (1, 2) else D)
                chain.step(dve.tensor_scalar(wsc[:, n:n + 1], ps[:, 7, n:n + 1], 1.0 / count,
                                             QUANT_EPS, ALU.mult, ALU.max))
            chain.settle()
            dve.scalar_tensor_tensor(qsc[:, :], wsc[:, 0:1], float(np.float32(HD) ** -0.5),
                                     wsc[:, 1:2], ALU.mult, ALU.mult).then_inc(s_scale, 1)
            dve.wait_ge(s_vec, 16)
            chain.step(dve.tensor_tensor(so2[:, :], wsc[:, 3:4], wsc[:, 3:4], ALU.mult))
            for q, v in enumerate((TMR, TMK, TMV)):
                chain.step(dve.tensor_scalar(omt[:, q, :], vec[:, v, :], -1.0, 1.0,
                                             ALU.mult, ALU.add))
            chain.step(dve.tensor_tensor(ubk[:, :], vec[:, UK, :], vec[:, BK, :], ALU.add))
            chain.step(dve.tensor_scalar(nwd[:, :], vec[:, WD, :], -1.0, None, ALU.mult))
            chain.settle()
            dve.wait_ge(s_w2, 32)
            dve.tensor_copy(hadr[:, :], had[:, :]).then_inc(w2_split, 1)
            chain.step(dve.tensor_tensor(ubw[:, :], ubk[:, :], vec[:, WD, :], ALU.subtract))
            for b in range(B):
                h = slice(b * TPB, (b + 1) * TPB)
                cs = slice(b * T, (b + 1) * T)
                dve.wait_ge(ln_rstd, b + 1)
                chain.step(dve.scalar_tensor_tensor(nmr[:, h], mv[:, h, 0], -1.0, rstd[:, h],
                                                    ALU.mult, ALU.mult))
                chain.settle()
                if b >= 1:
                    dve.wait_ge(tr_done, 2 * b)
                for t in range(TPB):
                    u = b * TPB + t
                    dve.tensor_scalar(xn0[:, t, :], xa[:, u, :], rstd[:, u:u + 1], nmr[:, u:u + 1],
                                      ALU.mult, ALU.add).then_inc(ln_rows, 1)
                for k in range(DC):
                    dve.wait_ge(hi_done, 2 * b + k + 1)
                    dve.tensor_tensor(cols0_lo[:, k, cs], ps[:, 2 * b + k, :],
                                      cols0_hi[:, k, cs].bitcast(F32), ALU.subtract)\
                        .then_inc(lo_done, 1)
            for b in range(B):
                dve.wait_ge(k_scaled, b + 1)
                if b >= 1:
                    dve.wait_ge(k_spilled, 16 * b)
                chain.step(dve.tensor_copy(kparts[:, 0, :], kf[:, :]))
                chain.settle()
                chain.step(dve.tensor_tensor(kf[:, :], kf[:, :], kparts[:, 0, :], ALU.subtract))
                chain.settle()
                chain.step(dve.tensor_copy(kparts[:, 1, :], kf[:, :]))
                chain.settle()
                dve.tensor_tensor(kparts[:, 2, :], kf[:, :], kparts[:, 1, :], ALU.subtract)\
                    .then_inc(k_split, 1)
                dve.wait_ge(q_scaled, 2 * b + 1)
                if b >= 1:
                    dve.wait_ge(q_spilled, 48 * b)
                chain.step(dve.tensor_copy(qparts[:, 0, 0, :], qf[:, 0, :]))
                chain.settle()
                chain.step(dve.tensor_tensor(qf[:, 0, :], qf[:, 0, :], qparts[:, 0, 0, :],
                                             ALU.subtract))
                chain.settle()
                chain.step(dve.tensor_copy(qparts[:, 1, 0, :], qf[:, 0, :]))
                chain.settle()
                dve.tensor_tensor(qparts[:, 2, 0, :], qf[:, 0, :], qparts[:, 1, 0, :],
                                  ALU.subtract).then_inc(q_split0, 1)
                dve.wait_ge(kv_mm, 2 * b + 2)
                dve.wait_ge(s_ready, 4)
                dve.tensor_scalar(
                    v_all[:, :].rearrange("p (g s c) -> p g s c", g=NG, c=32)
                    [:, b * NKV:(b + 1) * NKV, :, 0:HD],
                    ps[:, 2 * b + 1, 0:TPB * 64].rearrange("p (s g d) -> p g s d", s=TPB, d=HD),
                    wsc[:, 2:3], None, ALU.mult).then_inc(v_stored, 1)

            dve.wait_ge(w2_hi_done, 1)
            dve.scalar_tensor_tensor(
                w2lo[:, :, :].rearrange("p c d -> p (c d)"),
                ps[:, 4:8, :].rearrange("p b f -> p (b f)"), 1.0 / 32,
                w2hi[:, :, :].bitcast(F32).rearrange("p c d -> p (c d)"), ALU.mult,
                ALU.subtract).then_inc(w2_lo_done, 1)

            def slot(n, par, pair):
                for u, (qt, h0, nh) in enumerate(UNITS):
                    if has(n, 0):
                        g = n
                        if u == 0:
                            need(dve, msplit, g - 1)
                        need(dve, s1_full, g * 12 + u + 1)
                        w = (qt + 1) * P
                        dve.tensor_reduce(
                            negm[:, par, qt, h0:h0 + nh],
                            ps[:, u % 4, 0:nh * w].rearrange("p (h t) -> p h t", h=nh),
                            AX.X, ALU.max, negate=True).then_inc(s1_read, 1)
                    if u == 2 and has(n, 2):
                        g = n - 2
                        need(dve, pv_done, g - 1)
                        dve.tensor_scalar(v_now[:, par, :, :].rearrange("p s c -> p (s c)"),
                                          v_all[:, bass.ds(g * (TPB * 32), TPB * 32)],
                                          1.0, None, ALU.mult).then_inc(v_ready, 1)
                    if u == 6 and has(n, 1):
                        g = n - 1
                        need(dve, mt_full, g + 1)
                        need(dve, m_in[par ^ 1], (pair - 1 + par) * 48)
                        dve.tensor_copy(mrow[:, par ^ 1, :], mt_bank)\
                            .then_inc(mrow_ready, 1)
                    if u == 4 and has(n, 4):
                        g = n - 4
                        need(dve, ot_full, g + 1)
                        o4 = ps[:, 7, :].rearrange("p (s h c) -> p s h c", s=TPB, h=GQ)
                        chain.step(dve.reciprocal(rsum[:, par, :, :], o4[:, :, :, HD]))
                        chain.settle()
                        dve.tensor_tensor(
                            att4[:, bass.ds(g // 4 * TPB, TPB), bass.ds(g % 4 * 32, 32)]
                            .rearrange("p s (h d) -> p s h d", h=GQ),
                            o4[:, :, :, 0:HD],
                            rsum[:, par, :, :].unsqueeze(3).to_broadcast((P, TPB, GQ, HD)),
                            ALU.mult).then_inc(att_ready, 1)
            mt_bank = ps[0:3 * GQ, 6, 0:T // 2].bitcast(BF16)
            att4 = att[:, :].rearrange("p (g s c) -> p (g s) c", s=TPB, c=4 * 32)
            slots(chain, slot, 2)

            def statistics(b, source):
                for t in range(TPB):
                    chain.step(dve.bn_stats(st6[:, b * TPB + t, :], source(t)))
                chain.settle()
                for t in range(TPB):
                    chain.step(dve.bn_aggr(mv[:, b * TPB + t, :], st6[:, b * TPB + t, :]))
                chain.settle()

            def out_norm(part, b):
                h = slice(b * TPB, (b + 1) * TPB)
                if part % 2 == 0:
                    dve.wait_ge(z_done, part + b + 1)
                elif part == 1:
                    dve.wait_ge(down_done, HC * (b + 1))
                else:
                    dve.wait_ge(down_done, HC * B + 2 * MC - 1 + b)
                if part == 2:
                    for pair in range(2):
                        dve.tensor_tensor(
                            rows[:, b * TPB + 2 * pair:b * TPB + 2 * pair + 2, :],
                            ps[:, 4 + 2 * b + pair, :].rearrange("p (t d) -> p t d", t=2),
                            bo_sb[:, :].unsqueeze(1).to_broadcast((P, 2, D)), ALU.add)\
                            .then_inc(z_biased, 1)
                    dve.wait_ge(z_biased, 2 * b + 2)
                    statistics(b, lambda t: rows[:, b * TPB + t, :])
                else:
                    statistics(b, lambda t: z_tile(b, t))
                if part == 0:
                    dve.tensor_scalar(ve[:, h], mv[:, h, 1], so2[:, 0:1], LN_EPS,
                                      ALU.mult, ALU.add).then_inc(ln_var, 1)
                else:
                    dve.tensor_scalar(ve[:, h], mv[:, h, 1], LN_EPS, None, ALU.add)\
                        .then_inc(ln_var, 1)
                n = 2 + part * 4 + 2 * b if part < 3 else 14 + b
                dve.wait_ge(ln_rstd, n + 1)
                if part == 0:
                    chain.step(dve.tensor_scalar(rstd[:, h], rstd[:, h], wsc[:, 3:4], None,
                                                 ALU.mult))
                    chain.settle()
                dve.scalar_tensor_tensor(nmr[:, h], mv[:, h, 0], -1.0, rstd[:, h],
                                         ALU.mult, ALU.mult).then_inc(z_ready, 1)

            def residual(part, b):
                old, new = ((xa, xb), (xb, xa))[part % 2]
                h = slice(b * TPB, (b + 1) * TPB)
                dve.wait_ge(z_norm, part * B + b + 1)
                dve.tensor_tensor(new[:, h, :], old[:, h, :], rows[:, h, :], ALU.add)\
                    .then_inc(x_new, 1)
                dve.wait_ge(x_new, part * B + b + 1)
                return new

            def in_norm(part, b):
                new = residual(part, b)
                h = slice(b * TPB, (b + 1) * TPB)
                statistics(b, lambda t: new[:, b * TPB + t, :])
                dve.tensor_scalar(ve[:, h], mv[:, h, 1], LN_EPS, None, ALU.add)\
                    .then_inc(ln_var, 1)
                dve.wait_ge(ln_rstd, 2 + part * 4 + 2 * b + 2)
                chain.step(dve.scalar_tensor_tensor(nmr[:, h], mv[:, h, 0], -1.0, rstd[:, h],
                                                    ALU.mult, ALU.mult))
                chain.settle()
                for t in range(b * TPB, (b + 1) * TPB):
                    dve.tensor_scalar(rows[:, t, :], new[:, t, :], rstd[:, t:t + 1],
                                      nmr[:, t:t + 1], ALU.mult, ALU.add).then_inc(rows_ready, 1)

            def split_low(turn, b):
                for k in range(DC):
                    dve.wait_ge(cols_h, turn * 4 + 2 * b + k + 1)
                    dve.tensor_tensor(cols_lo[:, k, b * T:(b + 1) * T], ps[:, 2 * b + k, :],
                                      cols_hi[:, k, b * T:(b + 1) * T].bitcast(F32),
                                      ALU.subtract).then_inc(cols_l, 1)

            for b in range(B):
                split_low(0, b)
            for b in range(B):
                out_norm(0, b)
                in_norm(0, b)
            for b in range(B):
                split_low(1, b)

            def mlp_unit(u):
                par, bank = u % 2, 2 * (u % 2)
                dve.wait_ge(silu_done, u + 1)
                dve.wait_ge(up_u, u + 1)
                if u >= 2:
                    dve.wait_ge(h_hi_done, u - 1)
                dve.tensor_tensor(hf[:, par, :], sg[:, par, :], ps[:, bank + 1, :], ALU.mult)\
                    .then_inc(mul_done, 1)
                dve.wait_ge(h_hi_done, u + 1)
                if u >= 2:
                    dve.wait_ge(down_done, u - 1)
                dve.tensor_tensor(h_lo[:, par, :], hf[:, par, :], h_hi[:, par, :].bitcast(F32),
                                  ALU.subtract).then_inc(h_lo_done, 1)

            for u in range(HC):
                mlp_unit(u)
            for j in range(HC):
                mlp_unit(HC + j)
                if j == 2:
                    out_norm(1, 0)
                if j == 4:
                    in_norm(1, 0)

            def mixes(b):
                for q, v in enumerate((TMR, TMK, TMV)):
                    for k in range(DC):
                        n = (3 * b + q) * DC + k
                        dve.wait_ge(mix_tmp, n + 1)
                        if n >= 4:
                            dve.wait_ge(mix_lo, (n - 4) // 2 + 1)
                        dve.scalar_tensor_tensor(
                            mixed[:, (3 * b + q) % 2, k, :], xT[:, k, b, 1:T + 1], vec[:, v, k:k + 1],
                            mix[:, k, :], ALU.mult, ALU.add).then_inc(mix_done, 1)

            def read_keys(b):
                for m in range(DC):
                    dve.wait_ge(proj_k, 2 * b + m + 1)
                    if b >= 1:
                        dve.wait_ge(wkv_lo, DC * b)
                        dve.wait_ge(wkv_hi, DC * b)
                    dve.tensor_scalar(decay_in[:, m, :], ps[:, 2 * b + m, :], ubk[:, m:m + 1],
                                      vec[:, WD, m:m + 1], ALU.add, ALU.max).then_inc(k_read, 1)
                    dve.tensor_scalar(gain[:, m, :], ps[:, 2 * b + m, :], ubw[:, m:m + 1],
                                      0.0, ALU.add, ALU.min).then_inc(k_read, 1)

            def scan(b):
                for m in range(DC):
                    dve.wait_ge(gain_done, 2 * b + m + 1)
                    dve.wait_ge(proj_v, 2 * b + m + 1)
                    dve.scalar_tensor_tensor(gained[:, m, :], ps[:, 4 + 2 * b + m, :],
                                             vec[:, BV, m:m + 1], gain[:, m, :], ALU.add,
                                             ALU.mult).then_inc(v_read, 1)
                    chain.step(dve.tensor_tensor_scan(den[:, m, :], decay[:, m, :],
                                                      gain[:, m, :], 0.0, ALU.mult, ALU.add))
                    dve.wait_ge(v_read, 2 * b + m + 1)
                    chain.step(dve.tensor_tensor_scan(num[:, m, :], decay[:, m, :],
                                                      gained[:, m, :], 0.0, ALU.mult, ALU.add))
                    chain.settle()
                    chain.step(dve.reciprocal(gain[:, m, :], den[:, m, :]))
                    chain.settle()
                    chain.step(dve.tensor_tensor(num[:, m, :], num[:, m, :], gain[:, m, :],
                                                 ALU.mult))
                    chain.settle()
                    dve.wait_ge(proj_r, 2 * b + m + 1)
                    dve.scalar_tensor_tensor(den[:, m, :], ps[:, 2 * b + m, :],
                                             vec[:, BR, m:m + 1], num[:, m, :], ALU.add,
                                             ALU.mult).then_inc(wkv_done, 1)
                    dve.wait_ge(wkv_hi, 2 * b + m + 1)
                    dve.tensor_tensor(cols_lo[:, m, b * T:(b + 1) * T], den[:, m, :],
                                      cols_hi[:, m, b * T:(b + 1) * T].bitcast(F32),
                                      ALU.subtract).then_inc(wkv_lo, 1)

            mixes(0)
            read_keys(0)
            out_norm(1, 1)
            in_norm(1, 1)
            mixes(1)
            scan(0)
            read_keys(1)
            out_norm(2, 0)
            in_norm(2, 0)
            scan(1)
            split_low(2, 0)
            out_norm(2, 1)
            in_norm(2, 1)

            def route(b):
                h = slice(b * TPB, (b + 1) * TPB)
                dve.wait_ge(route_mm, b + 1)
                chain.step(dve.tensor_copy(
                    logits[:, h, :],
                    ps[:, 4 + 2 * b, 0:TPB * RW].rearrange("p (t c) -> p t c", c=RW)))
                chain.settle()
                for t in range(b * TPB, (b + 1) * TPB):
                    chain.step(dve.max(top8[:, t, :], logits[:, t, 0:E]))
                chain.settle()
                for t in range(b * TPB, (b + 1) * TPB):
                    chain.step(dve.max_index(topi[:, t, :], top8[:, t, :], logits[:, t, 0:E]))
                chain.step(dve.tensor_tensor(
                    wtop[:, h, 0:TOPK], top8[:, h, 0:TOPK],
                    top8[:, h, 0:1].to_broadcast((P, TPB, TOPK)), ALU.subtract))
                chain.step(dve.tensor_scalar(wtop[:, h, TOPK], logits[:, h, E], -1.0, None,
                                             ALU.mult))
                chain.settle()
                dve.tensor_copy(topf[:, h, :], topi[:, h, :]).then_inc(route_ex, 1)
                dve.wait_ge(route_exp, b + 1)
                dve.wait_ge(route_ex, b + 1)
                chain.step(dve.tensor_reduce(wsum[:, h, 0], wtop[:, h, 0:TOPK], AX.X, ALU.add))
                chain.step(dve.tensor_scalar(wsum[:, h, 1], wtop[:, h, TOPK], 1.0, None, ALU.add))
                chain.settle()
                chain.step(dve.reciprocal(wsum[:, h, :], wsum[:, h, :]))
                if b >= 1:
                    dve.wait_ge(route_t, b)
                chain.step(dve.memset(cb[:, :, :], 0.0))
                chain.settle()
                chain.step(dve.tensor_tensor(
                    wtop[:, h, 0:TOPK], wtop[:, h, 0:TOPK],
                    wsum[:, h, 0:1].to_broadcast((P, TPB, TOPK)), ALU.mult))
                for k in range(TOPK):
                    chain.settle()
                    chain.step(dve.tensor_tensor(
                        eq[:, :, :], iota[:, :].unsqueeze(1).to_broadcast((P, TPB, E)),
                        topf[:, h, k:k + 1].to_broadcast((P, TPB, E)), ALU.is_equal))
                    chain.settle()
                    dst = comb[:, :, 0:E] if k == 0 else eq[:, :, :]
                    chain.step(dve.tensor_tensor(
                        dst, eq[:, :, :], wtop[:, h, k:k + 1].to_broadcast((P, TPB, E)),
                        ALU.mult))
                    if k:
                        chain.settle()
                        chain.step(dve.tensor_tensor(comb[:, :, 0:E], comb[:, :, 0:E],
                                                     eq[:, :, :], ALU.add))
                chain.step(dve.tensor_copy(comb[:, :, E], wsum[:, h, 1]))
                for i in range(3):
                    chain.settle()
                    chain.step(dve.tensor_copy(cb[:, :, i * E:(i + 1) * E], comb[:, :, 0:E]))
                    if i == 2:
                        chain.settle()
                        dve.tensor_copy(cb[:, :, 3 * E + i], comb[:, :, E]).then_inc(route_rows, 1)
                    else:
                        chain.step(dve.tensor_copy(cb[:, :, 3 * E + i], comb[:, :, E]))
                        chain.settle()
                        chain.step(dve.tensor_tensor(comb[:, :, 0:E], comb[:, :, 0:E],
                                                     cb[:, :, i * E:(i + 1) * E], ALU.subtract))
                        chain.step(dve.tensor_tensor(comb[:, :, E], comb[:, :, E],
                                                     cb[:, :, 3 * E + i], ALU.subtract))
                dve.wait_ge(route_t, b + 1)
                dve.tensor_copy(ct[:, b * T:(b + 1) * T],
                                ps[:, 5 + 2 * b, 0:T // 2].bitcast(BF16)).then_inc(route_cols, 1)

            route(0)
            split_low(2, 1)
            route(1)

            def expert_unit(turn, r):
                par = r % 2
                v = turn * 4 + r
                u = v + HC * B
                dve.wait_ge(silu_done, u + 1)
                dve.wait_ge(up_u, u + 1)
                dve.wait_ge(h_hi_done, u - 1)
                dve.tensor_tensor(sg[:, par, :], sg[:, par, :], ps[:, (3 * r + 1) % 4, :],
                                  ALU.mult).then_inc(t_done, 1)
                dve.wait_ge(t_done, v + 1)
                dve.wait_ge(bc_full, v + 1)
                dve.tensor_tensor(hf[:, par, :], sg[:, par, :], ps[:, (3 * r + 2) % 4, :],
                                  ALU.mult).then_inc(mul_done, 1)
                dve.wait_ge(h_hi_done, u + 1)
                dve.wait_ge(down_done, u - 1)
                dve.tensor_tensor(h_lo[:, par, :], hf[:, par, :], h_hi[:, par, :].bitcast(F32),
                                  ALU.subtract).then_inc(h_lo_done, 1)
            with dve.Fori(0, MC // 2) as i:
                for r in range(4):
                    expert_unit(i, r)
            for b in range(B):
                out_norm(3, b)
                residual(3, b)

        @block.scalar
        def _(act):
            act.wait_ge(s_w, 64)
            for n in range(4):
                cols = DC * (64 if n in (1, 2) else D)
                act.activation(wsg[:, n, 0:cols], wraw[:, n, 0:cols], ACT.Sign)\
                    .then_inc(s_sign, 1)
            for b in range(B):
                cs = slice(b * T, (b + 1) * T)
                for k in range(DC):
                    act.wait_ge(tr_done, 2 * b + k + 1)
                    act.copy(cols0_hi[:, k, cs], ps[:, 2 * b + k, :]).then_inc(hi_done, 1)
            act.wait_ge(s_scale, 1)
            for b in range(B):
                act.wait_ge(kv_mm, 2 * b + 1)
                if b >= 1:
                    act.wait_ge(k_split, b)
                act.copy(kf[:, :], ps[0:64, 2 * b, :]).then_inc(k_scaled, 1)
                for m in range(DC):
                    act.wait_ge(q_mm, 2 * b + m + 1)
                    if b >= 1:
                        act.wait_ge([q_split0, q_split1][m], b)
                    act.mul(qf[:, m, :], ps[:, 4 + 2 * b + m, :], qsc[:, 0:1])\
                        .then_inc(q_scaled, 1)

            act.wait_ge(w2_mm, HC // 2)
            act.mul(w2hi[:, :, :], ps[:, 4:8, :].rearrange("p b (c d) -> p (b c) d", d=D),
                    1.0 / 32).then_inc(w2_hi_done, 1)

            def slot(n, par, pair):
                for u in range(10):
                    if has(n, 2):
                        g = n - 2
                        if u == 0:
                            need(act, pv_done, g - 1)
                        need(act, st_full, g * 10 + u + 1)
                        act.activation(probs[:, par, u, :], ps[:, 4 + u % 2, :], ACT.Exp)\
                            .then_inc(st_exp, 1)
                    if u == 7 and has(n, 3):
                        g = n - 3
                        need(act, pv_done, g + 1)
                        need(act, ot_full, g - 1)
                        act.copy(o_cols[:, par ^ 1, :], ps[:, 7, :]).then_inc(o_copied, 1)
            slots(act, slot)

            def split_high(turn, b):
                for k in range(DC):
                    act.wait_ge(cols_full, turn * 4 + 2 * b + k + 1)
                    act.copy(cols_hi[:, k, b * T:(b + 1) * T], ps[:, 2 * b + k, :])\
                        .then_inc(cols_h, 1)

            def normalise(part, b):
                act.wait_ge(z_ready, part * B + b + 1)
                for t in range(TPB):
                    u = b * TPB + t
                    z = rows[:, u, :] if part == 2 else z_tile(b, t)
                    ins = act.activation(rows[:, u, :], z, ACT.Identity,
                                         bias=nmr[:, u:u + 1], scale=rstd[:, u:u + 1])
                ins.then_inc(z_norm, 1)

            for n, (raw, hi) in enumerate(((w1raw, w1hi), (w3raw, w3hi))):
                act.wait_ge(s_post, 32)
                act.copy(hi[:, :, :], raw[:, :, :]).then_inc(w13_hi, 1)
            for b in range(B):
                split_high(0, b)
            for b in range(B):
                normalise(0, b)
            for b in range(B):
                split_high(1, b)

            def silu(u, bank, par, out_u=None):
                act.wait_ge(up_g, u + 1)
                act.activation(sg[:, par, :], ps[:, bank, :], ACT.Silu).then_inc(silu_done, 1)

            def high(u, par):
                act.wait_ge(mul_done, u + 1)
                need(act, down_done, u - 1)
                act.copy(h_hi[:, par, :], hf[:, par, :]).then_inc(h_hi_done, 1)

            for u in range(B * HC):
                par = u % 2
                need(act, mul_done, u - 1)
                silu(u, 2 * par, par)
                high(u, par)
                if u == HC + 2:
                    normalise(1, 0)

            def columns(b):
                act.wait_ge(xt_zero, 1)
                for k in range(DC):
                    act.wait_ge(cols_full, 8 + 2 * b + k + 1)
                    act.copy(xT[:, k, b, 1:T + 1], ps[:, 2 * b + k, :]).then_inc(xt_ready, 1)

            def mixes(b):
                act.wait_ge(xt_ready, 2 * b + 2)
                for q, v in enumerate((TMR, TMK, TMV)):
                    for k in range(DC):
                        n = (3 * b + q) * DC + k
                        if n >= 2:
                            act.wait_ge(mix_done, n - 1)
                        act.mul(mix[:, k, :], xT[:, k, b, 0:T], omt[:, q, k:k + 1])\
                            .then_inc(mix_tmp, 1)
                    act.wait_ge(mix_done, (3 * b + q) * DC + 2)
                    if q == 0:
                        act.activation(mixed[:, (3 * b + q) % 2, :, :], mixed[:, (3 * b + q) % 2, :, :], ACT.Silu)\
                            .then_inc(mix_silu, 1)
                        act.wait_ge(mix_silu, b + 1)
                    if b >= 1:
                        act.wait_ge([proj_r, proj_k, proj_v][q], DC * b)
                    act.copy(m_hi[:, q, :, :], mixed[:, (3 * b + q) % 2, :, :]).then_inc(mix_hi, 1)

            def exponents(b):
                for m in range(DC):
                    act.wait_ge(k_read, 4 * b + 2 * m + 2)
                    act.activation(decay[:, m, :], decay_in[:, m, :], ACT.Exp,
                                   bias=nwd[:, m:m + 1], scale=-1.0).then_inc(decay_done, 1)
                    act.activation(gain[:, m, :], gain[:, m, :], ACT.Exp).then_inc(gain_done, 1)

            def wkv_high(b):
                for m in range(DC):
                    act.wait_ge(wkv_done, 2 * b + m + 1)
                    act.copy(cols_hi[:, m, b * T:(b + 1) * T], den[:, m, :]).then_inc(wkv_hi, 1)

            columns(0)
            mixes(0)
            normalise(1, 1)
            columns(1)
            mixes(1)
            exponents(0)
            wkv_high(0)
            act.wait_ge(z_biased, 2)
            normalise(2, 0)
            exponents(1)
            wkv_high(1)
            split_high(3, 0)
            act.wait_ge(z_biased, 4)
            normalise(2, 1)

            def route(b):
                h = slice(b * TPB, (b + 1) * TPB)
                act.wait_ge(route_ex, b + 1)
                act.activation(wtop[:, h, :], wtop[:, h, :], ACT.Exp).then_inc(route_exp, 1)
            route(0)
            split_high(3, 1)
            route(1)
            with act.Fori(0, MC // 2) as i:
                for r in range(4):
                    u = i * 4 + (r + HC * B)
                    par = r % 2
                    act.wait_ge(mul_done, u - 1)
                    silu(u, (3 * r) % 4, par)
                    high(u, par)
            for b in range(B):
                normalise(3, b)

        @block.tensor
        def _(pe):
            pe.wait_ge(s_ready, 1)
            pe.wait_ge(s_abs, 4)
            pe.matmul(ps[:, 7, 0:4], ones[:, :], asum[:, :], start=True, stop=True)\
                .then_inc(s_tot, 1)
            pe.wait_ge(s_const, 16)
            pe.wait_ge(s_constb, 48)
            for b in range(B):
                for k in range(DC):
                    for t in range(TPB):
                        pe.wait_ge(ln_rows, b * TPB + t + 1)
                        mm = pe.transpose(ps[:, 2 * b + k, t * P:(t + 1) * P],
                                          xn0[:, t, k * P:(k + 1) * P], ident[:, :])
                    mm.then_inc(tr_done, 1)
            pe.wait_ge(s_sign, 4)
            pe.wait_ge(s_scale, 1)
            for b in range(B):
                cs = slice(b * T, (b + 1) * T)
                pe.wait_ge(lo_done, 2 * b + 2)
                parts = [(k, c) for k in range(DC) for c in (cols0_hi, cols0_lo)]
                for n, (k, c) in enumerate(parts):
                    mm = pe.matmul(ps[0:64, 2 * b, :], wsg[:, 1, k * 64:(k + 1) * 64],
                                   c[:, k, cs], start=(n == 0), stop=(n == 3))
                mm.then_inc(kv_mm, 1)
                for m in range(DC):
                    for n, (k, c) in enumerate(parts):
                        mm = pe.matmul(ps[:, 4 + 2 * b + m, :],
                                       wsg[:, 0, k * D + m * P:k * D + (m + 1) * P],
                                       c[:, k, cs], start=(n == 0), stop=(n == 3))
                    mm.then_inc(q_mm, 1)
                for t in range(TPB):
                    ts = slice(b * T + t * P, b * T + (t + 1) * P)
                    for n, (k, c) in enumerate(parts):
                        mm = pe.matmul(ps[:, 2 * b + 1, t * 64:(t + 1) * 64], c[:, k, ts],
                                       wsg[:, 2, k * 64:(k + 1) * 64],
                                       start=(n == 0), stop=(n == 3))
                mm.then_inc(kv_mm, 1)
            pe.wait_ge(butterfly, 2)
            pe.wait_ge(q_scaled, 2 * B)
            pe.wait_ge(w2_split, 1)
            for c in range(4):
                for n, half in enumerate((w2hi, w2lo)):
                    mm = pe.matmul(ps[:, 4 + c, :], hadr[:, :],
                                   half[:, 2 * c:2 * c + 2, :].rearrange("p c d -> p (c d)"),
                                   start=(n == 0), stop=(n == 1))
                mm.then_inc(w2_mm, 1)
            pe.wait_ge(w2_lo_done, 1)
            pe.wait_ge(q_scaled, 2 * B)
            pe.wait_ge(v_stored, B)

            def score_rows(g, u):
                qt, h0, nh = UNITS[u]
                need(pe, s1_read, g * 12 + u - 3)
                w = (qt + 1) * P
                for h in range(h0, h0 + nh):
                    c = (h - h0) * w
                    pe.matmul(ps[:, u % 4, c:c + w],
                              q_all[0:72, bass.ds(g * (GQ * T) + (h * T + qt * P), P)],
                              k_all[0:72, bass.ds(g * T, w)], start=True, stop=False)
                    mm = pe.matmul(ps[:, u % 4, c + w - P:c + w], identb[:, :], hide_cols[:, :],
                                   start=False, stop=True)
                mm.then_inc(s1_full, 1)

            def score_cols(g, u):
                need(pe, st_exp, g * 10 + u - 1)
                for kt, h, c in PIECES[u]:
                    w = T - kt * P
                    pe.matmul(ps[:, 4 + u % 2, c:c + w],
                              k_all[0:75, bass.ds(g * T + kt * P, P)],
                              q_all[0:75, bass.ds(g * (GQ * T) + (h * T + kt * P), w)],
                              start=True, stop=False)
                    mm = pe.matmul(ps[:, 4 + u % 2, c:c + P], identb[:, :], hide_rows[:, :],
                                   start=False, stop=True)
                mm.then_inc(st_full, 1)

            mt_bank = ps[0:3 * GQ, 6, 0:T // 2].bitcast(BF16)

            def slot(n, par, pair):
                if has(n, 2):
                    need(pe, m_in[par], pair * 48)
                for u in range(12):
                    if has(n, 0):
                        g = n
                        if u == 0:
                            need(pe, q_in[par], pair * 48 + 48)
                            for b in range(B):
                                if not isinstance(g, int) or g // NKV == b:
                                    pe.wait_ge(k_in[b], 144)
                        score_rows(g, u)
                    if has(n, 2) and 1 <= u <= 10:
                        score_cols(n - 2, u - 1)
                    if u == 3 and has(n, 1):
                        g = n - 1
                        need(pe, msplit, g + 1)
                        need(pe, mrow_ready, g)
                        for s in range(TPB):
                            mm = pe.transpose(mt_bank[:, s * P:(s + 1) * P],
                                              m3[:, par ^ 1, s, :, :].rearrange("p i h -> p (i h)"),
                                              identb[:, :])
                        mm.then_inc(mt_full, 1)
                    if u == 1 and has(n, 4):
                        g = n - 4
                        need(pe, o_copied, g + 1)
                        for s in range(TPB):
                            mm = pe.transpose(ps[:, 7, s * P:(s + 1) * P],
                                              o_cols[:, par, s * P:(s + 1) * P], ident[:, :])
                        mm.then_inc(ot_full, 1)
                    if u == 7 and has(n, 3):
                        g = n - 3
                        need(pe, att_ready, g)
                        need(pe, v_ready, g + 1)
                        need(pe, st_exp, g * 10 + 10)
                        for kt in range(TPB):
                            for h in range(GQ):
                                un, c = WHERE[kt, h]
                                w = T - kt * P
                                mm = pe.matmul(ps[32 * h:32 * h + 32, 7, kt * P:T],
                                               v_now[:, par ^ 1, kt, :],
                                               probs[:, par ^ 1, un, c:c + w],
                                               start=(kt == 0), stop=(kt == TPB - 1))
                        mm.then_inc(pv_done, 1)
            slots(pe, slot)

            def transposes(turn, b, tile):
                for k in range(DC):
                    for t in range(TPB):
                        mm = pe.transpose(ps[:, 2 * b + k, t * P:(t + 1) * P],
                                          tile(t, k), ident[:, :])
                    mm.then_inc(cols_full, 1)

            def rows_tile(b):
                return lambda t, k: rows[:, b * TPB + t, k * P:(k + 1) * P]

            att_v = att[:, :].rearrange("p (b k s c) -> p b k s c", b=B, k=DC, c=P)
            pe.wait_ge(att_ready, NG)
            for b in range(B):
                transposes(0, b, lambda t, k: att_v[:, b, k, t, :])
            for b in range(B):
                pe.wait_ge(cols_l, 2 * b + 2)
                for t in range(TPB):
                    ts = slice(b * T + t * P, b * T + (t + 1) * P)
                    for n, (k, c) in enumerate((k, c) for k in range(DC)
                                               for c in (cols_hi, cols_lo)):
                        mm = pe.matmul(z_tile(b, t), c[:, k, ts],
                                       wsg[:, 3, k * D:(k + 1) * D],
                                       start=(n == 0), stop=(n == 2 * DC - 1))
                mm.then_inc(z_done, 1)
            for b in range(B):
                pe.wait_ge(rows_ready, TPB * (b + 1))
                transposes(1, b, rows_tile(b))

            def three_passes(out, lhs_hi, lhs_lo, rhs_hi, rhs_lo, first, last):
                pe.matmul(out, lhs_hi, rhs_hi, start=first, stop=False)
                pe.matmul(out, lhs_lo, rhs_hi, start=False, stop=False)
                return pe.matmul(out, lhs_hi, rhs_lo, start=False, stop=last)

            def down(b, u, par, w_hi, w_lo, start):
                pe.wait_ge(h_lo_done, u + 1)
                for t in range(TPB):
                    ts = slice(t * P, (t + 1) * P)
                    pairs = ((h_hi, w_hi), (h_lo, w_hi), (h_hi, w_lo))
                    for n, (h, w) in enumerate(pairs):
                        mm = pe.matmul(z_tile(b, t), h[:, par, ts], w,
                                       start=start and n == 0 and t % 2 == 0, stop=False,
                                       skip_group_check=True)
                return mm

            def mlp_up(u):
                b, j, bank = u // HC, u % HC, 2 * (u % 2)
                cs = slice(b * T, (b + 1) * T)
                js = slice(j * P, (j + 1) * P)
                for w, (hi, lo) in enumerate(((w1hi, w1lo), (w3hi, w3lo))):
                    need(pe, silu_done if w == 0 else mul_done, u - 1)
                    for k in range(DC):
                        mm = three_passes(ps[:, bank + w, :], hi[:, k, js], lo[:, k, js],
                                          cols_hi[:, k, cs], cols_lo[:, k, cs],
                                          k == 0, k == DC - 1)
                    mm.then_inc(up_u if w else up_g, 1)

            def mlp_down(u):
                b, j = u // HC, u % HC
                if j == 0:
                    pe.wait_ge(z_norm, b + 1)
                mm = down(b, u, u % 2, w2hi[:, j, :], w2lo[:, j, :], j == 0)
                mm.then_inc(down_done, 1)

            pe.wait_ge(cols_l, 4 + 4)
            pe.wait_ge(w13_lo, 2)
            pe.wait_ge(w2_lo_done, 1)
            mlp_up(0)
            for u in range(1, B * HC):
                mlp_up(u)
                mlp_down(u - 1)
            pe.wait_ge(rows_ready, TILES + TPB)
            pe.wait_ge(mul_done, B * HC)
            transposes(2, 0, rows_tile(0))
            mlp_down(B * HC - 1)

            def project(b, q, w, bank, done):
                pe.wait_ge(mix_lo, 3 * b + q + 1)
                for m in range(DC):
                    ms = slice(m * P, (m + 1) * P)
                    for k in range(DC):
                        mm = three_passes(ps[:, bank + m, :], rwhi[:, w, k, ms],
                                          rwlo[:, w, k, ms], m_hi[:, q, k, :],
                                          m_lo[:, q, k, :], k == 0, k == DC - 1)
                    mm.then_inc(done, 1)

            def projections(b):
                pe.wait_ge(rw_lo, 1)
                pe.wait_ge(xt_ready, 2 * b + 2)
                project(b, 1, 0, 2 * b, proj_k)
                pe.wait_ge(z_norm, B + b + 1)
                project(b, 2, 1, 4 + 2 * b, proj_v)
                pe.wait_ge(k_read, 4 * b + 4)
                project(b, 0, 2, 2 * b, proj_r)

            def mix_out(b):
                pe.wait_ge(v_read, 2 * b + 2)
                pe.wait_ge(wkv_lo, 2 * b + 2)
                for t in range(TPB):
                    ts = slice(b * T + t * P, b * T + (t + 1) * P)
                    for k in range(DC):
                        mm = three_passes(z_tile(b, t), cols_hi[:, k, ts], cols_lo[:, k, ts],
                                          rwhi[:, 3, k, :], rwlo[:, 3, k, :],
                                          k == 0, k == DC - 1)
                mm.then_inc(z_done, 1)

            projections(0)
            pe.wait_ge(rows_ready, 2 * TILES)
            transposes(2, 1, rows_tile(1))
            projections(1)
            mix_out(0)
            pe.wait_ge(wkv_done, 2)
            pe.wait_ge(rows_ready, 2 * TILES + TPB)
            transposes(3, 0, rows_tile(0))
            mix_out(1)
            pe.wait_ge(wkv_done, 4)

            def logits_of(b):
                pe.wait_ge(gate_split, 1)
                pe.wait_ge(cols_l, 8 + 2 * b + 2)
                pe.wait_ge(z_biased, 2 * b + 2)
                for t in range(TPB):
                    ts = slice(b * T + t * P, b * T + (t + 1) * P)
                    for k in range(DC):
                        mm = three_passes(ps[:, 4 + 2 * b, t * RW:(t + 1) * RW],
                                          cols_hi[:, k, ts], cols_lo[:, k, ts],
                                          gate_hi[:, k, :], gate_lo[:, k, :],
                                          k == 0, k == DC - 1)
                mm.then_inc(route_mm, 1)

            def route_columns(b):
                pe.wait_ge(route_rows, b + 1)
                for t in range(TPB):
                    mm = pe.transpose(
                        ps[:, 5 + 2 * b, 0:T // 2].bitcast(BF16)[:, t * P:(t + 1) * P],
                        cb[:, t, :], identb[:, :])
                mm.then_inc(route_t, 1)

            logits_of(0)
            pe.wait_ge(rows_ready, 3 * TILES)
            transposes(3, 1, rows_tile(1))
            route_columns(0)
            logits_of(1)
            route_columns(1)

            def expert_up(turn, r, first=False):
                b, par = r % 2, r // 2
                v = turn * 4 + r
                u = v + HC * B
                cs = slice(b * T, (b + 1) * T)
                if b == 0:
                    pe.wait_ge(m_lo_ready, turn * 2 + (par + 1))
                for w in range(2):
                    if w == 0:
                        pe.wait_ge(mul_done, u - 1)
                    else:
                        pe.wait_ge(silu_done, u)
                    for k in range(DC):
                        c = w * D + k * P
                        mm = three_passes(ps[:, (3 * r + w) % 4, :],
                                          mslot_hi[:, par, c:c + P], mslot_lo[:, par, c:c + P],
                                          cols_hi[:, k, cs], cols_lo[:, k, cs],
                                          k == 0, k == DC - 1)
                    mm.then_inc(up_u if w else up_g, 1)
                need(pe, t_done, v)
                pe.matmul(ps[:, (3 * r + 2) % 4, :],
                          select_sb[:, bass.ds(turn * (2 * P) + par * P, P)], ct[:, cs],
                          start=True, stop=True).then_inc(bc_full, 1)

            def expert_down(turn, r, start=False):
                u = turn * 4 + (r + HC * B)
                par = r // 2
                down(r % 2, u, r % 2, mslot_hi[:, par, 2 * D:3 * D],
                     mslot_lo[:, par, 2 * D:3 * D], start).then_inc(down_done, 1)

            pe.wait_ge(s_select, 16)
            pe.wait_ge(route_cols, 2)
            pe.wait_ge(cols_l, 12)
            expert_up(0, 0)
            for r in range(1, 4):
                expert_up(0, r)
                expert_down(0, r - 1, start=r < 3)
            with pe.Fori(1, MC // 2) as i:
                for r in range(4):
                    expert_up(i, r)
                    if r:
                        expert_down(i, r - 1)
                    else:
                        expert_down(i - 1, 3)
            expert_down(MC // 2 - 1, 3)


def kernel(**inputs):
    import numpy as _np
    import concourse.bacc as _bacc
    from concourse import mybir as _mybir
    from concourse.bass_utils import run_bass_kernel_spmd as _run

    a = {n: _np.asarray(v) for n, v in inputs.items()}

    def turned(w):
        return _np.ascontiguousarray(w.T)

    def by_part(w, heads):
        return _np.ascontiguousarray(
            w.reshape(D, heads, HD).transpose(0, 2, 1).reshape(D, heads * HD))

    def chunked(experts, shared):
        flat = _np.concatenate([
            experts.transpose(1, 0, 2).reshape(D, E * F), shared,
            _np.zeros((D, MC * P - E * F - SF), shared.dtype)], axis=1)
        return flat.reshape(DC, P, MC, P).transpose(2, 1, 0, 3).reshape(MC, P, D)

    place = _np.arange(P)
    had = _np.ones((1, 1), _np.float32)
    while had.shape[0] < P:
        had = _np.block([[had, had], [had, -had]])
    hide = _np.where(place[None, :] > place[:, None], _np.float32(MASKED), _np.float32(0))
    consts = _np.concatenate([
        _np.eye(P), hide, hide.T, had, _np.tile(_np.arange(E), (P, 1))], axis=1)
    feature = _np.arange(MC * P)
    select = _np.zeros((P, MC * P), _np.float32)
    for part in range(3):
        of_expert = feature < E * F
        select[part * E + feature[of_expert] // F, feature[of_expert]] = 1.0
        select[3 * E + part, E * F:E * F + SF] = 1.0

    moe = _np.concatenate([
        chunked(a["L1_ffn_wg"], a["L1_ffn_sg"]), chunked(a["L1_ffn_wu"], a["L1_ffn_su"]),
        _np.concatenate([
            a["L1_ffn_wd"].reshape(E * F, D), a["L1_ffn_sd"],
            _np.zeros((MC * P - E * F - SF, D), _np.float32)]).reshape(MC, P, D)], axis=2)
    vecs = _np.stack([a["L1_attn_" + n] for n in ("tmr", "tmk", "tmv", "u", "w", "bk", "bv", "br")])
    arrays = {
        "x": a["L0_attn_x"].reshape(N, D),
        "consts": consts.astype(_np.float32),
        "wq": by_part(a["L0_attn_wq"].T, NKV * GQ), "wk": by_part(a["L0_attn_wk"].T, NKV),
        "wv": turned(a["L0_attn_wv"]), "wo": turned(a["L0_attn_wo"]),
        "w1": turned(a["L0_ffn_W1"]), "w3": turned(a["L0_ffn_W3"]), "w2": turned(a["L0_ffn_W2"]),
        "mix_w": _np.stack([a["L1_attn_W" + n].T for n in "kvro"]),
        "vecs": vecs.reshape(8, DC, P).transpose(2, 0, 1),
        "bo": a["L1_attn_bo"].reshape(1, D),
        "route_w": _np.concatenate([
            a["L1_ffn_gate_w"], a["L1_ffn_seg"], _np.zeros((D, RW - E - 1), _np.float32)], axis=1),
        "moe_w": moe,
        "select": select,
    }
    nc = _bacc.Bacc("TRN2", target_bir_lowering=False, num_devices=1)
    aps, named = [], {}
    for name, v in arrays.items():
        v = _np.ascontiguousarray(v)
        named[f"in_{name}"] = v
        aps.append(nc.dram_tensor(f"in_{name}", v.shape, _mybir.dt.from_np(v.dtype),
                                  kind="ExternalInput").ap())
    aps.append(nc.dram_tensor("out_x", (N, D), _mybir.dt.float32, kind="ExternalOutput").ap())
    sandwich_kernel(nc, *aps)
    r = _run(nc, [named], core_ids=[0])
    return r.results[0]["out_x"].reshape(B, T, D)
```

```python
from contextlib import ExitStack, contextmanager

import numpy as np

import concourse.bass as bass
from concourse import mybir

F32 = mybir.dt.float32
F32R = mybir.dt.float32r
BF16 = mybir.dt.bfloat16
U32 = mybir.dt.uint32
ALU = mybir.AluOpType
ACT = mybir.ActivationFunctionType
AX = mybir.AxisListType

P = 128
D = 256
DC = D // P
B, T = 2, 512
N = B * T
TILES = N // P
TPB = T // P
NKV, GQ, HD = 8, 4, 8
NG = B * NKV
HID = 1024
HC = HID // P
E, TOPK, F, SF = 32, 4, 96, 704
MC = -(-(E * F + SF) // P)
PLACES = 4
RW = 34
TMR, TMK, TMV, UK, WD, BK, BV, BR = range(8)
MIXES = (TMK, TMV, TMR)
LN_EPS = 1e-5
QUANT_EPS = 1e-5
MASKED = -1e30


class Chain:

    def __init__(self, eng, sem):
        self.eng, self.sem, self.n, self.off = eng, sem, 0, 0

    def step(self, ins):
        ins.then_inc(self.sem, 1)
        self.n += 1
        return ins

    def settle(self):
        self.eng.wait_ge(self.sem, self.off + self.n)

    @contextmanager
    def loop(self, count, per):
        before = self.n
        with self.eng.Fori(0, count) as i:
            self.off = i * per
            yield i
            assert self.n - before == per, (self.n - before, per)
        self.off, self.n = 0, before + count * per


def need(eng, sem, value):
    if not isinstance(value, int) or value > 0:
        eng.wait_ge(sem, value)


def sandwich_kernel(nc, x, consts, wq, wk, wv, wo, w1, w3, w2, mix_w, vecs, bo, route_w, moe_w,
                    select, out):
    ctx = ExitStack()
    with ctx:
        def sem(name):
            return ctx.enter_context(nc.semaphore(name))

        at = [(nc.sbuf_base + 31) // 32 * 32]
        SIZE = {F32: 4, F32R: 4, BF16: 2, U32: 4}

        def sb(name, shape, dt):
            size = int(np.prod(shape[1:])) * SIZE[dt]
            t = nc.alloc_sbuf_tensor_at(name, shape, dt, offset=at[0])
            at[0] += (size + 31) // 32 * 32
            assert at[0] <= nc.sbuf_usable_end, (name, at[0])
            return t

        xa = sb("xa", [P, TILES, D], F32)
        xb = sb("xb", [P, TILES, D], F32)
        ident = sb("ident", [P, P], F32)
        identb = sb("identb", [P, P], BF16)
        had = sb("had", [P, P], F32)
        hadr = sb("hadr", [P, P], F32R)
        ones = sb("ones", [P, P], F32)
        zero = sb("zero", [P, 1, 1], F32)
        hide_cols = sb("hide_cols", [P, P], BF16)
        hide_rows = sb("hide_rows", [P, P], BF16)
        halfneg = sb("halfneg", [P, TILES], F32)
        st6 = sb("st6", [P, TILES, 6], F32)
        mv = sb("mv", [P, TILES, 2], F32)
        ve = sb("ve", [P, TILES], F32)
        rstd = sb("rstd", [P, TILES], F32)
        nmr = sb("nmr", [P, TILES], F32)
        nmrz = sb("nmrz", [P, TILES], F32)
        asum = sb("asum", [P, 4], F32)
        wsc = sb("wsc", [P, 4], F32)
        qsc = sb("qsc", [P, 1], F32)
        wsg_at = at[0]
        wsg = sb("wsg", [P, 4, DC * D], F32R)
        w2hi = sb("w2hi", [P, HC, D], F32R)
        w2lo = sb("w2lo", [P, HC, D], F32R)
        att = sb("att", [P, NG * TPB * 32], F32)
        vec = sb("vec", [P, 8, DC], F32)
        omt = sb("omt", [P, 3, DC], F32)
        ubk = sb("ubk", [P, DC], F32)
        ubw = sb("ubw", [P, DC], F32)
        nwd = sb("nwd", [P, DC], F32)
        so2 = sb("so2", [P, 1], F32)

        def place(start, *wanted):
            at[0] = start
            made = [sb(*w) for w in wanted]
            return made, at[0]

        region = at[0]
        (q_all, k_all, v_all), stage = place(
            region, ("q_all", [P, NG * GQ * T], BF16), ("k_all", [P, NG * T], BF16),
            ("v_all", [P, NG * TPB * 32], F32))
        (probs, v_now, o_cols), end = place(
            stage, ("probs", [P, 2, 10, T], F32), ("v_now", [P, 2, TPB, 32], F32),
            ("o_cols", [P, 2, T], F32))
        (negm, negr, m3, mrow, rsum), region_end = place(
            end, ("negm", [P, 2, TPB, GQ], F32), ("negr", [P, 2, TPB, GQ], F32),
            ("m3", [P, 2, TPB, 3, GQ], BF16), ("mrow", [3 * GQ, 2, T], BF16),
            ("rsum", [P, 2, TPB, GQ], F32))
        (xn0, cols0_hi, cols0_lo, w2b, wraw, qf), end = place(
            stage, ("xn0", [P, TPB, D], F32), ("cols0_hi", [P, DC, N], F32R),
            ("cols0_lo", [P, DC, N], F32R), ("w2b", [P, HC, D], F32),
            ("wraw", [P, 4, DC * D], F32), ("qf", [P, DC, T], F32))
        assert end <= region_end
        (qparts, kf, kparts, w2a), _ = place(
            region_end, ("qparts", [P, 3, DC, T], BF16), ("kf", [64, T], F32),
            ("kparts", [64, 3, T], BF16), ("w2a", [P, HC, D], F32))
        (w1hi, w3hi, w1lo, w3lo), half_q = place(
            region, ("w1hi", [P, DC, HID], F32R), ("w3hi", [P, DC, HID], F32R),
            ("w1lo", [P, DC, HID], F32R), ("w3lo", [P, DC, HID], F32R))
        (w1raw, w3raw), _ = place(half_q - 2 * DC * HID * 4, ("w1raw", [P, DC, HID], F32),
                                  ("w3raw", [P, DC, HID], F32))
        (cols_hi, cols_lo, rows, rwhi, rwlo, sg, hf, select_sb), end = place(
            half_q, ("cols_hi", [P, DC, N], F32R), ("cols_lo", [P, DC, N], F32R),
            ("rows", [P, TILES, D], F32), ("rwhi", [P, 4, DC, D], F32R),
            ("rwlo", [P, 4, DC, D], F32R), ("sg", [P, 2, T], F32), ("hf", [P, 2, T], F32),
            ("select_sb", [P, MC * P], BF16))
        assert end <= stage
        (rwraw,), _ = place(half_q + 4 * DC * N * 4, ("rwraw", [P, 4, DC, D], F32))
        (h_hi, h_lo), end = place(stage, ("h_hi", [P, 2, T], F32R), ("h_lo", [P, 2, T], F32R))
        mixing = end
        (xT, mix, mixed, m_hi, m_lo, ct, iota), end = place(
            mixing, ("xT", [P, DC, T + 8], F32), ("mix", [P, DC, T], F32),
            ("mixed", [P, 2, DC, T], F32), ("m_hi", [P, 3, DC, T], F32R),
            ("m_lo", [P, 3, DC, T], F32R), ("ct", [P, N], BF16),
            ("iota", [P, E], F32))
        (gate_hi, gate_lo, bo_sb), end = place(
            end, ("gate_hi", [P, DC, RW], F32R), ("gate_lo", [P, DC, RW], F32R),
            ("bo_sb", [P, D], F32))
        (logits, top8, topi, topf, wtop, wsum, comb, eq, cb), end = place(
            end, ("logits", [P, TILES, RW], F32), ("top8", [P, TILES, 8], F32),
            ("topi", [P, TILES, 8], U32), ("topf", [P, TILES, 8], F32),
            ("wtop", [P, TILES, TOPK + 1], F32), ("wsum", [P, TILES, 2], F32),
            ("comb", [P, TPB, E + 1], F32), ("eq", [P, TPB, E], F32), ("cb", [P, TPB, P], BF16))
        (gate_raw,), end = place(end, ("gate_raw", [P, DC, RW], F32))
        (decay, gain), _ = place(mixing, ("decay", [P, DC, T], F32), ("gain", [P, DC, T], F32))
        (num, den), _ = place(mixing + DC * (T + 8 + T) * 4, ("num", [P, DC, T], F32),
                              ("den", [P, DC, T], F32))
        (mraw,), _ = place(wsg_at, ("mraw", [P, PLACES, 3 * D], F32))
        (mslot_hi, mslot_lo), end = place(region, ("mslot_hi", [P, PLACES, 3 * D], F32R),
                                          ("mslot_lo", [P, PLACES, 3 * D], F32R))
        assert end <= half_q

        ps = ctx.enter_context(nc.psum_tensor("ps", [P, 8, 512], F32))
        q_dram = nc.dram_tensor("q_parts_scratch", (3, D, N), BF16).ap()
        k_dram = nc.dram_tensor("k_parts_scratch", (3, NKV * HD, N), BF16).ap()

        x_rows = x.rearrange("(t p) d -> p t d", p=P)
        out_rows = out.rearrange("(t p) d -> p t d", p=P)

        s_x = [sem("x0_loaded"), sem("x1_loaded")]
        s_const = sem("consts_loaded")
        s_constb = sem("bf16_consts_loaded")
        s_w = sem("attn_weights_loaded")
        s_dve = sem("vector_order")
        s_act = sem("scalar_order")
        s_pool = sem("pool_order")
        s_ready = sem("pool_constants_ready")
        ln_var = sem("ln_variance_ready")
        ln_rstd = sem("ln_rstd_ready")
        ln_rows = sem("ln_rows_ready")
        tr_done = sem("rows_transposed")
        hi_done = sem("cols_hi_ready")
        lo_done = sem("cols_lo_ready")
        s_abs = sem("weight_abs_sums_ready")
        s_tot = sem("weight_totals_ready")
        s_sign = sem("weight_signs_ready")
        s_scale = sem("weight_scales_ready")
        q_mm = sem("q_product_done")
        kv_mm = sem("kv_product_done")
        q_scaled = sem("q_scaled")
        k_scaled = sem("k_scaled")
        v_stored = sem("v_stored")
        q_split0 = sem("q_chunk0_split")
        q_split1 = sem("q_chunk1_split")
        k_split = sem("k_split")
        q_spilled = sem("q_parts_in_dram")
        k_spilled = sem("k_parts_in_dram")
        q_in = [sem("q_even_group_loaded"), sem("q_odd_group_loaded")]
        k_in = [sem("k_batch0_loaded"), sem("k_batch1_loaded")]
        s1_full = sem("score_rows_full")
        s1_read = sem("score_rows_read")
        msplit = sem("max_split")
        mt_full = sem("max_rows_full")
        mrow_ready = sem("max_rows_ready")
        m_in = [sem("max_rows_even_loaded"), sem("max_rows_odd_loaded")]
        st_full = sem("score_cols_full")
        st_exp = sem("probs_ready")
        v_ready = sem("v_group_ready")
        pv_done = sem("pv_done")
        o_copied = sem("o_copied")
        ot_full = sem("o_rows_full")
        att_ready = sem("att_rows_ready")
        s_w2 = sem("w2_loaded")
        butterfly = sem("w2_butterfly_done")
        w2_split = sem("w2_split")
        w2_mm = sem("w2_hadamard_done")
        w2_hi_done = sem("w2_hi_ready")
        w2_lo_done = sem("w2_lo_ready")
        s_vec = sem("vectors_loaded")
        s_post = sem("post_attention_weights_loaded")
        s_rw = sem("mix_weights_loaded")
        s_tail = sem("routing_weights_and_vectors_loaded")
        s_select = sem("select_loaded")
        w13_hi = sem("w1_w3_hi_ready")
        w13_lo = sem("w1_w3_lo_ready")
        rw_hi = sem("mix_weights_hi_ready")
        rw_lo = sem("mix_weights_lo_ready")
        gate_split = sem("routing_weights_split")
        z_done = sem("z_done")
        z_read = sem("z_scaled_and_added")
        x_new = sem("residual_ready")
        rows_ready = sem("rows_ready")
        cols_full = sem("cols_in_psum")
        cols_h = sem("cols_hi_done")
        cols_l = sem("cols_lo_done")
        up_g = sem("gate_product_done")
        up_u = sem("linear_product_done")
        silu_done = sem("silu_done")
        mul_done = sem("gated")
        h_hi_done = sem("hidden_hi_ready")
        h_lo_done = sem("hidden_lo_ready")
        down_done = sem("down_product_done")
        xt_ready = sem("xT_ready")
        xt_zero = sem("xT_start_zeroed")
        mix_tmp = sem("shifted_mix_ready")
        mix_done = sem("mix_ready")
        mix_silu = sem("receptance_silu_ready")
        mix_hi = sem("mix_hi_ready")
        mix_lo = sem("mix_lo_ready")
        proj_k = sem("key_projection_done")
        proj_v = sem("value_projection_done")
        proj_r = sem("receptance_projection_done")
        k_read = sem("key_projection_read")
        decay_done = sem("decay_ready")
        gain_done = sem("gain_ready")
        v_read = sem("value_projection_read")
        wkv_done = sem("wkv_ready")
        wkv_hi = sem("wkv_hi_ready")
        wkv_lo = sem("wkv_lo_ready")
        z_biased = sem("z_biased")
        route_mm = sem("routing_logits_done")
        route_ex = sem("routing_exponent_ready")
        route_exp = sem("routing_exp_done")
        route_rows = sem("routing_rows_ready")
        route_t = sem("routing_transposed")
        route_cols = sem("routing_cols_ready")
        m_loaded = [sem(f"expert_chunk_loaded_{i}") for i in range(PLACES)]
        m_hi_ready = sem("expert_hi_ready")
        m_lo_ready = sem("expert_lo_ready")
        bc_full = sem("routing_broadcast_done")
        t_done = sem("hidden_product_done")
        s_out = sem("out_stored")

        UNITS = ([(3, h, 1) for h in range(4)] + [(2, h, 1) for h in range(4)]
                 + [(1, 0, 2), (1, 2, 2), (0, 0, 2), (0, 2, 2)])
        PIECES = ([[(0, h, 0)] for h in range(4)] + [[(1, h, 0), (3, h, 384)] for h in range(4)]
                  + [[(2, 0, 0), (2, 1, 256)], [(2, 2, 0), (2, 3, 256)]])
        WHERE = {(t, h): (u, c) for u, pieces in enumerate(PIECES) for t, h, c in pieces}
        SLOTS = NG + 4
        FIRST, PAIRS = 4, 5

        def slots(eng, body, per=None):
            for n in range(FIRST):
                body(n, n % 2, n // 2)
            with (eng.Fori(0, PAIRS) if per is None else eng.loop(PAIRS, per)) as i:
                body(i * 2 + FIRST, 0, i + FIRST // 2)
                body(i * 2 + (FIRST + 1), 1, i + FIRST // 2)
            for n in range(FIRST + 2 * PAIRS, SLOTS):
                body(n, n % 2, n // 2)

        def has(n, lag):
            return not isinstance(n, int) or 0 <= n - lag < NG

        def col_bank(turn, b, k):
            return k if b == 0 and turn < 2 else 4 + 2 * b + k

        TURNS = {(0, 0): 0, (1, 0): 1, (0, 1): 2, (1, 1): 3, (3, 0): 4, (3, 1): 5}
        ALL_TURNS = {(0, 0): 0, (1, 0): 1, (0, 1): 2, (1, 1): 3, (2, 0): 4, (2, 1): 5,
                     (3, 0): 6, (3, 1): 7}
        SCAN_AT, OUT_AT, COL_AT, ROUTE_AT = 3, 13, 16, 17

        SCAN_STEPS = [(0, 0), (1, 0), (0, 1), (0, 2), (0, 3), (1, 1), (1, 2), (1, 3)]

        def z_bank(part, b):
            return 2 if part == 0 and b == 0 else 4 + 2 * b

        def z_tile(part, b, t):
            return ps[:, z_bank(part, b) + t // 2, (t % 2) * D:(t % 2 + 1) * D]

        block = ctx.enter_context(nc.Block())

        @block.sync
        def _(sp):
            for b in range(B):
                sp.dma_start(xa[:, b * TPB:(b + 1) * TPB, :],
                             x_rows[:, b * TPB:(b + 1) * TPB, :]).then_inc(s_x[b], 16)
                if b == 0:
                    sp.dma_start(ident[:], consts[:, 0:P]).then_inc(s_const, 16)
            for n, w in enumerate((wq, wk, wv, wo)):
                cols = w.shape[1]
                sp.dma_start(wraw[:, n, 0:DC * cols],
                             w.rearrange("(k p) o -> p k o", p=P)).then_inc(s_w, 16)
            sp.dma_start(w2a[:, :, :], w2.rearrange("(c p) d -> p c d", p=P)).then_inc(s_w2, 16)
            sp.dma_start(had[:, :], consts[:, 3 * P:4 * P]).then_inc(s_w2, 16)
            sp.dma_start(vec[:, :, :], vecs).then_inc(s_vec, 16)
            def load_q(g, b, kv, par):
                need(sp, q_in[par], (g // 2) * 48)
                for j in range(3):
                    sp.dma_start(
                        q_all[24 * j:24 * j + 24, bass.ds(g * (GQ * T), GQ * T)]
                        .rearrange("r (h t) -> r h t", h=GQ),
                        q_dram[:, :, b * T:(b + 1) * T]
                        .rearrange("i (d h) t -> (i d) h t", d=HD)
                        [:, kv * GQ:(kv + 1) * GQ, :]).then_inc(q_in[par], 16)

            for b in range(B):
                sp.wait_ge(k_split, b + 1)
                sp.dma_start(k_dram[:, :, b * T:(b + 1) * T].rearrange("j r t -> r j t"),
                             kparts[:, :, :]).then_inc(k_spilled, 16)
                sp.wait_ge(q_split0, b + 1)
                sp.wait_ge(q_split1, b + 1)
                for i in range(3):
                    sp.dma_start(
                        q_dram[i, :, b * T:(b + 1) * T].rearrange("(m p) t -> p m t", p=P),
                        qparts[:, i, :, :]).then_inc(q_spilled, 16)
                sp.wait_ge(k_spilled, 16 * (b + 1))
                if b == 0:
                    sp.wait_ge(s_ready, 3)
                for j in range(3):
                    for i in range(3):
                        r = 24 * j + 8 * i
                        sp.dma_start(
                            k_all[r:r + 8, b * NKV * T:(b + 1) * NKV * T]
                            .rearrange("d (k t) -> d k t", k=NKV),
                            k_dram[j, :, b * T:(b + 1) * T]
                            .rearrange("(d k) t -> d k t", d=HD)).then_inc(k_in[b], 16)
                sp.wait_ge(q_spilled, 48 * (b + 1))
                for kv in range(NKV):
                    load_q(b * NKV + kv, b, kv, kv % 2)
            sp.wait_ge(st_full, 10 * NKV)
            for w, dst in ((w1, w1raw), (w3, w3raw)):
                sp.dma_start(dst[:, :, :], w.rearrange("(k p) h -> p k h", p=P))\
                    .then_inc(s_post, 16)
            sp.dma_start(rwraw[:, :, :, :], mix_w.rearrange("w (k p) o -> p w k o", p=P))\
                .then_inc(s_rw, 16)
            sp.wait_ge(att_ready, NG)
            sp.dma_start(gate_raw[:, :, :], route_w.rearrange("(k p) o -> p k o", p=P))\
                .then_inc(s_tail, 16)
            sp.dma_start(iota[:, :], consts[:, 4 * P:4 * P + E]).then_inc(s_tail, 16)
            sp.dma_start(bo_sb[:, :], bo.to_broadcast((P, D))).then_inc(s_tail, 16)

            sp.wait_ge(z_done, 2)

            def load_chunk(v, place):
                if not isinstance(v, int) or v >= PLACES:
                    sp.wait_ge(m_lo_ready, v - (PLACES - 1))
                elif v == 2:
                    sp.wait_ge(down_done, B * HC)
                sp.dma_start(mraw[:, place, :],
                             moe_w[bass.ds(v % MC, 1)].rearrange("o p f -> p (o f)"))\
                    .then_inc(m_loaded[place], 16)
            for v in range(PLACES):
                load_chunk(v, v)
            with sp.Fori(1, MC * B // PLACES) as i:
                for r in range(PLACES):
                    load_chunk(i * PLACES + r, r)
            for b in range(B):
                sp.wait_ge(x_new, 3 * B + b + 1)
                sp.dma_start(out_rows[:, b * TPB:(b + 1) * TPB, :],
                             xa[:, b * TPB:(b + 1) * TPB, :]).then_inc(s_out, 16)
            sp.wait_ge(s_out, 16 * B)

        @block.gpsimd
        def _(pool):
            chain = Chain(pool, s_pool)
            chain.step(pool.memset(zero[:], 0.0))
            chain.settle()
            none = zero[:, :, :].to_broadcast((P, TPB, GQ))
            pool.memset(ones[:], 1.0).then_inc(s_ready, 1)
            pool.memset(halfneg[:], -0.5).then_inc(s_ready, 1)
            pool.wait_ge(s_ready, 2)
            pool.memset(k_all[64:96, :].bitcast(U32), 0x3F803F80).then_inc(s_ready, 1)
            pool.wait_ge(s_ready, 3)
            chain.step(pool.memset(v_all[:, :], 0.0))
            pool.dma_start(identb[:], consts[:, 0:P]).then_inc(s_constb, 16)
            pool.dma_start(hide_cols[:], consts[:, P:2 * P]).then_inc(s_constb, 16)
            pool.dma_start(hide_rows[:], consts[:, 2 * P:3 * P]).then_inc(s_constb, 16)
            chain.settle()
            pool.memset(v_all[:, :].rearrange("p (a c) -> p a c", c=32)[:, :, HD:HD + 1],
                        1.0).then_inc(s_ready, 1)
            pool.wait_ge(s_ready, 4)

            def power(n):
                b = n if n < 2 else (n // 2 - 1) % 2 if n < 14 else n % 2
                h = slice(b * TPB, (b + 1) * TPB)
                pool.wait_ge(ln_var, n + 1)
                pool.tensor_tensor(rstd[:, h], ve[:, h], halfneg[:, h], ALU.pow)\
                    .then_inc(ln_rstd, 1)
            power(0)
            power(1)
            pool.wait_ge(s_w2, 32)
            src, dst = w2a, w2b
            for width in (1, 2, 4):
                a4 = src[:, :, :].rearrange("p (n two w) d -> p n two (w d)", two=2, w=width)
                b4 = dst[:, :, :].rearrange("p (n two w) d -> p n two (w d)", two=2, w=width)
                chain.step(pool.tensor_tensor(b4[:, :, 0], a4[:, :, 0], a4[:, :, 1], ALU.add))
                chain.step(pool.tensor_tensor(b4[:, :, 1], a4[:, :, 0], a4[:, :, 1],
                                              ALU.subtract))
                chain.settle()
                src, dst = dst, src
            pool.tensor_copy(w2hi[:, :, :], w2b[:, :, :]).then_inc(butterfly, 1)
            pool.wait_ge(butterfly, 1)
            pool.tensor_tensor(w2lo[:, :, :], w2b[:, :, :], w2hi[:, :, :].bitcast(F32),
                               ALU.subtract).then_inc(butterfly, 1)
            for b in range(B):
                pool.wait_ge(q_scaled, 2 * b + 2)
                if b >= 1:
                    pool.wait_ge(q_spilled, 48 * b)
                chain.step(pool.tensor_copy(qparts[:, 0, 1, :], qf[:, 1, :]))
                chain.settle()
                chain.step(pool.tensor_tensor(qf[:, 1, :], qf[:, 1, :], qparts[:, 0, 1, :],
                                              ALU.subtract))
                chain.settle()
                chain.step(pool.tensor_copy(qparts[:, 1, 1, :], qf[:, 1, :]))
                chain.settle()
                pool.tensor_tensor(qparts[:, 2, 1, :], qf[:, 1, :], qparts[:, 1, 1, :],
                                   ALU.subtract).then_inc(q_split1, 1)

            def slot(n, par, pair):
                if isinstance(n, int) and n in (15, 16):
                    k = n - 15
                    raw, hi, lo = ((w1raw, w1hi, w1lo), (w3raw, w3hi, w3lo))[k]
                    pool.wait_ge(w13_hi, k + 1)
                    pool.tensor_tensor(lo[:, :, :], raw[:, :, :], hi[:, :, :].bitcast(F32),
                                       ALU.subtract).then_inc(w13_lo, 1)
                if has(n, 1):
                    g = n - 1
                    need(pool, mrow_ready, g + 1)
                    for i in range(3):
                        pool.dma_start(
                            q_all[72 + i:73 + i, bass.ds(g * (GQ * T), GQ * T)]
                            .rearrange("o (h t) -> o h t", h=GQ),
                            mrow[GQ * i:GQ * i + GQ, par ^ 1, :]).then_inc(m_in[par ^ 1], 16)
                if has(n, 0):
                    g = n
                    need(pool, s1_read, g * 12 + 12)
                    need(pool, mt_full, g - 1)
                    chain.step(pool.tensor_tensor(m3[:, par, :, 0, :], negm[:, par, :, :], none, ALU.add))
                    chain.settle()
                    chain.step(pool.tensor_tensor(negr[:, par, :, :], negm[:, par, :, :],
                                                  m3[:, par, :, 0, :], ALU.subtract))
                    chain.settle()
                    chain.step(pool.tensor_tensor(m3[:, par, :, 1, :], negr[:, par, :, :], none, ALU.add))
                    chain.settle()
                    pool.tensor_tensor(m3[:, par, :, 2, :], negr[:, par, :, :],
                                       m3[:, par, :, 1, :], ALU.subtract).then_inc(msplit, 1)
                if isinstance(n, int) and n in (17, 18):
                    power(n - 15)
            slots(chain, slot, 6)
            power(4)
            power(5)
            pool.wait_ge(s_rw, 16)
            pool.wait_ge(pv_done, NG)
            pool.tensor_copy(rwhi[:, :, :, :], rwraw[:, :, :, :]).then_inc(rw_hi, 1)
            pool.wait_ge(rw_hi, 1)
            pool.tensor_tensor(rwlo[:, :, :, :], rwraw[:, :, :, :], rwhi[:, :, :, :].bitcast(F32),
                               ALU.subtract).then_inc(rw_lo, 1)
            pool.wait_ge(s_tail, 48)
            chain.step(pool.tensor_copy(gate_hi[:, :, :], gate_raw[:, :, :]))
            chain.settle()
            pool.tensor_tensor(gate_lo[:, :, :], gate_raw[:, :, :], gate_hi[:, :, :].bitcast(F32),
                               ALU.subtract).then_inc(gate_split, 1)
            pool.dma_start(select_sb[:, :], select).then_inc(s_select, 16)

            def mix_low(b, q):
                for k in range(DC):
                    pool.wait_ge(mix_hi, (3 * b + q) * DC + k + 1)
                    pool.tensor_tensor(m_lo[:, q, k, :], mixed[:, (3 * b + q) % 2, k, :],
                                       m_hi[:, q, k, :].bitcast(F32), ALU.subtract)\
                        .then_inc(mix_lo, 1)

            def chunk_low(v, place):
                pool.wait_ge(m_hi_ready, v + 1)
                pool.tensor_tensor(mslot_lo[:, place, :], mraw[:, place, :],
                                   mslot_hi[:, place, :].bitcast(F32), ALU.subtract)\
                    .then_inc(m_lo_ready, 1)

            power(6)
            power(7)
            for q in range(3):
                mix_low(0, q)
            for v in range(2):
                chunk_low(v, v)
            for n in range(8, 12):
                power(n)
            mix_low(1, 0)
            for v in range(MC):
                chunk_low(v + 2, (v + 2) % PLACES)
                if v < 2:
                    mix_low(1, v + 1)
                if v == OUT_AT:
                    power(12)
                if v == OUT_AT + 1:
                    power(13)
            for v in range(MC, MC + 2):
                chunk_low(v + 2, (v + 2) % PLACES)
            power(14)
            with pool.Fori(0, (MC - 2) // 4 - 1) as i:
                for r in range(4):
                    chunk_low(i * 4 + (MC + 4 + r), (MC + 4 + r) % PLACES)
            for v in range(2 * MC - 4, 2 * MC - 2):
                chunk_low(v + 2, (v + 2) % PLACES)
            power(15)

        @block.vector
        def _(dve):
            chain = Chain(dve, s_dve)
            dve.wait_ge(s_w, 64)
            for n in range(4):
                cols = DC * (64 if n in (1, 2) else D)
                dve.tensor_reduce(asum[:, n:n + 1], wraw[:, n, 0:cols], AX.X, ALU.add,
                                  apply_absolute_value=True).then_inc(s_abs, 1)
            for b in range(B):
                h = slice(b * TPB, (b + 1) * TPB)
                dve.wait_ge(s_x[b], 16)
                for t in range(b * TPB, (b + 1) * TPB):
                    chain.step(dve.bn_stats(st6[:, t, :], xa[:, t, :]))
                chain.settle()
                for t in range(b * TPB, (b + 1) * TPB):
                    chain.step(dve.bn_aggr(mv[:, t, :], st6[:, t, :]))
                chain.settle()
                dve.tensor_scalar(ve[:, h], mv[:, h, 1], LN_EPS, None, ALU.add).then_inc(ln_var, 1)
            dve.wait_ge(s_tot, 1)
            for n in range(4):
                count = D * (64 if n in (1, 2) else D)
                chain.step(dve.tensor_scalar(wsc[:, n:n + 1], ps[:, 7, n:n + 1], 1.0 / count,
                                             QUANT_EPS, ALU.mult, ALU.max))
            chain.settle()
            dve.scalar_tensor_tensor(qsc[:, :], wsc[:, 0:1], float(np.float32(HD) ** -0.5),
                                     wsc[:, 1:2], ALU.mult, ALU.mult).then_inc(s_scale, 1)
            dve.wait_ge(s_vec, 16)
            chain.step(dve.tensor_tensor(so2[:, :], wsc[:, 3:4], wsc[:, 3:4], ALU.mult))
            for q, v in enumerate(MIXES):
                chain.step(dve.tensor_scalar(omt[:, q, :], vec[:, v, :], -1.0, 1.0,
                                             ALU.mult, ALU.add))
            chain.step(dve.tensor_tensor(ubk[:, :], vec[:, UK, :], vec[:, BK, :], ALU.add))
            chain.step(dve.tensor_scalar(nwd[:, :], vec[:, WD, :], -1.0, None, ALU.mult))
            chain.settle()
            dve.wait_ge(s_w2, 32)
            dve.tensor_copy(hadr[:, :], had[:, :]).then_inc(w2_split, 1)
            chain.step(dve.tensor_tensor(ubw[:, :], ubk[:, :], vec[:, WD, :], ALU.subtract))
            for b in range(B):
                h = slice(b * TPB, (b + 1) * TPB)
                cs = slice(b * T, (b + 1) * T)
                dve.wait_ge(ln_rstd, b + 1)
                chain.step(dve.scalar_tensor_tensor(nmr[:, h], mv[:, h, 0], -1.0, rstd[:, h],
                                                    ALU.mult, ALU.mult))
                chain.settle()
                if b >= 1:
                    dve.wait_ge(tr_done, 2 * b)
                for t in range(TPB):
                    u = b * TPB + t
                    dve.tensor_scalar(xn0[:, t, :], xa[:, u, :], rstd[:, u:u + 1], nmr[:, u:u + 1],
                                      ALU.mult, ALU.add).then_inc(ln_rows, 1)
                for k in range(DC):
                    dve.wait_ge(hi_done, 2 * b + k + 1)
                    dve.tensor_tensor(cols0_lo[:, k, cs], ps[:, 2 * b + k, :],
                                      cols0_hi[:, k, cs].bitcast(F32), ALU.subtract)\
                        .then_inc(lo_done, 1)
            for b in range(B):
                dve.wait_ge(k_scaled, b + 1)
                if b >= 1:
                    dve.wait_ge(k_spilled, 16 * b)
                chain.step(dve.tensor_copy(kparts[:, 0, :], kf[:, :]))
                chain.settle()
                chain.step(dve.tensor_tensor(kf[:, :], kf[:, :], kparts[:, 0, :], ALU.subtract))
                chain.settle()
                chain.step(dve.tensor_copy(kparts[:, 1, :], kf[:, :]))
                chain.settle()
                dve.tensor_tensor(kparts[:, 2, :], kf[:, :], kparts[:, 1, :], ALU.subtract)\
                    .then_inc(k_split, 1)
                dve.wait_ge(q_scaled, 2 * b + 1)
                if b >= 1:
                    dve.wait_ge(q_spilled, 48 * b)
                chain.step(dve.tensor_copy(qparts[:, 0, 0, :], qf[:, 0, :]))
                chain.settle()
                chain.step(dve.tensor_tensor(qf[:, 0, :], qf[:, 0, :], qparts[:, 0, 0, :],
                                             ALU.subtract))
                chain.settle()
                chain.step(dve.tensor_copy(qparts[:, 1, 0, :], qf[:, 0, :]))
                chain.settle()
                dve.tensor_tensor(qparts[:, 2, 0, :], qf[:, 0, :], qparts[:, 1, 0, :],
                                  ALU.subtract).then_inc(q_split0, 1)
                dve.wait_ge(kv_mm, 2 * b + 2)
                dve.wait_ge(s_ready, 4)
                dve.tensor_scalar(
                    v_all[:, :].rearrange("p (g s c) -> p g s c", g=NG, c=32)
                    [:, b * NKV:(b + 1) * NKV, :, 0:HD],
                    ps[:, 2 * b + 1, 0:TPB * 64].rearrange("p (s g d) -> p g s d", s=TPB, d=HD),
                    wsc[:, 2:3], None, ALU.mult).then_inc(v_stored, 1)

            dve.wait_ge(w2_hi_done, 1)
            dve.scalar_tensor_tensor(
                w2lo[:, :, :].rearrange("p c d -> p (c d)"),
                ps[:, 4:8, :].rearrange("p b f -> p (b f)"), 1.0 / 32,
                w2hi[:, :, :].bitcast(F32).rearrange("p c d -> p (c d)"), ALU.mult,
                ALU.subtract).then_inc(w2_lo_done, 1)

            def statistics(b, source):
                for t in range(TPB):
                    chain.step(dve.bn_stats(st6[:, b * TPB + t, :], source(t)))
                chain.settle()
                for t in range(TPB):
                    chain.step(dve.bn_aggr(mv[:, b * TPB + t, :], st6[:, b * TPB + t, :]))
                chain.settle()

            def out_stats(part, b):
                h = slice(b * TPB, (b + 1) * TPB)
                if part % 2 == 0:
                    dve.wait_ge(z_done, part + b + 1)
                elif part == 1:
                    dve.wait_ge(down_done, HC * (b + 1))
                else:
                    dve.wait_ge(down_done, HC * B + MC * (b + 1))
                if part == 2:
                    for pair in range(2):
                        dve.tensor_tensor(
                            rows[:, b * TPB + 2 * pair:b * TPB + 2 * pair + 2, :],
                            ps[:, z_bank(part, b) + pair, :].rearrange("p (t d) -> p t d", t=2),
                            bo_sb[:, :].unsqueeze(1).to_broadcast((P, 2, D)), ALU.add)\
                            .then_inc(z_biased, 1)
                    dve.wait_ge(z_biased, 2 * b + 2)
                    statistics(b, lambda t: rows[:, b * TPB + t, :])
                else:
                    statistics(b, lambda t: z_tile(part, b, t))
                if part == 0:
                    dve.tensor_scalar(ve[:, h], mv[:, h, 1], so2[:, 0:1], LN_EPS,
                                      ALU.mult, ALU.add).then_inc(ln_var, 1)
                else:
                    dve.tensor_scalar(ve[:, h], mv[:, h, 1], LN_EPS, None, ALU.add)\
                        .then_inc(ln_var, 1)

            def out_apply(part, b):
                old, new = ((xa, xb), (xb, xa))[part % 2]
                h = slice(b * TPB, (b + 1) * TPB)
                n = 2 + part * 4 + 2 * b if part < 3 else 14 + b
                dve.wait_ge(ln_rstd, n + 1)
                if part == 0:
                    chain.step(dve.tensor_scalar(rstd[:, h], rstd[:, h], wsc[:, 3:4], None,
                                                 ALU.mult))
                    chain.settle()
                else:
                    dve.wait_ge(x_new, (part - 1) * B + b + 1)
                chain.step(dve.scalar_tensor_tensor(nmrz[:, h], mv[:, h, 0], -1.0, rstd[:, h],
                                                    ALU.mult, ALU.mult))
                for t in range(b * TPB, (b + 1) * TPB):
                    z = rows[:, t, :] if part == 2 else z_tile(part, b, t - b * TPB)
                    dve.scalar_tensor_tensor(new[:, t, :], z, rstd[:, t:t + 1], old[:, t, :],
                                             ALU.mult, ALU.add).then_inc(z_read, 1)
                if part < 3:
                    dve.wait_ge(z_read, (part * B + b + 1) * TPB)
                    statistics(b, lambda t: new[:, b * TPB + t, :])
                    dve.tensor_scalar(ve[:, h], mv[:, h, 1], LN_EPS, None, ALU.add)\
                        .then_inc(ln_var, 1)

            def in_apply(part, b):
                new = (xb, xa)[part % 2]
                h = slice(b * TPB, (b + 1) * TPB)
                dve.wait_ge(ln_rstd, 2 + part * 4 + 2 * b + 2)
                chain.step(dve.scalar_tensor_tensor(nmr[:, h], mv[:, h, 0], -1.0, rstd[:, h],
                                                    ALU.mult, ALU.mult))
                chain.settle()
                for t in range(b * TPB, (b + 1) * TPB):
                    dve.tensor_scalar(rows[:, t, :], new[:, t, :], rstd[:, t:t + 1],
                                      nmr[:, t:t + 1], ALU.mult, ALU.add).then_inc(rows_ready, 1)

            def split_low(turn, b):
                for k in range(DC):
                    dve.wait_ge(cols_h, DC * TURNS[turn, b] + k + 1)
                    dve.tensor_tensor(cols_lo[:, k, b * T:(b + 1) * T],
                                      ps[:, col_bank(turn, b, k), :],
                                      cols_hi[:, k, b * T:(b + 1) * T].bitcast(F32),
                                      ALU.subtract).then_inc(cols_l, 1)

            def slot(n, par, pair):
                for u, (qt, h0, nh) in enumerate(UNITS):
                    if has(n, 0):
                        g = n
                        if u == 0:
                            need(dve, msplit, g - 1)
                        need(dve, s1_full, g * 12 + u + 1)
                        w = (qt + 1) * P
                        dve.tensor_reduce(
                            negm[:, par, qt, h0:h0 + nh],
                            ps[:, u % 4, 0:nh * w].rearrange("p (h t) -> p h t", h=nh),
                            AX.X, ALU.max, negate=True).then_inc(s1_read, 1)
                    if u == 2 and has(n, 2):
                        g = n - 2
                        need(dve, pv_done, g - 1)
                        dve.tensor_scalar(v_now[:, par, :, :].rearrange("p s c -> p (s c)"),
                                          v_all[:, bass.ds(g * (TPB * 32), TPB * 32)],
                                          1.0, None, ALU.mult).then_inc(v_ready, 1)
                    if u == 6 and has(n, 1):
                        g = n - 1
                        need(dve, mt_full, g + 1)
                        need(dve, m_in[par ^ 1], (pair - 1 + par) * 48)
                        dve.tensor_copy(mrow[:, par ^ 1, :], mt_bank)\
                            .then_inc(mrow_ready, 1)
                    if u == 4 and has(n, 4):
                        g = n - 4
                        need(dve, ot_full, g + 1)
                        o4 = ps[:, 7, :].rearrange("p (s h c) -> p s h c", s=TPB, h=GQ)
                        chain.step(dve.reciprocal(rsum[:, par, :, :], o4[:, :, :, HD]))
                        chain.settle()
                        dve.tensor_tensor(
                            att4[:, bass.ds(g // 4 * TPB, TPB), bass.ds(g % 4 * 32, 32)]
                            .rearrange("p s (h d) -> p s h d", h=GQ),
                            o4[:, :, :, 0:HD],
                            rsum[:, par, :, :].unsqueeze(3).to_broadcast((P, TPB, GQ, HD)),
                            ALU.mult).then_inc(att_ready, 1)
                if isinstance(n, int) and n == 16:
                    split_low(0, 0)
                if isinstance(n, int) and n == 17:
                    out_stats(0, 0)
                    out_apply(0, 0)
                if isinstance(n, int) and n == 18:
                    in_apply(0, 0)
            mt_bank = ps[0:3 * GQ, 6, 0:T // 2].bitcast(BF16)
            att4 = att[:, :].rearrange("p (g s c) -> p (g s) c", s=TPB, c=4 * 32)
            slots(chain, slot, 2)

            split_low(1, 0)
            split_low(0, 1)

            def mlp_unit(u):
                par, bank = u % 2, 2 * (u % 2)
                dve.wait_ge(silu_done, u + 1)
                dve.wait_ge(up_u, u + 1)
                if u >= 2:
                    dve.wait_ge(h_hi_done, u - 1)
                dve.tensor_tensor(hf[:, par, :], sg[:, par, :], ps[:, bank + 1, :], ALU.mult)\
                    .then_inc(mul_done, 1)
                dve.wait_ge(h_hi_done, u + 1)
                if u >= 2:
                    dve.wait_ge(down_done, u - 1)
                dve.tensor_tensor(h_lo[:, par, :], hf[:, par, :], h_hi[:, par, :].bitcast(F32),
                                  ALU.subtract).then_inc(h_lo_done, 1)

            def mixes(b, q):
                for k in range(DC):
                    n = (3 * b + q) * DC + k
                    dve.wait_ge(mix_tmp, n + 1)
                    if n >= 2 * DC:
                        dve.wait_ge(mix_lo, n - 2 * DC + 1)
                    dve.scalar_tensor_tensor(
                        mixed[:, (3 * b + q) % 2, k, :], xT[:, k, 1:T + 1],
                        vec[:, MIXES[q], k:k + 1], mix[:, k, :], ALU.mult, ALU.add)\
                        .then_inc(mix_done, 1)

            def read_keys(b):
                dve.wait_ge(mix_done, 3 * (b + 1) * DC)
                for m in range(DC):
                    dve.wait_ge(proj_k, 2 * b + m + 1)
                    dve.tensor_scalar(decay[:, m, :], ps[:, 4 + 2 * b + m, :], ubk[:, m:m + 1],
                                      vec[:, WD, m:m + 1], ALU.add, ALU.max).then_inc(k_read, 1)
                    dve.tensor_scalar(gain[:, m, :], ps[:, 4 + 2 * b + m, :], ubw[:, m:m + 1],
                                      0.0, ALU.add, ALU.min).then_inc(k_read, 1)

            def scan(b, m, step):
                if step == 0:
                    dve.wait_ge(gain_done, 2 * b + m + 1)
                    dve.wait_ge(mix_lo, 3 * (b + 1) * DC)
                    dve.wait_ge(proj_v, 2 * b + m + 1)
                    dve.scalar_tensor_tensor(num[:, m, :], ps[:, 4 + 2 * b + m, :],
                                             vec[:, BV, m:m + 1], gain[:, m, :], ALU.add,
                                             ALU.mult).then_inc(v_read, 1)
                    chain.step(dve.tensor_tensor_scan(den[:, m, :], decay[:, m, :],
                                                      gain[:, m, :], 0.0, ALU.mult, ALU.add))
                    dve.wait_ge(v_read, 2 * b + m + 1)
                    chain.step(dve.tensor_tensor_scan(num[:, m, :], decay[:, m, :],
                                                      num[:, m, :], 0.0, ALU.mult, ALU.add))
                    chain.settle()
                elif step < 3:
                    part = slice((step - 1) * T // 2, step * T // 2)
                    chain.step(dve.reciprocal(gain[:, m, part], den[:, m, part]))
                else:
                    chain.settle()
                    chain.step(dve.tensor_tensor(num[:, m, :], num[:, m, :], gain[:, m, :],
                                                 ALU.mult))
                    chain.settle()
                    dve.wait_ge(proj_r, 2 * b + m + 1)
                    dve.scalar_tensor_tensor(den[:, m, :], ps[:, 4 + 2 * b + m, :],
                                             vec[:, BR, m:m + 1], num[:, m, :], ALU.add,
                                             ALU.mult).then_inc(wkv_done, 1)
                    dve.wait_ge(wkv_hi, 2 * b + m + 1)
                    dve.tensor_tensor(cols_lo[:, m, b * T:(b + 1) * T], den[:, m, :],
                                      cols_hi[:, m, b * T:(b + 1) * T].bitcast(F32),
                                      ALU.subtract).then_inc(wkv_lo, 1)

            def start_columns(b):
                if b >= 1:
                    dve.wait_ge(wkv_lo, DC * b)
                dve.memset(xT[:, :, 0:1], 0.0).then_inc(xt_zero, 1)

            dve.wait_ge(pv_done, NG)
            start_columns(0)
            for u in range(B * HC):
                mlp_unit(u)
                if u == 1:
                    out_stats(0, 1)
                if u == 2:
                    out_apply(0, 1)
                if u == 3:
                    in_apply(0, 1)
                if u == 5:
                    split_low(1, 1)
                if u == HC - 1:
                    out_stats(1, 0)
                if u == HC:
                    out_apply(1, 0)
                    in_apply(1, 0)
                if 9 <= u < 12:
                    mixes(0, u - 9)
                if u == 12:
                    read_keys(0)
                if u == 13:
                    scan(0, 0, 0)
                    scan(0, 1, 0)
                if u == 14:
                    scan(0, 0, 1)
            for m, step in SCAN_STEPS[3:]:
                scan(0, m, step)
            start_columns(1)
            out_stats(1, 1)
            out_apply(1, 1)
            out_stats(2, 0)
            in_apply(1, 1)
            out_apply(2, 0)
            in_apply(2, 0)
            split_low(3, 0)
            mixes(1, 0)

            def route(b):
                h = slice(b * TPB, (b + 1) * TPB)
                dve.wait_ge(route_mm, b + 1)
                chain.step(dve.tensor_copy(
                    logits[:, h, :],
                    ps[:, 4 + 2 * b, 0:TPB * RW].rearrange("p (t c) -> p t c", c=RW)))
                chain.settle()
                for t in range(b * TPB, (b + 1) * TPB):
                    chain.step(dve.max(top8[:, t, :], logits[:, t, 0:E]))
                chain.settle()
                for t in range(b * TPB, (b + 1) * TPB):
                    chain.step(dve.max_index(topi[:, t, :], top8[:, t, :], logits[:, t, 0:E]))
                chain.step(dve.tensor_tensor(
                    wtop[:, h, 0:TOPK], top8[:, h, 0:TOPK],
                    top8[:, h, 0:1].to_broadcast((P, TPB, TOPK)), ALU.subtract))
                chain.step(dve.tensor_scalar(wtop[:, h, TOPK], logits[:, h, E], -1.0, None,
                                             ALU.mult))
                chain.settle()
                dve.tensor_copy(topf[:, h, :], topi[:, h, :]).then_inc(route_ex, 1)
                dve.wait_ge(route_exp, b + 1)
                dve.wait_ge(route_ex, b + 1)
                chain.step(dve.tensor_reduce(wsum[:, h, 0], wtop[:, h, 0:TOPK], AX.X, ALU.add))
                chain.step(dve.tensor_scalar(wsum[:, h, 1], wtop[:, h, TOPK], 1.0, None, ALU.add))
                chain.settle()
                chain.step(dve.reciprocal(wsum[:, h, :], wsum[:, h, :]))
                if b >= 1:
                    dve.wait_ge(route_t, b)
                chain.step(dve.memset(cb[:, :, :], 0.0))
                chain.settle()
                chain.step(dve.tensor_tensor(
                    wtop[:, h, 0:TOPK], wtop[:, h, 0:TOPK],
                    wsum[:, h, 0:1].to_broadcast((P, TPB, TOPK)), ALU.mult))
                chain.settle()
                for k in range(TOPK):
                    dst = comb if k == 0 else eq
                    if k > 1:
                        chain.settle()
                    for t in range(TPB):
                        u = b * TPB + t
                        chain.step(dve.tensor_scalar(
                            dst[:, t, 0:E], iota[:, :], topf[:, u, k:k + 1],
                            wtop[:, u, k:k + 1], ALU.is_equal, ALU.mult))
                    if k:
                        chain.settle()
                        chain.step(dve.tensor_tensor(comb[:, :, 0:E], comb[:, :, 0:E],
                                                     eq[:, :, :], ALU.add))
                chain.step(dve.tensor_copy(comb[:, :, E], wsum[:, h, 1]))
                for i in range(3):
                    chain.settle()
                    chain.step(dve.tensor_copy(cb[:, :, i * E:(i + 1) * E], comb[:, :, 0:E]))
                    if i == 2:
                        chain.settle()
                        dve.tensor_copy(cb[:, :, 3 * E + i], comb[:, :, E]).then_inc(route_rows, 1)
                    else:
                        chain.step(dve.tensor_copy(cb[:, :, 3 * E + i], comb[:, :, E]))
                        chain.settle()
                        chain.step(dve.tensor_tensor(comb[:, :, 0:E], comb[:, :, 0:E],
                                                     cb[:, :, i * E:(i + 1) * E], ALU.subtract))
                        chain.step(dve.tensor_tensor(comb[:, :, E], comb[:, :, E],
                                                     cb[:, :, 3 * E + i], ALU.subtract))

            def keep_route(b):
                dve.wait_ge(route_t, b + 1)
                dve.tensor_copy(ct[:, b * T:(b + 1) * T],
                                ps[:, 5 + 2 * b, 0:T // 2].bitcast(BF16)).then_inc(route_cols, 1)

            route(0)
            keep_route(0)

            def expert_unit(v, r, par):
                u = v + HC * B
                dve.wait_ge(silu_done, u + 1)
                dve.wait_ge(up_u, u + 1)
                dve.tensor_tensor(sg[:, par, :], sg[:, par, :], ps[:, (3 * r + 1) % 4, :],
                                  ALU.mult).then_inc(t_done, 1)
                dve.wait_ge(t_done, v + 1)
                dve.wait_ge(bc_full, v + 1)
                dve.wait_ge(h_hi_done, u - 1)
                dve.tensor_tensor(hf[:, par, :], sg[:, par, :], ps[:, (3 * r + 2) % 4, :],
                                  ALU.mult).then_inc(mul_done, 1)
                dve.wait_ge(h_hi_done, u + 1)
                dve.wait_ge(down_done, u - 1)
                dve.tensor_tensor(h_lo[:, par, :], hf[:, par, :], h_hi[:, par, :].bitcast(F32),
                                  ALU.subtract).then_inc(h_lo_done, 1)

            for v in range(MC):
                expert_unit(v, v % 4, v % 2)
                if v < 2:
                    mixes(1, v + 1)
                if v == 1:
                    read_keys(1)
                if SCAN_AT <= v < SCAN_AT + 8:
                    scan(1, *SCAN_STEPS[v - SCAN_AT])
                if v == OUT_AT:
                    out_stats(2, 1)
                if v == OUT_AT + 1:
                    out_apply(2, 1)
                if v == OUT_AT + 2:
                    in_apply(2, 1)
                if v == COL_AT:
                    split_low(3, 1)
                if v == ROUTE_AT:
                    route(1)
                if v == ROUTE_AT + 3:
                    keep_route(1)
            for v in range(MC, MC + 2):
                expert_unit(v, v % 4, v % 2)
            out_stats(3, 0)
            out_apply(3, 0)
            with dve.Fori(0, (MC - 2) // 4) as i:
                for r in range(4):
                    expert_unit(i * 4 + (MC + 2 + r), (MC + 2 + r) % 4, r % 2)
            out_stats(3, 1)
            out_apply(3, 1)

        @block.scalar
        def _(act):
            act.wait_ge(s_w, 64)
            for n in range(4):
                cols = DC * (64 if n in (1, 2) else D)
                act.activation(wsg[:, n, 0:cols], wraw[:, n, 0:cols], ACT.Sign)\
                    .then_inc(s_sign, 1)
            for b in range(B):
                cs = slice(b * T, (b + 1) * T)
                for k in range(DC):
                    act.wait_ge(tr_done, 2 * b + k + 1)
                    act.copy(cols0_hi[:, k, cs], ps[:, 2 * b + k, :]).then_inc(hi_done, 1)
            act.wait_ge(s_scale, 1)
            for b in range(B):
                act.wait_ge(kv_mm, 2 * b + 1)
                if b >= 1:
                    act.wait_ge(k_split, b)
                act.copy(kf[:, :], ps[0:64, 2 * b, :]).then_inc(k_scaled, 1)
                for m in range(DC):
                    act.wait_ge(q_mm, 2 * b + m + 1)
                    if b >= 1:
                        act.wait_ge([q_split0, q_split1][m], b)
                    act.mul(qf[:, m, :], ps[:, 4 + 2 * b + m, :], qsc[:, 0:1])\
                        .then_inc(q_scaled, 1)

            act.wait_ge(w2_mm, HC // 2)
            act.mul(w2hi[:, :, :], ps[:, 4:8, :].rearrange("p b (c d) -> p (b c) d", d=D),
                    1.0 / 32).then_inc(w2_hi_done, 1)

            def split_high(turn, b):
                for k in range(DC):
                    act.wait_ge(cols_full, DC * ALL_TURNS[turn, b] + k + 1)
                    act.copy(cols_hi[:, k, b * T:(b + 1) * T], ps[:, col_bank(turn, b, k), :])\
                        .then_inc(cols_h, 1)

            def shift(part, b):
                new = (xb, xa)[part % 2]
                if part < 3:
                    act.wait_ge(rows_ready, (part * B + b + 1) * TPB)
                for t in range(b * TPB, (b + 1) * TPB):
                    if part == 3:
                        act.wait_ge(z_read, 3 * TILES + t + 1)
                    ins = act.activation(new[:, t, :], new[:, t, :], ACT.Identity,
                                         bias=nmrz[:, t:t + 1])
                ins.then_inc(x_new, 1)

            def slot(n, par, pair):
                for u in range(10):
                    if has(n, 2):
                        g = n - 2
                        if u == 0:
                            need(act, pv_done, g - 1)
                        need(act, st_full, g * 10 + u + 1)
                        act.activation(probs[:, par, u, :], ps[:, 4 + u % 2, :], ACT.Exp)\
                            .then_inc(st_exp, 1)
                    if u == 7 and has(n, 3):
                        g = n - 3
                        need(act, pv_done, g + 1)
                        need(act, ot_full, g - 1)
                        act.copy(o_cols[:, par ^ 1, :], ps[:, 7, :]).then_inc(o_copied, 1)
                if isinstance(n, int) and n in (14, 15):
                    raw, hi = ((w1raw, w1hi), (w3raw, w3hi))[n - 14]
                    act.wait_ge(s_post, 32)
                    act.copy(hi[:, :, :], raw[:, :, :]).then_inc(w13_hi, 1)
                if isinstance(n, int) and n == 16:
                    split_high(0, 0)
            slots(act, slot)
            split_high(1, 0)
            split_high(0, 1)
            shift(0, 0)

            def silu(u, bank, par):
                act.wait_ge(up_g, u + 1)
                act.activation(sg[:, par, :], ps[:, bank, :], ACT.Silu).then_inc(silu_done, 1)

            def high(u, par):
                act.wait_ge(mul_done, u + 1)
                need(act, down_done, u - 1)
                act.copy(h_hi[:, par, :], hf[:, par, :]).then_inc(h_hi_done, 1)

            def columns(b):
                act.wait_ge(xt_zero, b + 1)
                for k in range(DC):
                    act.wait_ge(cols_full, DC * ALL_TURNS[2, b] + k + 1)
                    act.copy(xT[:, k, 1:T + 1], ps[:, col_bank(2, b, k), :]).then_inc(xt_ready, 1)

            def mixes(b, q):
                act.wait_ge(xt_ready, 2 * b + 2)
                at = (3 * b + q) % 2
                first = (3 * b + q) * DC
                for k in range(DC):
                    need(act, mix_done, first + k - 1)
                    act.mul(mix[:, k, :], xT[:, k, 0:T], omt[:, q, k:k + 1]).then_inc(mix_tmp, 1)
                if b >= 1:
                    act.wait_ge([proj_k, proj_v, proj_r][q], DC * b)
                for k in range(DC):
                    act.wait_ge(mix_done, first + k + 1)
                    if MIXES[q] == TMR:
                        act.activation(mixed[:, at, k, :], mixed[:, at, k, :], ACT.Silu)\
                            .then_inc(mix_silu, 1)
                        act.wait_ge(mix_silu, DC * b + k + 1)
                    act.copy(m_hi[:, q, k, :], mixed[:, at, k, :]).then_inc(mix_hi, 1)

            def exponents(b):
                for m in range(DC):
                    act.wait_ge(k_read, 4 * b + 2 * m + 2)
                    act.activation(decay[:, m, :], decay[:, m, :], ACT.Exp,
                                   bias=nwd[:, m:m + 1], scale=-1.0).then_inc(decay_done, 1)
                    act.activation(gain[:, m, :], gain[:, m, :], ACT.Exp).then_inc(gain_done, 1)

            def wkv_high(b, m):
                act.wait_ge(wkv_done, 2 * b + m + 1)
                act.copy(cols_hi[:, m, b * T:(b + 1) * T], den[:, m, :]).then_inc(wkv_hi, 1)

            def chunk_high(v, place, turn):
                act.wait_ge(m_loaded[place], turn * 16 + 16)
                need(act, down_done, v + (B * HC - PLACES + 1) if not isinstance(v, int)
                     else max(v - PLACES, -2) + 1 + B * HC)
                act.copy(mslot_hi[:, place, :], mraw[:, place, :]).then_inc(m_hi_ready, 1)

            for u in range(B * HC):
                par = u % 2
                need(act, mul_done, u - 1)
                silu(u, 2 * par, par)
                high(u, par)
                if u == 5:
                    split_high(1, 1)
                    shift(0, 1)
                if u == 9:
                    columns(0)
                    mixes(0, 0)
                if u == 10:
                    mixes(0, 1)
                if u == 11:
                    mixes(0, 2)
                    shift(1, 0)
                if u == 12:
                    exponents(0)
            chunk_high(0, 0, 0)
            chunk_high(1, 1, 0)
            wkv_high(0, 0)
            wkv_high(0, 1)
            columns(1)
            split_high(3, 0)
            mixes(1, 0)
            shift(1, 1)
            shift(2, 0)

            def route(b):
                h = slice(b * TPB, (b + 1) * TPB)
                act.wait_ge(route_ex, b + 1)
                act.activation(wtop[:, h, :], wtop[:, h, :], ACT.Exp).then_inc(route_exp, 1)
            route(0)

            def expert(u, r, par):
                act.wait_ge(mul_done, u - 1)
                silu(u, (3 * r) % 4, par)
                high(u, par)

            for v in range(MC):
                expert(v + HC * B, v % 4, v % 2)
                chunk_high(v + 2, (v + 2) % PLACES, (v + 2) // PLACES)
                if v < 2:
                    mixes(1, v + 1)
                if v == 1:
                    exponents(1)
                if v in (SCAN_AT + 4, SCAN_AT + 7):
                    wkv_high(1, v == SCAN_AT + 7)
                if v == COL_AT:
                    split_high(3, 1)
                    shift(2, 1)
                if v == ROUTE_AT:
                    route(1)
            for v in range(MC, MC + 2):
                expert(v + HC * B, v % 4, v % 2)
                chunk_high(v + 2, (v + 2) % PLACES, (v + 2) // PLACES)
            shift(3, 0)
            with act.Fori(0, (MC - 2) // 4 - 1) as i:
                for r in range(4):
                    expert(i * 4 + (HC * B + MC + 2 + r), (MC + 2 + r) % 4, r % 2)
                    chunk_high(i * 4 + (MC + 4 + r), (MC + 4 + r) % PLACES,
                               i + (MC + 4 + r) // PLACES)
            for v in range(2 * MC - 4, 2 * MC):
                expert(v + HC * B, v % 4, v % 2)
                if v + 2 < 2 * MC:
                    chunk_high(v + 2, (v + 2) % PLACES, (v + 2) // PLACES)
            shift(3, 1)

        @block.tensor
        def _(pe):
            pe.wait_ge(s_ready, 1)
            pe.wait_ge(s_abs, 4)
            pe.matmul(ps[:, 7, 0:4], ones[:, :], asum[:, :], start=True, stop=True)\
                .then_inc(s_tot, 1)
            pe.wait_ge(s_const, 16)
            pe.wait_ge(s_constb, 48)
            for b in range(B):
                for k in range(DC):
                    for t in range(TPB):
                        pe.wait_ge(ln_rows, b * TPB + t + 1)
                        mm = pe.transpose(ps[:, 2 * b + k, t * P:(t + 1) * P],
                                          xn0[:, t, k * P:(k + 1) * P], ident[:, :])
                    mm.then_inc(tr_done, 1)
            pe.wait_ge(s_sign, 4)
            pe.wait_ge(s_scale, 1)
            for b in range(B):
                cs = slice(b * T, (b + 1) * T)
                pe.wait_ge(lo_done, 2 * b + 2)
                parts = [(k, c) for k in range(DC) for c in (cols0_hi, cols0_lo)]
                for n, (k, c) in enumerate(parts):
                    mm = pe.matmul(ps[0:64, 2 * b, :], wsg[:, 1, k * 64:(k + 1) * 64],
                                   c[:, k, cs], start=(n == 0), stop=(n == 3))
                mm.then_inc(kv_mm, 1)
                for m in range(DC):
                    for n, (k, c) in enumerate(parts):
                        mm = pe.matmul(ps[:, 4 + 2 * b + m, :],
                                       wsg[:, 0, k * D + m * P:k * D + (m + 1) * P],
                                       c[:, k, cs], start=(n == 0), stop=(n == 3))
                    mm.then_inc(q_mm, 1)
                for t in range(TPB):
                    ts = slice(b * T + t * P, b * T + (t + 1) * P)
                    for n, (k, c) in enumerate(parts):
                        mm = pe.matmul(ps[:, 2 * b + 1, t * 64:(t + 1) * 64], c[:, k, ts],
                                       wsg[:, 2, k * 64:(k + 1) * 64],
                                       start=(n == 0), stop=(n == 3))
                mm.then_inc(kv_mm, 1)
            pe.wait_ge(butterfly, 2)
            pe.wait_ge(q_scaled, 2 * B)
            pe.wait_ge(w2_split, 1)
            for c in range(4):
                for n, half in enumerate((w2hi, w2lo)):
                    mm = pe.matmul(ps[:, 4 + c, :], hadr[:, :],
                                   half[:, 2 * c:2 * c + 2, :].rearrange("p c d -> p (c d)"),
                                   start=(n == 0), stop=(n == 1))
                mm.then_inc(w2_mm, 1)
            pe.wait_ge(w2_lo_done, 1)
            pe.wait_ge(q_scaled, 2 * B)
            pe.wait_ge(v_stored, B)

            def score_rows(g, u):
                qt, h0, nh = UNITS[u]
                need(pe, s1_read, g * 12 + u - 3)
                w = (qt + 1) * P
                for h in range(h0, h0 + nh):
                    c = (h - h0) * w
                    pe.matmul(ps[:, u % 4, c:c + w],
                              q_all[0:72, bass.ds(g * (GQ * T) + (h * T + qt * P), P)],
                              k_all[0:72, bass.ds(g * T, w)], start=True, stop=False)
                    mm = pe.matmul(ps[:, u % 4, c + w - P:c + w], identb[:, :], hide_cols[:, :],
                                   start=False, stop=True)
                mm.then_inc(s1_full, 1)

            def score_cols(g, u):
                need(pe, st_exp, g * 10 + u - 1)
                for kt, h, c in PIECES[u]:
                    w = T - kt * P
                    pe.matmul(ps[:, 4 + u % 2, c:c + w],
                              k_all[0:75, bass.ds(g * T + kt * P, P)],
                              q_all[0:75, bass.ds(g * (GQ * T) + (h * T + kt * P), w)],
                              start=True, stop=False)
                    mm = pe.matmul(ps[:, 4 + u % 2, c:c + P], identb[:, :], hide_rows[:, :],
                                   start=False, stop=True)
                mm.then_inc(st_full, 1)


            def transposes(turn, b, tile):
                for k in range(DC):
                    for t in range(TPB):
                        mm = pe.transpose(ps[:, col_bank(turn, b, k), t * P:(t + 1) * P],
                                          tile(t, k), ident[:, :])
                    mm.then_inc(cols_full, 1)

            def rows_tile(b):
                return lambda t, k: rows[:, b * TPB + t, k * P:(k + 1) * P]

            att_v = att[:, :].rearrange("p (b k s c) -> p b k s c", b=B, k=DC, c=P)

            def att_tile(b):
                return lambda t, k: att_v[:, b, k, t, :]

            def out_product(b):
                pe.wait_ge(cols_l, DC * TURNS[0, b] + DC)
                for t in range(TPB):
                    ts = slice(b * T + t * P, b * T + (t + 1) * P)
                    for n, (k, c) in enumerate((k, c) for k in range(DC)
                                               for c in (cols_hi, cols_lo)):
                        mm = pe.matmul(z_tile(0, b, t), c[:, k, ts],
                                       wsg[:, 3, k * D:(k + 1) * D],
                                       start=(n == 0), stop=(n == 2 * DC - 1))
                mm.then_inc(z_done, 1)

            def three_passes(out, lhs_hi, lhs_lo, rhs_hi, rhs_lo, first, last):
                pe.matmul(out, lhs_hi, rhs_hi, start=first, stop=False)
                pe.matmul(out, lhs_lo, rhs_hi, start=False, stop=False)
                return pe.matmul(out, lhs_hi, rhs_lo, start=False, stop=last)

            def down(part, b, u, par, w_hi, w_lo, start):
                pe.wait_ge(h_lo_done, u + 1)
                for t in range(TPB):
                    ts = slice(t * P, (t + 1) * P)
                    pairs = ((h_hi, w_hi), (h_lo, w_hi), (h_hi, w_lo))
                    for n, (h, w) in enumerate(pairs):
                        mm = pe.matmul(z_tile(part, b, t), h[:, par, ts], w,
                                       start=start and n == 0 and t % 2 == 0, stop=False,
                                       skip_group_check=True)
                return mm

            mt_bank = ps[0:3 * GQ, 6, 0:T // 2].bitcast(BF16)

            def slot(n, par, pair):
                if has(n, 2):
                    need(pe, m_in[par], pair * 48)
                for u in range(12):
                    if has(n, 0):
                        g = n
                        if u == 0:
                            need(pe, q_in[par], pair * 48 + 48)
                            for b in range(B):
                                if not isinstance(g, int) or g // NKV == b:
                                    pe.wait_ge(k_in[b], 144)
                        score_rows(g, u)
                    if has(n, 2) and 1 <= u <= 10:
                        score_cols(n - 2, u - 1)
                    if u == 3 and has(n, 1):
                        g = n - 1
                        need(pe, msplit, g + 1)
                        need(pe, mrow_ready, g)
                        for s in range(TPB):
                            mm = pe.transpose(mt_bank[:, s * P:(s + 1) * P],
                                              m3[:, par ^ 1, s, :, :].rearrange("p i h -> p (i h)"),
                                              identb[:, :])
                        mm.then_inc(mt_full, 1)
                    if u == 1 and has(n, 4):
                        g = n - 4
                        need(pe, o_copied, g + 1)
                        for s in range(TPB):
                            mm = pe.transpose(ps[:, 7, s * P:(s + 1) * P],
                                              o_cols[:, par, s * P:(s + 1) * P], ident[:, :])
                        mm.then_inc(ot_full, 1)
                    if isinstance(n, int) and n == 16 and u == 2:
                        pe.wait_ge(att_ready, NKV)
                        pe.wait_ge(s1_read, 12 * NG)
                        transposes(0, 0, att_tile(0))
                    if isinstance(n, int) and n == 17 and u == 2:
                        out_product(0)
                    if u == 7 and has(n, 3):
                        g = n - 3
                        need(pe, att_ready, g)
                        need(pe, v_ready, g + 1)
                        need(pe, st_exp, g * 10 + 10)
                        for kt in range(TPB):
                            for h in range(GQ):
                                un, c = WHERE[kt, h]
                                w = T - kt * P
                                mm = pe.matmul(ps[32 * h:32 * h + 32, 7, kt * P:T],
                                               v_now[:, par ^ 1, kt, :],
                                               probs[:, par ^ 1, un, c:c + w],
                                               start=(kt == 0), stop=(kt == TPB - 1))
                        mm.then_inc(pv_done, 1)
            def mlp_up(u):
                b, j, bank = u // HC, u % HC, 2 * (u % 2)
                cs = slice(b * T, (b + 1) * T)
                js = slice(j * P, (j + 1) * P)
                for w, (hi, lo) in enumerate(((w1hi, w1lo), (w3hi, w3lo))):
                    need(pe, silu_done if w == 0 else mul_done, u - 1)
                    for k in range(DC):
                        mm = three_passes(ps[:, bank + w, :], hi[:, k, js], lo[:, k, js],
                                          cols_hi[:, k, cs], cols_lo[:, k, cs],
                                          k == 0, k == DC - 1)
                    mm.then_inc(up_u if w else up_g, 1)

            def mlp_down(u):
                b, j = u // HC, u % HC
                if j == 0:
                    pe.wait_ge(z_read, (b + 1) * TPB)
                mm = down(1, b, u, u % 2, w2hi[:, j, :], w2lo[:, j, :], j == 0)
                mm.then_inc(down_done, 1)

            slots(pe, slot)
            pe.wait_ge(rows_ready, TPB)
            transposes(1, 0, rows_tile(0))
            pe.wait_ge(att_ready, NG)
            transposes(0, 1, att_tile(1))
            pe.wait_ge(w13_lo, 2)
            pe.wait_ge(cols_l, DC * TURNS[1, 0] + DC)
            pe.wait_ge(pv_done, NG)

            def project(b, q, w, bank, done):
                pe.wait_ge(mix_lo, (3 * b + q + 1) * DC)
                for m in range(DC):
                    ms = slice(m * P, (m + 1) * P)
                    for k in range(DC):
                        mm = three_passes(ps[:, bank + m, :], rwhi[:, w, k, ms],
                                          rwlo[:, w, k, ms], m_hi[:, q, k, :],
                                          m_lo[:, q, k, :], k == 0, k == DC - 1)
                    mm.then_inc(done, 1)

            def keys(b):
                pe.wait_ge(rw_lo, 1)
                pe.wait_ge(xt_ready, 2 * b + 2)
                project(b, 0, 0, 4 + 2 * b, proj_k)

            def values(b):
                pe.wait_ge(k_read, 4 * b + 4)
                project(b, 1, 1, 4 + 2 * b, proj_v)

            def receptances(b):
                pe.wait_ge(v_read, 2 * b + 2)
                project(b, 2, 2, 4 + 2 * b, proj_r)

            def mix_out(b):
                pe.wait_ge(wkv_lo, 2 * b + 2)
                for t in range(TPB):
                    ts = slice(b * T + t * P, b * T + (t + 1) * P)
                    for k in range(DC):
                        mm = three_passes(z_tile(2, b, t), cols_hi[:, k, ts], cols_lo[:, k, ts],
                                          rwhi[:, 3, k, :], rwlo[:, 3, k, :],
                                          k == 0, k == DC - 1)
                mm.then_inc(z_done, 1)

            def logits_of(b):
                pe.wait_ge(gate_split, 1)
                pe.wait_ge(cols_l, DC * TURNS[3, b] + DC)
                for t in range(TPB):
                    ts = slice(b * T + t * P, b * T + (t + 1) * P)
                    for k in range(DC):
                        mm = three_passes(ps[:, 4 + 2 * b, t * RW:(t + 1) * RW],
                                          cols_hi[:, k, ts], cols_lo[:, k, ts],
                                          gate_hi[:, k, :], gate_lo[:, k, :],
                                          k == 0, k == DC - 1)
                mm.then_inc(route_mm, 1)

            def route_columns(b):
                pe.wait_ge(route_rows, b + 1)
                for t in range(TPB):
                    mm = pe.transpose(
                        ps[:, 5 + 2 * b, 0:T // 2].bitcast(BF16)[:, t * P:(t + 1) * P],
                        cb[:, t, :], identb[:, :])
                mm.then_inc(route_t, 1)

            def expert_up(v, r, b, chunk):
                u = v + HC * B
                cs = slice(b * T, (b + 1) * T)
                pe.wait_ge(m_lo_ready, v + 1)
                for w in range(2):
                    if w == 0:
                        pe.wait_ge(mul_done, u - 1)
                    else:
                        pe.wait_ge(silu_done, u)
                    for k in range(DC):
                        c = w * D + k * P
                        mm = three_passes(ps[:, (3 * r + w) % 4, :],
                                          mslot_hi[:, r, c:c + P], mslot_lo[:, r, c:c + P],
                                          cols_hi[:, k, cs], cols_lo[:, k, cs],
                                          k == 0, k == DC - 1)
                    mm.then_inc(up_u if w else up_g, 1)
                need(pe, t_done, v)
                if isinstance(v, int) and v == 0:
                    route_columns(0)
                if isinstance(chunk, int) and chunk == 0:
                    pe.wait_ge(route_cols, b + 1)
                pe.matmul(ps[:, (3 * r + 2) % 4, :], select_sb[:, bass.ds(chunk * P, P)],
                          ct[:, cs], start=True, stop=True).then_inc(bc_full, 1)

            def expert_down(v, r, b, start=False):
                par = r % 2
                down(3, b, v + HC * B, par, mslot_hi[:, r, 2 * D:3 * D],
                     mslot_lo[:, r, 2 * D:3 * D], start).then_inc(down_done, 1)

            mlp_up(0)
            out_product(1)
            for u in range(1, B * HC):
                if u == HC:
                    pe.wait_ge(cols_l, DC * TURNS[1, 1] + DC)
                mlp_up(u)
                if u == 10:
                    pe.wait_ge(rows_ready, 3 * TPB)
                    transposes(2, 0, rows_tile(0))
                mlp_down(u - 1)
                if u == 5:
                    pe.wait_ge(rows_ready, 2 * TPB)
                    transposes(1, 1, rows_tile(1))
                if u == 12:
                    keys(0)
                if u == 13:
                    values(0)
                if u == 14:
                    receptances(0)
            mlp_down(B * HC - 1)
            mix_out(0)
            pe.wait_ge(rows_ready, 4 * TPB)
            transposes(2, 1, rows_tile(1))
            pe.wait_ge(rows_ready, 5 * TPB)
            transposes(3, 0, rows_tile(0))
            logits_of(0)
            keys(1)
            pe.wait_ge(s_select, 16)

            expert_up(0, 0, 0, 0)
            for v in range(1, MC):
                expert_up(v, v % 4, 0, v)
                expert_down(v - 1, (v - 1) % 4, 0, start=v == 1)
                if v == 2:
                    values(1)
                if v == SCAN_AT + 2:
                    receptances(1)
                if v == SCAN_AT + 9:
                    mix_out(1)
                if v == COL_AT:
                    pe.wait_ge(rows_ready, 6 * TPB)
                    transposes(3, 1, rows_tile(1))
                if v == COL_AT + 1:
                    logits_of(1)
                if v == ROUTE_AT + 2:
                    route_columns(1)
            pe.wait_ge(cols_l, DC * TURNS[3, 1] + DC)
            for v in range(MC, MC + 2):
                expert_up(v, v % 4, 1, v - MC)
                expert_down(v - 1, (v - 1) % 4, 0 if v == MC else 1, start=v == MC + 1)
            with pe.Fori(0, (MC - 2) // 4) as i:
                for r in range(4):
                    q = (MC + 2 + r) % 4
                    expert_up(i * 4 + (MC + 2 + r), q, 1, i * 4 + (2 + r))
                    expert_down(i * 4 + (MC + 1 + r), (q + 3) % 4, 1)
            expert_down(2 * MC - 1, (2 * MC - 1) % 4, 1)


def kernel(**inputs):
    import numpy as _np
    import concourse.bacc as _bacc
    from concourse import mybir as _mybir
    from concourse.bass_utils import run_bass_kernel_spmd as _run

    a = {n: _np.asarray(v) for n, v in inputs.items()}

    def turned(w):
        return _np.ascontiguousarray(w.T)

    def by_part(w, heads):
        return _np.ascontiguousarray(
            w.reshape(D, heads, HD).transpose(0, 2, 1).reshape(D, heads * HD))

    def chunked(experts, shared):
        flat = _np.concatenate([
            experts.transpose(1, 0, 2).reshape(D, E * F), shared,
            _np.zeros((D, MC * P - E * F - SF), shared.dtype)], axis=1)
        return flat.reshape(DC, P, MC, P).transpose(2, 1, 0, 3).reshape(MC, P, D)

    place = _np.arange(P)
    had = _np.ones((1, 1), _np.float32)
    while had.shape[0] < P:
        had = _np.block([[had, had], [had, -had]])
    hide = _np.where(place[None, :] > place[:, None], _np.float32(MASKED), _np.float32(0))
    consts = _np.concatenate([
        _np.eye(P), hide, hide.T, had, _np.tile(_np.arange(E), (P, 1))], axis=1)
    feature = _np.arange(MC * P)
    select = _np.zeros((P, MC * P), _np.float32)
    for part in range(3):
        of_expert = feature < E * F
        select[part * E + feature[of_expert] // F, feature[of_expert]] = 1.0
        select[3 * E + part, E * F:E * F + SF] = 1.0

    moe = _np.concatenate([
        chunked(a["L1_ffn_wg"], a["L1_ffn_sg"]), chunked(a["L1_ffn_wu"], a["L1_ffn_su"]),
        _np.concatenate([
            a["L1_ffn_wd"].reshape(E * F, D), a["L1_ffn_sd"],
            _np.zeros((MC * P - E * F - SF, D), _np.float32)]).reshape(MC, P, D)], axis=2)
    vecs = _np.stack([a["L1_attn_" + n] for n in ("tmr", "tmk", "tmv", "u", "w", "bk", "bv", "br")])
    arrays = {
        "x": a["L0_attn_x"].reshape(N, D),
        "consts": consts.astype(_np.float32),
        "wq": by_part(a["L0_attn_wq"].T, NKV * GQ), "wk": by_part(a["L0_attn_wk"].T, NKV),
        "wv": turned(a["L0_attn_wv"]), "wo": turned(a["L0_attn_wo"]),
        "w1": turned(a["L0_ffn_W1"]), "w3": turned(a["L0_ffn_W3"]), "w2": turned(a["L0_ffn_W2"]),
        "mix_w": _np.stack([a["L1_attn_W" + n].T for n in "kvro"]),
        "vecs": vecs.reshape(8, DC, P).transpose(2, 0, 1),
        "bo": a["L1_attn_bo"].reshape(1, D),
        "route_w": _np.concatenate([
            a["L1_ffn_gate_w"], a["L1_ffn_seg"], _np.zeros((D, RW - E - 1), _np.float32)], axis=1),
        "moe_w": moe,
        "select": select,
    }
    nc = _bacc.Bacc("TRN2", target_bir_lowering=False, num_devices=1)
    aps, named = [], {}
    for name, v in arrays.items():
        v = _np.ascontiguousarray(v)
        named[f"in_{name}"] = v
        aps.append(nc.dram_tensor(f"in_{name}", v.shape, _mybir.dt.from_np(v.dtype),
                                  kind="ExternalInput").ap())
    aps.append(nc.dram_tensor("out_x", (N, D), _mybir.dt.float32, kind="ExternalOutput").ap())
    sandwich_kernel(nc, *aps)
    r = _run(nc, [named], core_ids=[0])
    return r.results[0]["out_x"].reshape(B, T, D)
```

```python
from contextlib import ExitStack, contextmanager

import numpy as np

import concourse.bass as bass
from concourse import mybir

F32 = mybir.dt.float32
F32R = mybir.dt.float32r
BF16 = mybir.dt.bfloat16
U32 = mybir.dt.uint32
ALU = mybir.AluOpType
ACT = mybir.ActivationFunctionType
AX = mybir.AxisListType

P = 128
D = 256
DC = D // P
B, T = 2, 512
N = B * T
TILES = N // P
TPB = T // P
NKV, GQ, HD = 8, 4, 8
NG = B * NKV
HID = 1024
HC = HID // P
E, TOPK, F, SF = 32, 4, 96, 704
MC = -(-(E * F + SF) // P)
PLACES = 4
RW = 34
TMR, TMK, TMV, UK, WD, BK, BV, BR = range(8)
MIXES = (TMK, TMV, TMR)
LN_EPS = 1e-5
QUANT_EPS = 1e-5
MASKED = -1e30


class Chain:

    def __init__(self, eng, sem):
        self.eng, self.sem, self.n, self.off = eng, sem, 0, 0

    def step(self, ins):
        ins.then_inc(self.sem, 1)
        self.n += 1
        return ins

    def settle(self):
        self.eng.wait_ge(self.sem, self.off + self.n)

    @contextmanager
    def loop(self, count, per):
        before = self.n
        with self.eng.Fori(0, count) as i:
            self.off = i * per
            yield i
            assert self.n - before == per, (self.n - before, per)
        self.off, self.n = 0, before + count * per


def need(eng, sem, value):
    if not isinstance(value, int) or value > 0:
        eng.wait_ge(sem, value)


def sandwich_kernel(nc, x, consts, wq, wk, wv, wo, w1, w3, w2, mix_w, vecs, bo, route_w, moe_w,
                    select, out):
    ctx = ExitStack()
    with ctx:
        def sem(name):
            return ctx.enter_context(nc.semaphore(name))

        at = [(nc.sbuf_base + 31) // 32 * 32]
        SIZE = {F32: 4, F32R: 4, BF16: 2, U32: 4}

        def sb(name, shape, dt):
            size = int(np.prod(shape[1:])) * SIZE[dt]
            t = nc.alloc_sbuf_tensor_at(name, shape, dt, offset=at[0])
            at[0] += (size + 31) // 32 * 32
            assert at[0] <= nc.sbuf_usable_end, (name, at[0])
            return t

        xa = sb("xa", [P, TILES, D], F32)
        xb = sb("xb", [P, TILES, D], F32)
        ident = sb("ident", [P, P], F32)
        identb = sb("identb", [P, P], BF16)
        had = sb("had", [P, P], F32)
        hadr = sb("hadr", [P, P], F32R)
        ones = sb("ones", [P, P], F32)
        zero = sb("zero", [P, 1, 1], F32)
        waited = sb("waited", [P, 3], F32)
        hide_cols = sb("hide_cols", [P, P], BF16)
        halfneg = sb("halfneg", [P, TILES], F32)
        st6 = sb("st6", [P, TILES, 6], F32)
        mv = sb("mv", [P, TILES, 2], F32)
        ve = sb("ve", [P, TILES], F32)
        rstd = sb("rstd", [P, TILES], F32)
        nmr = sb("nmr", [P, TILES], F32)
        nmrz = sb("nmrz", [P, TILES], F32)
        asum = sb("asum", [P, 4], F32)
        wsc = sb("wsc", [P, 4], F32)
        qsc = sb("qsc", [P, 1], F32)
        wsg_at = at[0]
        wsg = sb("wsg", [P, 4, DC * D], F32R)
        w2hi = sb("w2hi", [P, HC, D], F32R)
        w2lo = sb("w2lo", [P, HC, D], F32R)
        att_at = at[0]
        att = sb("att", [P, NG * TPB * 32], F32)
        vec = sb("vec", [P, 8, DC], F32)
        omt = sb("omt", [P, 3, DC], F32)
        ubk = sb("ubk", [P, DC], F32)
        ubw = sb("ubw", [P, DC], F32)
        nwd = sb("nwd", [P, DC], F32)
        so2 = sb("so2", [P, 1], F32)

        def place(start, *wanted):
            at[0] = start
            made = [sb(*w) for w in wanted]
            return made, at[0]

        region = at[0]
        (q_all, k_all, v_all), stage = place(
            region, ("q_all", [P, NG * GQ * T], BF16), ("k_all", [P, NG * T], BF16),
            ("v_all", [P, NG * TPB * 32], F32))
        (probs, v_now, o_cols), end = place(
            stage, ("probs", [P, 2, 10, T], F32), ("v_now", [P, 2, TPB, 32], F32),
            ("o_cols", [P, 2, T], F32))
        (kparts1,), _ = place(end - 2 * T * 4, ("kparts1", [64, 3, T], BF16))
        (negm, negr, m3, mrow, rsum), region_end = place(
            end, ("negm", [P, 2, TPB, GQ], F32), ("negr", [P, 2, TPB, GQ], F32),
            ("m3", [P, 2, TPB, 3, GQ], BF16), ("mrow", [3 * GQ, 2, T], BF16),
            ("rsum", [P, 2, TPB, GQ], F32))
        (xn0, cols0_hi, cols0_lo, w2b, wraw, qf), end = place(
            stage, ("xn0", [P, TPB, D], F32), ("cols0_hi", [P, DC, N], F32R),
            ("cols0_lo", [P, DC, N], F32R), ("w2b", [P, HC, D], F32),
            ("wraw", [P, 4, DC * D], F32), ("qf", [P, DC, T], F32))
        assert end <= region_end
        (qparts0, kf, kparts0, w2a), _ = place(
            region_end, ("qparts0", [P, 3, DC, T], BF16), ("kf", [64, T], F32),
            ("kparts0", [64, 3, T], BF16), ("w2a", [P, HC, D], F32))
        (qparts1,), _ = place(att_at, ("qparts1", [P, 3, DC, T], BF16))
        qparts, kparts = (qparts0, qparts1), (kparts0, kparts1)
        (w1hi, w3hi, w1lo, w3lo), half_q = place(
            region, ("w1hi", [P, DC, HID], F32R), ("w3hi", [P, DC, HID], F32R),
            ("w1lo", [P, DC, HID], F32R), ("w3lo", [P, DC, HID], F32R))
        (w1raw, w3raw), _ = place(half_q - 2 * DC * HID * 4, ("w1raw", [P, DC, HID], F32),
                                  ("w3raw", [P, DC, HID], F32))
        (cols_hi, cols_lo, rows, rwhi, rwlo, sg, hf, select_sb), end = place(
            half_q, ("cols_hi", [P, DC, N], F32R), ("cols_lo", [P, DC, N], F32R),
            ("rows", [P, TILES, D], F32), ("rwhi", [P, 4, DC, D], F32R),
            ("rwlo", [P, 4, DC, D], F32R), ("sg", [P, 2, T], F32), ("hf", [P, 2, T], F32),
            ("select_sb", [P, MC * P], BF16))
        assert end <= stage
        (rwraw,), _ = place(half_q + 4 * DC * N * 4, ("rwraw", [P, 4, DC, D], F32))
        (h_hi, h_lo), end = place(stage, ("h_hi", [P, 2, T], F32R), ("h_lo", [P, 2, T], F32R))
        mixing = end
        (xT, mix, mixed, m_hi, m_lo, ct, iota), end = place(
            mixing, ("xT", [P, DC, T + 8], F32), ("mix", [P, DC, T], F32),
            ("mixed", [P, 2, DC, T], F32), ("m_hi", [P, 3, DC, T], F32R),
            ("m_lo", [P, 3, DC, T], F32R), ("ct", [P, N], BF16),
            ("iota", [P, E], F32))
        (gate_hi, gate_lo, bo_sb), end = place(
            end, ("gate_hi", [P, DC, RW], F32R), ("gate_lo", [P, DC, RW], F32R),
            ("bo_sb", [P, D], F32))
        (logits, top8, topi, topf, wtop, wsum, comb, eq, cb), end = place(
            end, ("logits", [P, TILES, RW], F32), ("top8", [P, TILES, 8], F32),
            ("topi", [P, TILES, 8], U32), ("topf", [P, TILES, 8], F32),
            ("wtop", [P, TILES, TOPK + 1], F32), ("wsum", [P, TILES, 2], F32),
            ("comb", [P, TPB, E + 1], F32), ("eq", [P, TPB, TOPK, E], F32),
            ("cb", [P, TPB, P], BF16))
        (gate_raw, logits_t), end = place(end, ("gate_raw", [P, DC, RW], F32),
                                          ("logits_t", [RW, T], F32))
        (decay, gain), _ = place(mixing, ("decay", [P, DC, T], F32), ("gain", [P, DC, T], F32))
        (num, den), _ = place(mixing + DC * (T + 8 + T) * 4, ("num", [P, DC, T], F32),
                              ("den", [P, DC, T], F32))
        (mraw,), _ = place(wsg_at, ("mraw", [P, PLACES, 3 * D], F32))
        (mslot_hi, mslot_lo), end = place(region, ("mslot_hi", [P, PLACES, 3 * D], F32R),
                                          ("mslot_lo", [P, PLACES, 3 * D], F32R))
        assert end <= half_q

        ps = ctx.enter_context(nc.psum_tensor("ps", [P, 8, 512], F32))
        q_dram = nc.dram_tensor("q_parts_scratch", (3, D, N), BF16).ap()
        k_dram = nc.dram_tensor("k_parts_scratch", (3, 3 * NKV * HD, N), BF16).ap()

        x_rows = x.rearrange("(t p) d -> p t d", p=P)
        out_rows = out.rearrange("(t p) d -> p t d", p=P)

        s_x = [sem("x0_loaded"), sem("x1_loaded")]
        s_const = sem("consts_loaded")
        s_constb = sem("bf16_consts_loaded")
        s_w = sem("attn_weights_loaded")
        s_dve = sem("vector_order")
        s_pool = sem("pool_order")
        s_ready = sem("pool_constants_ready")
        ln_var = sem("ln_variance_ready")
        ln_rstd = sem("ln_rstd_ready")
        ln_rows = sem("ln_rows_ready")
        tr_done = sem("rows_transposed")
        hi_done = sem("cols_hi_ready")
        lo_done = sem("cols_lo_ready")
        s_abs = sem("weight_abs_sums_ready")
        s_tot = sem("weight_totals_ready")
        s_sign = sem("weight_signs_ready")
        s_scale = sem("weight_scales_ready")
        q_mm = sem("q_product_done")
        kv_mm = sem("kv_product_done")
        q_scaled = sem("q_scaled")
        k_scaled = sem("k_scaled")
        v_stored = sem("v_stored")
        q_split = sem("q_split")
        k_split = sem("k_split")
        q_spilled = sem("q_parts_in_dram")
        k_spilled = sem("k_parts_in_dram")
        q_in = [sem("q_even_group_loaded"), sem("q_odd_group_loaded")]
        k_in = [sem("k_batch0_loaded"), sem("k_batch1_loaded")]
        s1_full = sem("score_rows_full")
        s1_read = sem("score_rows_read")
        msplit = sem("max_split")
        mt_full = sem("max_rows_full")
        mrow_ready = sem("max_rows_ready")
        m_in = [sem("max_rows_even_loaded"), sem("max_rows_odd_loaded")]
        st_full = sem("score_cols_full")
        st_exp = sem("probs_ready")
        hidden = sem("future_keys_zeroed")
        v_ready = sem("v_group_ready")
        pv_done = sem("pv_done")
        o_copied = sem("o_copied")
        ot_full = sem("o_rows_full")
        att_ready = sem("att_rows_ready")
        s_w2 = sem("w2_loaded")
        butterfly = sem("w2_butterfly_done")
        w2_split = sem("w2_split")
        w2_mm = sem("w2_hadamard_done")
        w2_hi_done = sem("w2_hi_ready")
        w2_lo_done = sem("w2_lo_ready")
        s_vec = sem("vectors_loaded")
        s_post = [sem("w1_loaded"), sem("w3_loaded")]
        s_rw = sem("mix_weights_loaded")
        s_tail = sem("routing_weights_and_vectors_loaded")
        s_select = sem("select_loaded")
        w13_hi = sem("w1_w3_hi_ready")
        w13_lo = sem("w1_w3_lo_ready")
        rw_hi = sem("mix_weights_hi_ready")
        rw_lo = sem("mix_weights_lo_ready")
        gate_split = sem("routing_weights_split")
        z_done = sem("z_done")
        z_read = sem("z_scaled_and_added")
        x_new = sem("residual_ready")
        rows_ready = sem("rows_ready")
        cols_full = sem("cols_in_psum")
        cols_h = sem("cols_hi_done")
        cols_l = sem("cols_lo_done")
        up_g = sem("gate_product_done")
        up_u = sem("linear_product_done")
        silu_done = sem("silu_done")
        mul_done = sem("gated")
        h_hi_done = sem("hidden_hi_ready")
        h_lo_done = sem("hidden_lo_ready")
        down_done = sem("down_product_done")
        xt_ready = sem("xT_ready")
        xt_zero = sem("xT_start_zeroed")
        mix_tmp = sem("shifted_mix_ready")
        mix_done = sem("mix_ready")
        mix_silu = sem("receptance_silu_ready")
        mix_hi = sem("mix_hi_ready")
        mix_lo = sem("mix_lo_ready")
        proj_k = sem("key_projection_done")
        proj_v = sem("value_projection_done")
        proj_r = sem("receptance_projection_done")
        k_read = sem("key_projection_read")
        gain_done = sem("gain_ready")
        v_read = sem("value_projection_read")
        wkv_done = sem("wkv_ready")
        wkv_hi = sem("wkv_hi_ready")
        wkv_lo = sem("wkv_lo_ready")
        z_biased = sem("z_biased")
        logit_cols = sem("routing_logits_as_columns")
        logit_copied = sem("routing_logits_copied")
        route_mm = sem("routing_logits_as_rows")
        route_ex = sem("routing_exponent_ready")
        route_exp = sem("routing_exp_done")
        route_rows = sem("routing_rows_ready")
        route_t = sem("routing_transposed")
        route_cols = sem("routing_cols_ready")
        m_loaded = [sem(f"expert_chunk_loaded_{i}") for i in range(PLACES)]
        m_hi_ready = sem("expert_hi_ready")
        m_lo_ready = sem("expert_lo_ready")
        bc_full = sem("routing_broadcast_done")
        t_done = sem("hidden_product_done")
        s_out = sem("out_stored")

        UNITS = ([(3, h, 1) for h in range(4)] + [(2, h, 1) for h in range(4)]
                 + [(1, 0, 2), (1, 2, 2), (0, 0, 2), (0, 2, 2)])
        PIECES = ([[(0, h, 0)] for h in range(4)] + [[(1, h, 0), (3, h, 384)] for h in range(4)]
                  + [[(2, 0, 0), (2, 1, 256)], [(2, 2, 0), (2, 3, 256)]])
        WHERE = {(t, h): (u, c) for u, pieces in enumerate(PIECES) for t, h, c in pieces}
        SLOTS = NG + 4
        MT_AT, MROW_AT, OT_AT, DIV_AT, PV_AT, OC_AT = 3, 4, 1, 3, 7, 9
        FIRST, PAIRS = 4, 4

        def slots(eng, body, per=None):
            for n in range(FIRST):
                body(n, n % 2, n // 2)
            with (eng.Fori(0, PAIRS) if per is None else eng.loop(PAIRS, per)) as i:
                body(i * 2 + FIRST, 0, i + FIRST // 2)
                body(i * 2 + (FIRST + 1), 1, i + FIRST // 2)
            for n in range(FIRST + 2 * PAIRS, SLOTS):
                body(n, n % 2, n // 2)

        def has(n, lag):
            return not isinstance(n, int) or 0 <= n - lag < NG

        def col_bank(turn, b, k):
            return k if b == 0 and turn < 2 else 4 + 2 * b + k

        TURNS = {(0, 0): 0, (1, 0): 1, (0, 1): 2, (1, 1): 3, (3, 0): 4, (3, 1): 5}
        ALL_TURNS = {(0, 0): 0, (1, 0): 1, (0, 1): 2, (1, 1): 3, (2, 0): 4, (3, 0): 5,
                     (2, 1): 6, (3, 1): 7}
        NORMS = [(0, 0), (0, 1), (1, 0), (2, 0), (1, 1), (2, 1), (3, 0), (3, 1)]
        SCAN_AT, OUT_AT, COL_AT, ROUTE_AT = 4, 15, 18, 20

        SCAN_STEPS = [(0, 0), (1, 0), (0, 1), (0, 2), (0, 3), (1, 1), (0, 4), (1, 2), (1, 3),
                      (1, 4)]

        def z_bank(part, b):
            return 2 if part == 0 and b == 0 else 4 + 2 * b

        def z_tile(part, b, t):
            return ps[:, z_bank(part, b) + t // 2, (t % 2) * D:(t % 2 + 1) * D]

        block = ctx.enter_context(nc.Block())

        @block.sync
        def _(sp):
            for b in range(B):
                sp.dma_start(xa[:, b * TPB:(b + 1) * TPB, :],
                             x_rows[:, b * TPB:(b + 1) * TPB, :]).then_inc(s_x[b], 16)
                if b == 0:
                    sp.dma_start(ident[:], consts[:, 0:P]).then_inc(s_const, 16)
            for n, w in enumerate((wq, wk, wv, wo)):
                cols = w.shape[1]
                sp.dma_start(wraw[:, n, 0:DC * cols],
                             w.rearrange("(k p) o -> p k o", p=P)).then_inc(s_w, 16)
            sp.dma_start(w2a[:, :, :], w2.rearrange("(c p) d -> p c d", p=P)).then_inc(s_w2, 16)
            sp.dma_start(had[:, :], consts[:, 2 * P:3 * P]).then_inc(s_w2, 16)
            sp.dma_start(vec[:, :, :], vecs).then_inc(s_vec, 16)
            def spill(b):
                sp.wait_ge(k_split, b + 1)
                for i in range(3):
                    rows_i = slice(i * NKV * HD, (i + 1) * NKV * HD)
                    sp.dma_start(
                        k_dram[:, rows_i, b * T:(b + 1) * T].rearrange("j r t -> r j t"),
                        kparts[b][:, :, :]).then_inc(k_spilled, 16)
                sp.wait_ge(q_split, DC * (b + 1))
                for i in range(3):
                    sp.dma_start(
                        q_dram[i, :, b * T:(b + 1) * T].rearrange("(m p) t -> p m t", p=P),
                        qparts[b][:, i, :, :]).then_inc(q_spilled, 16)

            def load_k(b):
                sp.wait_ge(k_spilled, 48 * (b + 1))
                if b == 0:
                    sp.wait_ge(s_ready, 3)
                for j in range(3):
                    sp.dma_start(
                        k_all[24 * j:24 * j + 24, b * NKV * T:(b + 1) * NKV * T]
                        .rearrange("r (k t) -> r k t", k=NKV),
                        k_dram[j, :, b * T:(b + 1) * T]
                        .rearrange("(r k) t -> r k t", k=NKV)).then_inc(k_in[b], 16)

            def load_q(g, par, turn):
                need(sp, q_in[par], turn * 48)
                for j in range(3):
                    sp.dma_start(
                        q_all[24 * j:24 * j + 24, bass.ds(g * (GQ * T), GQ * T)]
                        .rearrange("r (h t) -> r h t", h=GQ),
                        q_dram[:, :, bass.ds(g // NKV * T, T)]
                        .rearrange("i (d h) t -> (i d) h t", d=HD)
                        [:, bass.ds(g % NKV * GQ, GQ), :]).then_inc(q_in[par], 16)

            spill(0)
            load_k(0)
            sp.wait_ge(q_spilled, 48)
            load_q(0, 0, 0)
            load_q(1, 1, 0)

            def slot(n, par, pair):
                if has(n, 1):
                    g = n - 1
                    need(sp, mrow_ready, g + 1)
                    for i in range(3):
                        sp.dma_start(
                            q_all[72 + i:73 + i, bass.ds(g * (GQ * T), GQ * T)]
                            .rearrange("o (h t) -> o h t", h=GQ),
                            mrow[GQ * i:GQ * i + GQ, par ^ 1, :]).then_inc(m_in[par ^ 1], 16)
                if isinstance(n, int) and n == 0:
                    spill(1)
                if isinstance(n, int) and n == 1:
                    load_k(1)
                if isinstance(n, int) and n == FIRST - 1:
                    sp.wait_ge(q_spilled, 48 * B)
                if not isinstance(n, int) or n + 2 < NG:
                    load_q(n + 2, par, pair + 1)
                after = n - (FIRST + 2 * PAIRS) if isinstance(n, int) else -1
                if after == 0:
                    sp.wait_ge(st_full, 10 * NKV)
                if 0 <= after < DC:
                    w, dst = ((w1, w1raw), (w3, w3raw))[after]
                    for k in range(DC):
                        sp.dma_start(dst[:, k, :], w[k * P:(k + 1) * P, :])\
                            .then_inc(s_post[after], 16)
                if after == DC:
                    sp.dma_start(rwraw[:, :, :, :], mix_w.rearrange("w (k p) o -> p w k o", p=P))\
                        .then_inc(s_rw, 16)
            slots(sp, slot)
            sp.wait_ge(att_ready, NG)
            sp.dma_start(gate_raw[:, :, :], route_w.rearrange("(k p) o -> p k o", p=P))\
                .then_inc(s_tail, 16)
            sp.dma_start(iota[:, :], consts[:, 3 * P:3 * P + E]).then_inc(s_tail, 16)
            sp.dma_start(bo_sb[:, :], bo.to_broadcast((P, D))).then_inc(s_tail, 16)

            sp.wait_ge(z_done, 2)

            def load_chunk(v, place):
                if not isinstance(v, int) or v >= PLACES:
                    sp.wait_ge(m_lo_ready, v - (PLACES - 1))
                elif v == 2:
                    sp.wait_ge(down_done, B * HC)
                sp.dma_start(mraw[:, place, :],
                             moe_w[bass.ds(v % MC, 1)].rearrange("o p f -> p (o f)"))\
                    .then_inc(m_loaded[place], 16)
            for v in range(PLACES):
                load_chunk(v, v)
            with sp.Fori(1, MC * B // PLACES) as i:
                for r in range(PLACES):
                    load_chunk(i * PLACES + r, r)
            for b in range(B):
                sp.wait_ge(x_new, 3 * B + b + 1)
                sp.dma_start(out_rows[:, b * TPB:(b + 1) * TPB, :],
                             xa[:, b * TPB:(b + 1) * TPB, :]).then_inc(s_out, 16)
            sp.wait_ge(s_out, 16 * B)

        @block.gpsimd
        def _(pool):
            chain = Chain(pool, s_pool)
            chain.step(pool.memset(zero[:], 0.0))
            chain.settle()
            none = zero[:, :, :].to_broadcast((P, TPB, GQ))
            pool.memset(ones[:], 1.0).then_inc(s_ready, 1)
            pool.memset(halfneg[:], -0.5).then_inc(s_ready, 1)
            pool.wait_ge(s_ready, 2)
            pool.dma_start(identb[:], consts[:, 0:P]).then_inc(s_constb, 16)
            pool.dma_start(hide_cols[:], consts[:, P:2 * P]).then_inc(s_constb, 16)

            def power(n):
                b = n if n < 2 else NORMS[n // 2 - 1][1] if n < 14 else n - 14
                h = slice(b * TPB, (b + 1) * TPB)
                pool.wait_ge(ln_var, n + 1)
                pool.tensor_tensor(rstd[:, h], ve[:, h], halfneg[:, h], ALU.pow)\
                    .then_inc(ln_rstd, 1)
            power(0)
            pool.wait_ge(ln_rstd, 1)
            pool.memset(k_all[64:96, :].bitcast(U32), 0x3F803F80).then_inc(s_ready, 1)
            pool.wait_ge(s_ready, 3)
            power(1)
            chain.step(pool.memset(v_all[:, :], 0.0))
            chain.settle()
            pool.memset(v_all[:, :].rearrange("p (a c) -> p a c", c=32)[:, :, HD:HD + 1],
                        1.0).then_inc(s_ready, 1)
            pool.wait_ge(s_ready, 4)
            pool.wait_ge(s_w2, 32)
            src, dst = w2a, w2b
            for width in (1, 2, 4):
                a4 = src[:, :, :].rearrange("p (n two w) d -> p n two (w d)", two=2, w=width)
                b4 = dst[:, :, :].rearrange("p (n two w) d -> p n two (w d)", two=2, w=width)
                chain.step(pool.tensor_tensor(b4[:, :, 0], a4[:, :, 0], a4[:, :, 1], ALU.add))
                ins = pool.tensor_tensor(b4[:, :, 1], a4[:, :, 0], a4[:, :, 1], ALU.subtract)
                if width < 4:
                    chain.step(ins)
                    chain.settle()
                else:
                    ins.then_inc(butterfly, 1)
                src, dst = dst, src
            pool.wait_ge(butterfly, 2)
            pool.tensor_tensor(w2lo[:, :, :], w2b[:, :, :], w2hi[:, :, :].bitcast(F32),
                               ALU.subtract).then_inc(butterfly, 1)

            def await_units(g, k, count):
                need(pool, st_exp, g * 10 + count)
                chain.step(pool.tensor_tensor(waited[:, k:k + 1], zero[:, :, 0], zero[:, :, 0],
                                              ALU.add))

            def hide(par, first, last, column, width):
                tiles = probs[:, par, first:last, :].rearrange("p u (b c) -> p (u b) c", c=width)
                tiles = tiles[:, :, column:column + P]
                pool.affine_select(
                    out=tiles, in_=tiles, compare_op=ALU.is_ge, fill=0.0, base=0,
                    pattern=[[0, GQ], [1, P]], channel_multiplier=-1).then_inc(hidden, 1)

            def slot(n, par, pair):
                if isinstance(n, int) and n == NG + 1:
                    power(2)
                if has(n, 2):
                    chain.settle()
                    await_units(n - 2, 0, 4)
                    hide(par, 0, 4, 0, T)
                    await_units(n - 2, 1, 8)
                    hide(par, 4, 8, 0, T)
                    hide(par, 4, 8, 3 * P, T)
                if has(n, 0):
                    g = n
                    need(pool, s1_read, g * 12 + 12)
                    need(pool, mt_full, g - 1)
                    chain.step(pool.tensor_tensor(m3[:, par, :, 0, :], negm[:, par, :, :],
                                                  none, ALU.add))
                    chain.settle()
                    chain.step(pool.tensor_tensor(negr[:, par, :, :], negm[:, par, :, :],
                                                  m3[:, par, :, 0, :], ALU.subtract))
                    chain.settle()
                    chain.step(pool.tensor_tensor(m3[:, par, :, 1, :], negr[:, par, :, :],
                                                  none, ALU.add))
                    chain.settle()
                    pool.tensor_tensor(m3[:, par, :, 2, :], negr[:, par, :, :],
                                       m3[:, par, :, 1, :], ALU.subtract).then_inc(msplit, 1)
                if has(n, 2):
                    await_units(n - 2, 2, 10)
                    hide(par, 8, 10, 0, T // 2)
                after = n - (FIRST + 2 * PAIRS) if isinstance(n, int) else -1
                if after in (0, 1):
                    pool.wait_ge(w2_hi_done, 2)
                    c = slice(after * HC // 2, (after + 1) * HC // 2)
                    pool.tensor_tensor(w2lo[:, c, :], w2a[:, c, :], w2hi[:, c, :].bitcast(F32),
                                       ALU.subtract).then_inc(w2_lo_done, 1)
                if after in (3, 4):
                    raw, hi, lo = ((w1raw, w1hi, w1lo), (w3raw, w3hi, w3lo))[after - 3]
                    pool.wait_ge(w13_hi, after - 2)
                    for k in range(DC):
                        pool.tensor_tensor(lo[:, k, :], raw[:, k, :], hi[:, k, :].bitcast(F32),
                                           ALU.subtract).then_inc(w13_lo, 1)
                if isinstance(n, int) and n == NG + 1:
                    power(3)
            slots(chain, slot, 12)
            power(4)
            power(5)
            pool.wait_ge(s_rw, 16)
            pool.wait_ge(pv_done, NG)
            pool.tensor_copy(rwhi[:, :, :, :], rwraw[:, :, :, :]).then_inc(rw_hi, 1)
            pool.wait_ge(rw_hi, 1)
            pool.tensor_tensor(rwlo[:, :, :, :], rwraw[:, :, :, :], rwhi[:, :, :, :].bitcast(F32),
                               ALU.subtract).then_inc(rw_lo, 1)
            pool.wait_ge(s_tail, 48)
            chain.step(pool.tensor_copy(gate_hi[:, :, :], gate_raw[:, :, :]))
            chain.settle()
            pool.tensor_tensor(gate_lo[:, :, :], gate_raw[:, :, :], gate_hi[:, :, :].bitcast(F32),
                               ALU.subtract).then_inc(gate_split, 1)
            pool.dma_start(select_sb[:, :], select).then_inc(s_select, 16)

            def mix_low(b, q):
                for k in range(DC):
                    pool.wait_ge(mix_hi, (3 * b + q) * DC + k + 1)
                    pool.tensor_tensor(m_lo[:, q, k, :], mixed[:, (3 * b + q) % 2, k, :],
                                       m_hi[:, q, k, :].bitcast(F32), ALU.subtract)\
                        .then_inc(mix_lo, 1)

            def chunk_low(v, place):
                pool.wait_ge(m_hi_ready, v + 1)
                pool.tensor_tensor(mslot_lo[:, place, :], mraw[:, place, :],
                                   mslot_hi[:, place, :].bitcast(F32), ALU.subtract)\
                    .then_inc(m_lo_ready, 1)

            power(6)
            power(7)
            for q in range(3):
                mix_low(0, q)
            for v in range(2):
                power(8 + v)
                chunk_low(v, v)
            power(10)
            power(11)
            for v in range(MC):
                chunk_low(v + 2, (v + 2) % PLACES)
                if v < 3:
                    mix_low(1, v)
                if v == OUT_AT:
                    power(12)
                if v == OUT_AT + 1:
                    power(13)
            for v in range(MC, MC + 2):
                chunk_low(v + 2, (v + 2) % PLACES)
            power(14)
            with pool.Fori(0, (MC - 2) // 4 - 1) as i:
                for r in range(4):
                    chunk_low(i * 4 + (MC + 4 + r), (MC + 4 + r) % PLACES)
            for v in range(2 * MC - 4, 2 * MC - 2):
                chunk_low(v + 2, (v + 2) % PLACES)
            power(15)

        @block.vector
        def _(dve):
            chain = Chain(dve, s_dve)

            def rows_of_batch(b):
                h = slice(b * TPB, (b + 1) * TPB)
                dve.wait_ge(ln_rstd, b + 1)
                chain.step(dve.scalar_tensor_tensor(nmr[:, h], mv[:, h, 0], -1.0, rstd[:, h],
                                                    ALU.mult, ALU.mult))
                chain.settle()
                if b >= 1:
                    dve.wait_ge(tr_done, 2 * b)
                for t in range(TPB):
                    u = b * TPB + t
                    dve.tensor_scalar(xn0[:, t, :], xa[:, u, :], rstd[:, u:u + 1], nmr[:, u:u + 1],
                                      ALU.mult, ALU.add).then_inc(ln_rows, 1)

            def cols_low(b):
                cs = slice(b * T, (b + 1) * T)
                for k in range(DC):
                    dve.wait_ge(hi_done, 2 * b + k + 1)
                    dve.tensor_tensor(cols0_lo[:, k, cs], ps[:, 2 * b + k, :],
                                      cols0_hi[:, k, cs].bitcast(F32), ALU.subtract)\
                        .then_inc(lo_done, 1)

            for b in range(B):
                h = slice(b * TPB, (b + 1) * TPB)
                dve.wait_ge(s_x[b], 16)
                for t in range(b * TPB, (b + 1) * TPB):
                    chain.step(dve.bn_stats(st6[:, t, :], xa[:, t, :]))
                chain.settle()
                for t in range(b * TPB, (b + 1) * TPB):
                    chain.step(dve.bn_aggr(mv[:, t, :], st6[:, t, :]))
                chain.settle()
                dve.tensor_scalar(ve[:, h], mv[:, h, 1], LN_EPS, None, ALU.add).then_inc(ln_var, 1)
                if b == 0:
                    rows_of_batch(0)
            dve.wait_ge(s_w, 64)
            for n in range(4):
                cols = DC * (64 if n in (1, 2) else D)
                dve.tensor_reduce(asum[:, n:n + 1], wraw[:, n, 0:cols], AX.X, ALU.add,
                                  apply_absolute_value=True).then_inc(s_abs, 1)
            cols_low(0)
            rows_of_batch(1)
            dve.wait_ge(s_tot, 1)
            for n in range(4):
                count = D * (64 if n in (1, 2) else D)
                chain.step(dve.tensor_scalar(wsc[:, n:n + 1], ps[:, 7, n:n + 1], 1.0 / count,
                                             QUANT_EPS, ALU.mult, ALU.max))
            chain.settle()
            dve.scalar_tensor_tensor(qsc[:, :], wsc[:, 0:1], float(np.float32(HD) ** -0.5),
                                     wsc[:, 1:2], ALU.mult, ALU.mult).then_inc(s_scale, 1)
            dve.wait_ge(s_vec, 16)
            chain.step(dve.tensor_tensor(so2[:, :], wsc[:, 3:4], wsc[:, 3:4], ALU.mult))
            for q, v in enumerate(MIXES):
                chain.step(dve.tensor_scalar(omt[:, q, :], vec[:, v, :], -1.0, 1.0,
                                             ALU.mult, ALU.add))
            chain.step(dve.tensor_tensor(ubk[:, :], vec[:, UK, :], vec[:, BK, :], ALU.add))
            chain.step(dve.tensor_scalar(nwd[:, :], vec[:, WD, :], -1.0, None, ALU.mult))
            chain.settle()
            dve.wait_ge(s_w2, 32)
            dve.tensor_copy(hadr[:, :], had[:, :]).then_inc(w2_split, 1)
            chain.step(dve.tensor_tensor(ubw[:, :], ubk[:, :], vec[:, WD, :], ALU.subtract))
            cols_low(1)

            def split_three(dst, src, done):
                chain.step(dve.tensor_copy(dst(0), src))
                chain.settle()
                chain.step(dve.tensor_tensor(src, src, dst(0), ALU.subtract))
                chain.settle()
                chain.step(dve.tensor_copy(dst(1), src))
                chain.settle()
                dve.tensor_tensor(dst(2), src, dst(1), ALU.subtract).then_inc(done, 1)

            for b in range(B):
                dve.wait_ge(k_scaled, b + 1)
                split_three(lambda i: kparts[b][:, i, :], kf[:, :], k_split)
                for m in range(DC):
                    dve.wait_ge(q_scaled, DC * b + m + 1)
                    split_three(lambda i: qparts[b][:, i, m, :], qf[:, m, :], q_split)
            def statistics(b, source):
                for t in range(TPB):
                    chain.step(dve.bn_stats(st6[:, b * TPB + t, :], source(t)))
                chain.settle()
                for t in range(TPB):
                    chain.step(dve.bn_aggr(mv[:, b * TPB + t, :], st6[:, b * TPB + t, :]))
                chain.settle()

            def out_stats(part, b):
                h = slice(b * TPB, (b + 1) * TPB)
                if part % 2 == 0:
                    dve.wait_ge(z_done, part + b + 1)
                elif part == 1:
                    dve.wait_ge(down_done, HC * (b + 1))
                else:
                    dve.wait_ge(down_done, HC * B + MC * (b + 1))
                if part == 2:
                    for pair in range(2):
                        dve.tensor_tensor(
                            rows[:, b * TPB + 2 * pair:b * TPB + 2 * pair + 2, :],
                            ps[:, z_bank(part, b) + pair, :].rearrange("p (t d) -> p t d", t=2),
                            bo_sb[:, :].unsqueeze(1).to_broadcast((P, 2, D)), ALU.add)\
                            .then_inc(z_biased, 1)
                    dve.wait_ge(z_biased, 2 * b + 2)
                    statistics(b, lambda t: rows[:, b * TPB + t, :])
                else:
                    statistics(b, lambda t: z_tile(part, b, t))
                if part == 0:
                    dve.tensor_scalar(ve[:, h], mv[:, h, 1], so2[:, 0:1], LN_EPS,
                                      ALU.mult, ALU.add).then_inc(ln_var, 1)
                else:
                    dve.tensor_scalar(ve[:, h], mv[:, h, 1], LN_EPS, None, ALU.add)\
                        .then_inc(ln_var, 1)

            def out_apply(part, b):
                old, new = ((xa, xb), (xb, xa))[part % 2]
                h = slice(b * TPB, (b + 1) * TPB)
                n = 2 + 2 * NORMS.index((part, b)) if part < 3 else 14 + b
                dve.wait_ge(ln_rstd, n + 1)
                if part == 0:
                    chain.step(dve.tensor_scalar(rstd[:, h], rstd[:, h], wsc[:, 3:4], None,
                                                 ALU.mult))
                    chain.settle()
                else:
                    dve.wait_ge(x_new, NORMS.index((part - 1, b)) + 1)
                chain.step(dve.scalar_tensor_tensor(nmrz[:, h], mv[:, h, 0], -1.0, rstd[:, h],
                                                    ALU.mult, ALU.mult))
                for t in range(b * TPB, (b + 1) * TPB):
                    z = rows[:, t, :] if part == 2 else z_tile(part, b, t - b * TPB)
                    dve.scalar_tensor_tensor(new[:, t, :], z, rstd[:, t:t + 1], old[:, t, :],
                                             ALU.mult, ALU.add).then_inc(z_read, 1)
                if part < 3:
                    dve.wait_ge(z_read, (NORMS.index((part, b)) + 1) * TPB)
                    statistics(b, lambda t: new[:, b * TPB + t, :])
                    dve.tensor_scalar(ve[:, h], mv[:, h, 1], LN_EPS, None, ALU.add)\
                        .then_inc(ln_var, 1)

            def in_apply(part, b):
                new = (xb, xa)[part % 2]
                h = slice(b * TPB, (b + 1) * TPB)
                dve.wait_ge(ln_rstd, 2 * NORMS.index((part, b)) + 4)
                chain.step(dve.scalar_tensor_tensor(nmr[:, h], mv[:, h, 0], -1.0, rstd[:, h],
                                                    ALU.mult, ALU.mult))
                chain.settle()
                for t in range(b * TPB, (b + 1) * TPB):
                    dve.tensor_scalar(rows[:, t, :], new[:, t, :], rstd[:, t:t + 1],
                                      nmr[:, t:t + 1], ALU.mult, ALU.add).then_inc(rows_ready, 1)

            def split_low(turn, b):
                for k in range(DC):
                    dve.wait_ge(cols_h, DC * TURNS[turn, b] + k + 1)
                    dve.tensor_tensor(cols_lo[:, k, b * T:(b + 1) * T],
                                      ps[:, col_bank(turn, b, k), :],
                                      cols_hi[:, k, b * T:(b + 1) * T].bitcast(F32),
                                      ALU.subtract).then_inc(cols_l, 1)

            def slot(n, par, pair):
                for u, (qt, h0, nh) in enumerate(UNITS):
                    if has(n, 0):
                        g = n
                        if u == 0:
                            need(dve, msplit, g - 1)
                        need(dve, s1_full, g * 12 + u + 1)
                        w = (qt + 1) * P
                        dve.tensor_reduce(
                            negm[:, par, qt, h0:h0 + nh],
                            ps[:, u % 4, 0:nh * w].rearrange("p (h t) -> p h t", h=nh),
                            AX.X, ALU.max, negate=True).then_inc(s1_read, 1)
                    if u == 2 and has(n, 2):
                        g = n - 2
                        need(dve, pv_done, g - 1)
                        dve.tensor_scalar(v_now[:, par, :, :].rearrange("p s c -> p (s c)"),
                                          v_all[:, bass.ds(g * (TPB * 32), TPB * 32)],
                                          1.0, None, ALU.mult).then_inc(v_ready, 1)
                    if u == MROW_AT and has(n, 1):
                        g = n - 1
                        need(dve, mt_full, g + 1)
                        need(dve, m_in[par ^ 1], (pair - 1 + par) * 48)
                        dve.tensor_copy(mrow[:, par ^ 1, :], mt_bank)\
                            .then_inc(mrow_ready, 1)
                    if u == DIV_AT and has(n, 4):
                        g = n - 4
                        need(dve, ot_full, g + 1)
                        o4 = ps[:, 7, :].rearrange("p (s h c) -> p s h c", s=TPB, h=GQ)
                        chain.step(dve.reciprocal(rsum[:, par, :, :], o4[:, :, :, HD]))
                        chain.settle()
                        dve.tensor_tensor(
                            att4[:, bass.ds(g // 4 * TPB, TPB), bass.ds(g % 4 * 32, 32)]
                            .rearrange("p s (h d) -> p s h d", h=GQ),
                            o4[:, :, :, 0:HD],
                            rsum[:, par, :, :].unsqueeze(3).to_broadcast((P, TPB, GQ, HD)),
                            ALU.mult).then_inc(att_ready, 1)
                if isinstance(n, int) and n == FIRST - 1:
                    dve.wait_ge(q_spilled, 48 * B)
                if isinstance(n, int) and n == NG:
                    split_low(0, 0)
                if isinstance(n, int) and n == NG + 1:
                    out_stats(0, 0)
                    out_apply(0, 0)
                if isinstance(n, int) and n == NG + 2:
                    in_apply(0, 0)
            mt_bank = ps[0:3 * GQ, 6, 0:T // 2].bitcast(BF16)
            att4 = att[:, :].rearrange("p (g s c) -> p (g s) c", s=TPB, c=4 * 32)
            slots(chain, slot, 2)

            split_low(1, 0)
            split_low(0, 1)

            def mlp_unit(u):
                par, bank = u % 2, 2 * (u % 2)
                dve.wait_ge(silu_done, u + 1)
                dve.wait_ge(up_u, u + 1)
                if u >= 2:
                    dve.wait_ge(h_hi_done, u - 1)
                dve.tensor_tensor(hf[:, par, :], sg[:, par, :], ps[:, bank + 1, :], ALU.mult)\
                    .then_inc(mul_done, 1)
                dve.wait_ge(h_hi_done, u + 1)
                if u >= 2:
                    dve.wait_ge(down_done, u - 1)
                dve.tensor_tensor(h_lo[:, par, :], hf[:, par, :], h_hi[:, par, :].bitcast(F32),
                                  ALU.subtract).then_inc(h_lo_done, 1)

            def mixes(b, q):
                for k in range(DC):
                    n = (3 * b + q) * DC + k
                    dve.wait_ge(mix_tmp, n + 1)
                    if n >= 2 * DC:
                        dve.wait_ge(mix_lo, n - 2 * DC + 1)
                    dve.scalar_tensor_tensor(
                        mixed[:, (3 * b + q) % 2, k, :], xT[:, k, 1:T + 1],
                        vec[:, MIXES[q], k:k + 1], mix[:, k, :], ALU.mult, ALU.add)\
                        .then_inc(mix_done, 1)

            def read_keys(b):
                dve.wait_ge(mix_done, 3 * (b + 1) * DC)
                for m in range(DC):
                    dve.wait_ge(proj_k, 2 * b + m + 1)
                    dve.tensor_scalar(decay[:, m, :], ps[:, 4 + 2 * b + m, :], ubk[:, m:m + 1],
                                      vec[:, WD, m:m + 1], ALU.add, ALU.max).then_inc(k_read, 1)
                    dve.tensor_scalar(gain[:, m, :], ps[:, 4 + 2 * b + m, :], ubw[:, m:m + 1],
                                      0.0, ALU.add, ALU.min).then_inc(k_read, 1)

            def scan(b, m, step):
                if step == 0:
                    dve.wait_ge(gain_done, 2 * b + m + 1)
                    dve.wait_ge(mix_lo, 3 * (b + 1) * DC)
                    dve.wait_ge(proj_v, 2 * b + m + 1)
                    dve.scalar_tensor_tensor(num[:, m, :], ps[:, 4 + 2 * b + m, :],
                                             vec[:, BV, m:m + 1], gain[:, m, :], ALU.add,
                                             ALU.mult).then_inc(v_read, 1)
                    chain.step(dve.tensor_tensor_scan(den[:, m, :], decay[:, m, :],
                                                      gain[:, m, :], 0.0, ALU.mult, ALU.add))
                    dve.wait_ge(v_read, 2 * b + m + 1)
                    chain.step(dve.tensor_tensor_scan(num[:, m, :], decay[:, m, :],
                                                      num[:, m, :], 0.0, ALU.mult, ALU.add))
                    chain.settle()
                elif step <= 2:
                    part = slice((step - 1) * T // 2, step * T // 2)
                    chain.step(dve.reciprocal(gain[:, m, part], den[:, m, part]))
                elif step == 3:
                    chain.settle()
                    chain.step(dve.tensor_tensor(num[:, m, :], num[:, m, :], gain[:, m, :],
                                                 ALU.mult))
                    chain.settle()
                    dve.wait_ge(proj_r, 2 * b + m + 1)
                    dve.scalar_tensor_tensor(den[:, m, :], ps[:, 4 + 2 * b + m, :],
                                             vec[:, BR, m:m + 1], num[:, m, :], ALU.add,
                                             ALU.mult).then_inc(wkv_done, 1)
                else:
                    dve.wait_ge(wkv_hi, 2 * b + m + 1)
                    dve.tensor_tensor(cols_lo[:, m, b * T:(b + 1) * T], den[:, m, :],
                                      cols_hi[:, m, b * T:(b + 1) * T].bitcast(F32),
                                      ALU.subtract).then_inc(wkv_lo, 1)

            def start_columns(b):
                if b >= 1:
                    dve.wait_ge(wkv_lo, DC * b)
                dve.memset(xT[:, :, 0:1], 0.0).then_inc(xt_zero, 1)

            dve.wait_ge(pv_done, NG)
            start_columns(0)
            for u in range(B * HC - 2):
                mlp_unit(u)
                if u == 1:
                    out_stats(0, 1)
                if u == 2:
                    out_apply(0, 1)
                if u == 3:
                    in_apply(0, 1)
                if u == 5:
                    split_low(1, 1)
                if u == HC - 1:
                    out_stats(1, 0)
                if u == HC:
                    out_apply(1, 0)
                    in_apply(1, 0)
                if 9 <= u < 12:
                    mixes(0, u - 9)
                if u == 12:
                    read_keys(0)
                if u == 13:
                    scan(0, 0, 0)
                    scan(0, 1, 0)
            for m, step in SCAN_STEPS[2:]:
                scan(0, m, step)
            start_columns(1)
            for u in range(B * HC - 2, B * HC):
                mlp_unit(u)
            out_stats(2, 0)
            out_apply(2, 0)
            in_apply(2, 0)
            out_stats(1, 1)
            split_low(3, 0)
            out_apply(1, 1)
            in_apply(1, 1)

            def route_top(b):
                h = slice(b * TPB, (b + 1) * TPB)
                dve.wait_ge(route_mm, b + 1)
                chain.step(dve.tensor_copy(
                    logits[:, h, :],
                    ps[:, 5 + 2 * b, 0:TPB * RW].rearrange("p (t c) -> p t c", c=RW)))
                chain.settle()
                for t in range(b * TPB, (b + 1) * TPB):
                    chain.step(dve.max(top8[:, t, :], logits[:, t, 0:E]))
                chain.settle()
                for t in range(b * TPB, (b + 1) * TPB):
                    chain.step(dve.max_index(topi[:, t, :], top8[:, t, :], logits[:, t, 0:E]))
                chain.step(dve.tensor_tensor(
                    wtop[:, h, 0:TOPK], top8[:, h, 0:TOPK],
                    top8[:, h, 0:1].to_broadcast((P, TPB, TOPK)), ALU.subtract))
                chain.step(dve.tensor_scalar(wtop[:, h, TOPK], logits[:, h, E], -1.0, None,
                                             ALU.mult))
                chain.settle()
                dve.tensor_copy(topf[:, h, :], topi[:, h, :]).then_inc(route_ex, 1)

            def route_weights(b):
                h = slice(b * TPB, (b + 1) * TPB)
                dve.wait_ge(route_exp, b + 1)
                dve.wait_ge(route_ex, b + 1)
                chain.step(dve.tensor_reduce(wsum[:, h, 0], wtop[:, h, 0:TOPK], AX.X, ALU.add))
                chain.step(dve.tensor_scalar(wsum[:, h, 1], wtop[:, h, TOPK], 1.0, None, ALU.add))
                chain.settle()
                chain.step(dve.reciprocal(wsum[:, h, :], wsum[:, h, :]))
                if b >= 1:
                    dve.wait_ge(route_t, b)
                chain.step(dve.memset(cb[:, :, :], 0.0))
                chain.settle()
                chain.step(dve.tensor_tensor(
                    wtop[:, h, 0:TOPK], wtop[:, h, 0:TOPK],
                    wsum[:, h, 0:1].to_broadcast((P, TPB, TOPK)), ALU.mult))
                shape = (P, TPB, TOPK, E)
                chain.step(dve.tensor_tensor(
                    eq[:, :, :, :], iota[:, :].unsqueeze(1).unsqueeze(1).to_broadcast(shape),
                    topf[:, h, 0:TOPK].unsqueeze(3).to_broadcast(shape), ALU.is_equal))
                chain.settle()
                chain.step(dve.tensor_tensor(
                    eq[:, :, :, :], eq[:, :, :, :],
                    wtop[:, h, 0:TOPK].unsqueeze(3).to_broadcast(shape), ALU.mult))
                chain.settle()
                chain.step(dve.tensor_reduce(
                    comb[:, :, 0:E], eq[:, :, :, :].rearrange("p t k e -> p t e k"), AX.X,
                    ALU.add))
                chain.step(dve.tensor_copy(comb[:, :, E], wsum[:, h, 1]))

            def route_split(b):
                for i in range(3):
                    chain.settle()
                    chain.step(dve.tensor_copy(cb[:, :, i * E:(i + 1) * E], comb[:, :, 0:E]))
                    if i == 2:
                        chain.settle()
                        dve.tensor_copy(cb[:, :, 3 * E + i], comb[:, :, E]).then_inc(route_rows, 1)
                    else:
                        chain.step(dve.tensor_copy(cb[:, :, 3 * E + i], comb[:, :, E]))
                        chain.settle()
                        chain.step(dve.tensor_tensor(comb[:, :, 0:E], comb[:, :, 0:E],
                                                     cb[:, :, i * E:(i + 1) * E], ALU.subtract))
                        chain.step(dve.tensor_tensor(comb[:, :, E], comb[:, :, E],
                                                     cb[:, :, 3 * E + i], ALU.subtract))

            def keep_route(b):
                dve.wait_ge(route_t, b + 1)
                dve.tensor_copy(ct[:, b * T:(b + 1) * T],
                                ps[:, 5 + 2 * b, 0:T // 2].bitcast(BF16)).then_inc(route_cols, 1)

            route_top(0)
            route_weights(0)
            route_split(0)
            keep_route(0)

            def expert_unit(v, r, par):
                u = v + HC * B
                dve.wait_ge(silu_done, u + 1)
                dve.wait_ge(up_u, u + 1)
                dve.tensor_tensor(sg[:, par, :], sg[:, par, :], ps[:, (3 * r + 1) % 4, :],
                                  ALU.mult).then_inc(t_done, 1)
                dve.wait_ge(t_done, v + 1)
                dve.wait_ge(bc_full, v + 1)
                dve.wait_ge(h_hi_done, u - 1)
                dve.tensor_tensor(hf[:, par, :], sg[:, par, :], ps[:, (3 * r + 2) % 4, :],
                                  ALU.mult).then_inc(mul_done, 1)
                dve.wait_ge(h_hi_done, u + 1)
                dve.wait_ge(down_done, u - 1)
                dve.tensor_tensor(h_lo[:, par, :], hf[:, par, :], h_hi[:, par, :].bitcast(F32),
                                  ALU.subtract).then_inc(h_lo_done, 1)

            for v in range(MC):
                expert_unit(v, v % 4, v % 2)
                if v < 3:
                    mixes(1, v)
                if v == 2:
                    read_keys(1)
                if SCAN_AT <= v < SCAN_AT + len(SCAN_STEPS):
                    scan(1, *SCAN_STEPS[v - SCAN_AT])
                if v == OUT_AT:
                    out_stats(2, 1)
                if v == OUT_AT + 1:
                    out_apply(2, 1)
                if v == OUT_AT + 2:
                    in_apply(2, 1)
                if v == COL_AT:
                    split_low(3, 1)
                if v == ROUTE_AT:
                    route_top(1)
                if v == ROUTE_AT + 1:
                    route_weights(1)
                if v == ROUTE_AT + 2:
                    route_split(1)
                if v == ROUTE_AT + 4:
                    keep_route(1)
            for v in range(MC, MC + 2):
                expert_unit(v, v % 4, v % 2)
            out_stats(3, 0)
            out_apply(3, 0)
            with dve.Fori(0, (MC - 2) // 4) as i:
                for r in range(4):
                    expert_unit(i * 4 + (MC + 2 + r), (MC + 2 + r) % 4, r % 2)
            out_stats(3, 1)
            out_apply(3, 1)

        @block.scalar
        def _(act):
            act.wait_ge(s_w, 64)
            for n in range(4):
                cols = DC * (64 if n in (1, 2) else D)
                act.activation(wsg[:, n, 0:cols], wraw[:, n, 0:cols], ACT.Sign)\
                    .then_inc(s_sign, 1)
            for b in range(B):
                cs = slice(b * T, (b + 1) * T)
                for k in range(DC):
                    act.wait_ge(tr_done, 2 * b + k + 1)
                    act.copy(cols0_hi[:, k, cs], ps[:, 2 * b + k, :]).then_inc(hi_done, 1)
            act.wait_ge(s_scale, 1)
            for b in range(B):
                act.wait_ge(kv_mm, 2 * b + 1)
                if b >= 1:
                    act.wait_ge(k_split, b)
                act.copy(kf[:, :], ps[0:64, 2 * b, :]).then_inc(k_scaled, 1)
                for m in range(DC):
                    act.wait_ge(q_mm, 2 * b + m + 1)
                    if b >= 1:
                        act.wait_ge(q_split, DC * (b - 1) + m + 1)
                    act.mul(qf[:, m, :], ps[:, 4 + 2 * b + m, :], qsc[:, 0:1])\
                        .then_inc(q_scaled, 1)
                act.wait_ge(kv_mm, 2 * b + 2)
                act.wait_ge(s_ready, 4)
                act.mul(v_all[:, :].rearrange("p (g s c) -> p s g c", g=NG, c=32)
                        [:, :, b * NKV:(b + 1) * NKV, 0:HD],
                        ps[:, 2 * b + 1, 0:TPB * 64]
                        .rearrange("p (s g d) -> p s g d", s=TPB, d=HD),
                        wsc[:, 2:3]).then_inc(v_stored, 1)

            act.wait_ge(butterfly, 1)
            act.copy(w2hi[:, :, :], w2b[:, :, :]).then_inc(butterfly, 1)

            def split_high(turn, b):
                for k in range(DC):
                    act.wait_ge(cols_full, DC * ALL_TURNS[turn, b] + k + 1)
                    act.copy(cols_hi[:, k, b * T:(b + 1) * T], ps[:, col_bank(turn, b, k), :])\
                        .then_inc(cols_h, 1)

            def shift(part, b):
                new = (xb, xa)[part % 2]
                if part < 3:
                    act.wait_ge(rows_ready, (NORMS.index((part, b)) + 1) * TPB)
                for t in range(b * TPB, (b + 1) * TPB):
                    if part == 3:
                        act.wait_ge(z_read, 3 * TILES + t + 1)
                    ins = act.activation(new[:, t, :], new[:, t, :], ACT.Identity,
                                         bias=nmrz[:, t:t + 1])
                ins.then_inc(x_new, 1)

            def slot(n, par, pair):
                for u in range(10):
                    if has(n, 2):
                        g = n - 2
                        if u == 0:
                            need(act, pv_done, g - 1)
                        need(act, st_full, g * 10 + u + 1)
                        act.activation(probs[:, par, u, :], ps[:, 4 + u % 2, :], ACT.Exp)\
                            .then_inc(st_exp, 1)
                    if u == OC_AT and has(n, 3):
                        g = n - 3
                        if isinstance(n, int) and n == 3:
                            act.wait_ge(k_spilled, 48 * B)
                        need(act, pv_done, g + 1)
                        need(act, ot_full, g - 1)
                        act.copy(o_cols[:, par ^ 1, :], ps[:, 7, :]).then_inc(o_copied, 1)
                if isinstance(n, int) and n == 0:
                    act.wait_ge(w2_mm, HC // 2)
                    act.mul(w2a[:, :, :],
                            ps[:, 4:8, :].rearrange("p b (c d) -> p (b c) d", d=D),
                            1.0 / 32).then_inc(w2_hi_done, 1)
                    act.wait_ge(w2_hi_done, 1)
                    act.copy(w2hi[:, :, :], w2a[:, :, :]).then_inc(w2_hi_done, 1)
                if isinstance(n, int) and n in (NG - 2, NG - 1):
                    raw, hi = ((w1raw, w1hi), (w3raw, w3hi))[n - NG + 2]
                    act.wait_ge(s_post[n - NG + 2], 16 * DC)
                    act.copy(hi[:, :, :], raw[:, :, :]).then_inc(w13_hi, 1)
                if isinstance(n, int) and n == NG:
                    split_high(0, 0)
            slots(act, slot)
            split_high(1, 0)
            split_high(0, 1)
            shift(0, 0)

            def silu(u, bank, par):
                act.wait_ge(up_g, u + 1)
                act.activation(sg[:, par, :], ps[:, bank, :], ACT.Silu).then_inc(silu_done, 1)

            def high(u, par):
                act.wait_ge(mul_done, u + 1)
                need(act, down_done, u - 1)
                act.copy(h_hi[:, par, :], hf[:, par, :]).then_inc(h_hi_done, 1)

            def columns(b):
                act.wait_ge(xt_zero, b + 1)
                for k in range(DC):
                    act.wait_ge(cols_full, DC * ALL_TURNS[2, b] + k + 1)
                    act.copy(xT[:, k, 1:T + 1], ps[:, col_bank(2, b, k), :]).then_inc(xt_ready, 1)

            def mixes(b, q):
                act.wait_ge(xt_ready, 2 * b + 2)
                at = (3 * b + q) % 2
                first = (3 * b + q) * DC
                for k in range(DC):
                    need(act, mix_done, first + k - 1)
                    act.mul(mix[:, k, :], xT[:, k, 0:T], omt[:, q, k:k + 1]).then_inc(mix_tmp, 1)
                if b >= 1:
                    act.wait_ge([proj_k, proj_v, proj_r][q], DC * b)
                for k in range(DC):
                    act.wait_ge(mix_done, first + k + 1)
                    if MIXES[q] == TMR:
                        act.activation(mixed[:, at, k, :], mixed[:, at, k, :], ACT.Silu)\
                            .then_inc(mix_silu, 1)
                        act.wait_ge(mix_silu, DC * b + k + 1)
                    act.copy(m_hi[:, q, k, :], mixed[:, at, k, :]).then_inc(mix_hi, 1)

            def copy_logits(b):
                act.wait_ge(logit_cols, b + 1)
                if b >= 1:
                    act.wait_ge(route_mm, b)
                act.copy(logits_t[:, :], ps[0:RW, 4 + 2 * b, :]).then_inc(logit_copied, 1)

            def exponents(b):
                for m in range(DC):
                    act.wait_ge(k_read, 4 * b + 2 * m + 2)
                    act.activation(decay[:, m, :], decay[:, m, :], ACT.Exp,
                                   bias=nwd[:, m:m + 1], scale=-1.0)
                    act.activation(gain[:, m, :], gain[:, m, :], ACT.Exp).then_inc(gain_done, 1)

            def wkv_high(b, m):
                act.wait_ge(wkv_done, 2 * b + m + 1)
                act.copy(cols_hi[:, m, b * T:(b + 1) * T], den[:, m, :]).then_inc(wkv_hi, 1)

            def chunk_high(v, place, turn):
                act.wait_ge(m_loaded[place], turn * 16 + 16)
                need(act, down_done, v + (B * HC - PLACES + 1) if not isinstance(v, int)
                     else max(v - PLACES, -2) + 1 + B * HC)
                act.copy(mslot_hi[:, place, :], mraw[:, place, :]).then_inc(m_hi_ready, 1)

            for u in range(B * HC - 2):
                par = u % 2
                need(act, mul_done, u - 1)
                silu(u, 2 * par, par)
                high(u, par)
                if u == 5:
                    split_high(1, 1)
                    shift(0, 1)
                if u == 9:
                    columns(0)
                    mixes(0, 0)
                if u == 10:
                    mixes(0, 1)
                if u == 11:
                    mixes(0, 2)
                    shift(1, 0)
                if u == 12:
                    exponents(0)
            for u in range(B * HC - 2, B * HC):
                act.wait_ge(mul_done, u - 1)
                silu(u, 2 * (u % 2), u % 2)
            wkv_high(0, 0)
            wkv_high(0, 1)
            for u in range(B * HC - 2, B * HC):
                high(u, u % 2)
            chunk_high(0, 0, 0)
            chunk_high(1, 1, 0)
            split_high(3, 0)
            copy_logits(0)

            def route(b):
                h = slice(b * TPB, (b + 1) * TPB)
                act.wait_ge(route_ex, b + 1)
                act.activation(wtop[:, h, :], wtop[:, h, :], ACT.Exp).then_inc(route_exp, 1)
            route(0)
            columns(1)
            shift(2, 0)
            shift(1, 1)

            def expert(u, r, par):
                act.wait_ge(mul_done, u - 1)
                silu(u, (3 * r) % 4, par)
                high(u, par)

            for v in range(MC):
                expert(v + HC * B, v % 4, v % 2)
                chunk_high(v + 2, (v + 2) % PLACES, (v + 2) // PLACES)
                if v < 3:
                    mixes(1, v)
                if v == 2:
                    exponents(1)
                if v in (SCAN_AT + 4, SCAN_AT + 8):
                    wkv_high(1, v == SCAN_AT + 8)
                if v == COL_AT:
                    split_high(3, 1)
                if v == COL_AT + 1:
                    copy_logits(1)
                    shift(2, 1)
                if v == ROUTE_AT:
                    route(1)
            for v in range(MC, MC + 2):
                expert(v + HC * B, v % 4, v % 2)
                chunk_high(v + 2, (v + 2) % PLACES, (v + 2) // PLACES)
            shift(3, 0)
            with act.Fori(0, (MC - 2) // 4 - 1) as i:
                for r in range(4):
                    expert(i * 4 + (HC * B + MC + 2 + r), (MC + 2 + r) % 4, r % 2)
                    chunk_high(i * 4 + (MC + 4 + r), (MC + 4 + r) % PLACES,
                               i + (MC + 4 + r) // PLACES)
            for v in range(2 * MC - 4, 2 * MC):
                expert(v + HC * B, v % 4, v % 2)
                if v + 2 < 2 * MC:
                    chunk_high(v + 2, (v + 2) % PLACES, (v + 2) // PLACES)
            shift(3, 1)

        @block.tensor
        def _(pe):
            pe.wait_ge(s_ready, 1)
            pe.wait_ge(s_abs, 4)
            pe.matmul(ps[:, 7, 0:4], ones[:, :], asum[:, :], start=True, stop=True)\
                .then_inc(s_tot, 1)
            pe.wait_ge(s_const, 16)
            pe.wait_ge(s_constb, 32)
            for b in range(B):
                for k in range(DC):
                    for t in range(TPB):
                        pe.wait_ge(ln_rows, b * TPB + t + 1)
                        mm = pe.transpose(ps[:, 2 * b + k, t * P:(t + 1) * P],
                                          xn0[:, t, k * P:(k + 1) * P], ident[:, :])
                    mm.then_inc(tr_done, 1)
            pe.wait_ge(s_sign, 4)
            pe.wait_ge(s_scale, 1)
            for b in range(B):
                cs = slice(b * T, (b + 1) * T)
                pe.wait_ge(lo_done, 2 * b + 2)
                parts = [(k, c) for k in range(DC) for c in (cols0_hi, cols0_lo)]
                for n, (k, c) in enumerate(parts):
                    mm = pe.matmul(ps[0:64, 2 * b, :], wsg[:, 1, k * 64:(k + 1) * 64],
                                   c[:, k, cs], start=(n == 0), stop=(n == 3))
                mm.then_inc(kv_mm, 1)
                for m in range(DC):
                    for n, (k, c) in enumerate(parts):
                        mm = pe.matmul(ps[:, 4 + 2 * b + m, :],
                                       wsg[:, 0, k * D + m * P:k * D + (m + 1) * P],
                                       c[:, k, cs], start=(n == 0), stop=(n == 3))
                    mm.then_inc(q_mm, 1)
                for t in range(TPB):
                    ts = slice(b * T + t * P, b * T + (t + 1) * P)
                    for n, (k, c) in enumerate(parts):
                        mm = pe.matmul(ps[:, 2 * b + 1, t * 64:(t + 1) * 64], c[:, k, ts],
                                       wsg[:, 2, k * 64:(k + 1) * 64],
                                       start=(n == 0), stop=(n == 3))
                mm.then_inc(kv_mm, 1)
            pe.wait_ge(q_scaled, 2 * B)
            pe.wait_ge(v_stored, B)

            def score_rows(g, u):
                qt, h0, nh = UNITS[u]
                need(pe, s1_read, g * 12 + u - 3)
                w = (qt + 1) * P
                for h in range(h0, h0 + nh):
                    c = (h - h0) * w
                    pe.matmul(ps[:, u % 4, c:c + w],
                              q_all[0:72, bass.ds(g * (GQ * T) + (h * T + qt * P), P)],
                              k_all[0:72, bass.ds(g * T, w)], start=True, stop=False)
                    mm = pe.matmul(ps[:, u % 4, c + w - P:c + w], identb[:, :], hide_cols[:, :],
                                   start=False, stop=True)
                mm.then_inc(s1_full, 1)

            def score_cols(g, u):
                need(pe, st_exp, g * 10 + u - 1)
                for kt, h, c in PIECES[u]:
                    w = T - kt * P
                    mm = pe.matmul(ps[:, 4 + u % 2, c:c + w],
                                   k_all[0:75, bass.ds(g * T + kt * P, P)],
                                   q_all[0:75, bass.ds(g * (GQ * T) + (h * T + kt * P), w)],
                                   start=True, stop=True)
                mm.then_inc(st_full, 1)


            def transposes(turn, b, tile):
                for k in range(DC):
                    for t in range(TPB):
                        mm = pe.transpose(ps[:, col_bank(turn, b, k), t * P:(t + 1) * P],
                                          tile(t, k), ident[:, :])
                    mm.then_inc(cols_full, 1)

            def rows_tile(b):
                return lambda t, k: rows[:, b * TPB + t, k * P:(k + 1) * P]

            att_v = att[:, :].rearrange("p (b k s c) -> p b k s c", b=B, k=DC, c=P)

            def att_tile(b):
                return lambda t, k: att_v[:, b, k, t, :]

            def out_product(b):
                pe.wait_ge(cols_l, DC * TURNS[0, b] + DC)
                for t in range(TPB):
                    ts = slice(b * T + t * P, b * T + (t + 1) * P)
                    for n, (k, c) in enumerate((k, c) for k in range(DC)
                                               for c in (cols_hi, cols_lo)):
                        mm = pe.matmul(z_tile(0, b, t), c[:, k, ts],
                                       wsg[:, 3, k * D:(k + 1) * D],
                                       start=(n == 0), stop=(n == 2 * DC - 1))
                mm.then_inc(z_done, 1)

            def three_passes(out, lhs_hi, lhs_lo, rhs_hi, rhs_lo, first, last):
                pe.matmul(out, lhs_hi, rhs_hi, start=first, stop=False)
                pe.matmul(out, lhs_lo, rhs_hi, start=False, stop=False)
                return pe.matmul(out, lhs_hi, rhs_lo, start=False, stop=last)

            def down(part, b, u, par, w_hi, w_lo, start):
                pe.wait_ge(h_lo_done, u + 1)
                for t in range(TPB):
                    ts = slice(t * P, (t + 1) * P)
                    pairs = ((h_hi, w_hi), (h_lo, w_hi), (h_hi, w_lo))
                    for n, (h, w) in enumerate(pairs):
                        mm = pe.matmul(z_tile(part, b, t), h[:, par, ts], w,
                                       start=start and n == 0 and t % 2 == 0, stop=False,
                                       skip_group_check=True)
                return mm

            mt_bank = ps[0:3 * GQ, 6, 0:T // 2].bitcast(BF16)

            def slot(n, par, pair):
                if has(n, 2):
                    need(pe, m_in[par], pair * 48)
                if isinstance(n, int) and n == SLOTS - 1:
                    pe.wait_ge(rows_ready, TPB)
                    transposes(1, 0, rows_tile(0))
                for u in range(12):
                    if has(n, 0):
                        g = n
                        if u == 0:
                            need(pe, q_in[par], pair * 48 + 48)
                            for b in range(B):
                                if not isinstance(g, int) or g // NKV == b:
                                    pe.wait_ge(k_in[b], 48)
                        score_rows(g, u)
                    if has(n, 2) and 1 <= u <= 10:
                        score_cols(n - 2, u - 1)
                    if u == MT_AT and has(n, 1):
                        g = n - 1
                        if isinstance(n, int) and n == 1:
                            pe.wait_ge(w2_hi_done, 1)
                        need(pe, msplit, g + 1)
                        need(pe, mrow_ready, g)
                        for s in range(TPB):
                            mm = pe.transpose(mt_bank[:, s * P:(s + 1) * P],
                                              m3[:, par ^ 1, s, :, :].rearrange("p i h -> p (i h)"),
                                              identb[:, :])
                        mm.then_inc(mt_full, 1)
                    if u == OT_AT and has(n, 4):
                        g = n - 4
                        need(pe, o_copied, g + 1)
                        for s in range(TPB):
                            mm = pe.transpose(ps[:, 7, s * P:(s + 1) * P],
                                              o_cols[:, par, s * P:(s + 1) * P], ident[:, :])
                        mm.then_inc(ot_full, 1)
                    if isinstance(n, int) and n == 0 and u == 6:
                        pe.wait_ge(butterfly, 3)
                        pe.wait_ge(w2_split, 1)
                        for c in range(4):
                            for j, half in enumerate((w2hi, w2lo)):
                                mm = pe.matmul(
                                    ps[:, 4 + c, :], hadr[:, :],
                                    half[:, 2 * c:2 * c + 2, :].rearrange("p c d -> p (c d)"),
                                    start=(j == 0), stop=(j == 1))
                            mm.then_inc(w2_mm, 1)
                    if isinstance(n, int) and n == NG and u == 2:
                        pe.wait_ge(att_ready, NKV)
                        pe.wait_ge(s1_read, 12 * NG)
                        transposes(0, 0, att_tile(0))
                    if isinstance(n, int) and n == NG + 1 and u == 2:
                        out_product(0)
                    if PV_AT <= u < PV_AT + TPB and has(n, 3):
                        g, kt = n - 3, u - PV_AT
                        if kt == 0:
                            need(pe, att_ready, g)
                            need(pe, v_ready, g + 1)
                            need(pe, hidden, g * 4 + 4)
                        for h in range(GQ):
                            un, c = WHERE[kt, h]
                            mm = pe.matmul(ps[32 * h:32 * h + 32, 7, kt * P:T],
                                           v_now[:, par ^ 1, kt, :],
                                           probs[:, par ^ 1, un, c:c + T - kt * P],
                                           start=(kt == 0), stop=(kt == TPB - 1))
                        if kt == TPB - 1:
                            mm.then_inc(pv_done, 1)

            def mlp_up(u):
                b, j, bank = u // HC, u % HC, 2 * (u % 2)
                cs = slice(b * T, (b + 1) * T)
                js = slice(j * P, (j + 1) * P)
                for w, (hi, lo) in enumerate(((w1hi, w1lo), (w3hi, w3lo))):
                    need(pe, silu_done if w == 0 else mul_done, u - 1)
                    for k in range(DC):
                        mm = three_passes(ps[:, bank + w, :], hi[:, k, js], lo[:, k, js],
                                          cols_hi[:, k, cs], cols_lo[:, k, cs],
                                          k == 0, k == DC - 1)
                    mm.then_inc(up_u if w else up_g, 1)

            def mlp_down(u):
                b, j = u // HC, u % HC
                if j == 0:
                    pe.wait_ge(z_read, (b + 1) * TPB)
                mm = down(1, b, u, u % 2, w2hi[:, j, :], w2lo[:, j, :], j == 0)
                mm.then_inc(down_done, 1)

            slots(pe, slot)
            pe.wait_ge(att_ready, NG)
            transposes(0, 1, att_tile(1))
            pe.wait_ge(w13_lo, 2 * DC)
            pe.wait_ge(cols_l, DC * TURNS[1, 0] + DC)
            pe.wait_ge(pv_done, NG)

            def project(b, q, w, bank, done):
                pe.wait_ge(mix_lo, (3 * b + q + 1) * DC)
                for m in range(DC):
                    ms = slice(m * P, (m + 1) * P)
                    for k in range(DC):
                        mm = three_passes(ps[:, bank + m, :], rwhi[:, w, k, ms],
                                          rwlo[:, w, k, ms], m_hi[:, q, k, :],
                                          m_lo[:, q, k, :], k == 0, k == DC - 1)
                    mm.then_inc(done, 1)

            def keys(b):
                pe.wait_ge(rw_lo, 1)
                pe.wait_ge(xt_ready, 2 * b + 2)
                project(b, 0, 0, 4 + 2 * b, proj_k)

            def values(b):
                pe.wait_ge(k_read, 4 * b + 4)
                project(b, 1, 1, 4 + 2 * b, proj_v)

            def receptances(b):
                pe.wait_ge(v_read, 2 * b + 2)
                project(b, 2, 2, 4 + 2 * b, proj_r)

            def mix_out(b):
                for k, t in [(0, 0), (0, 1), (0, 2), (0, 3), (1, 0), (1, 1), (1, 2), (1, 3)]:
                    if k == 0 and t % 2 == 0:
                        pe.wait_ge(wkv_lo, DC * b + t // 2 + 1)
                    ts = slice(b * T + t * P, b * T + (t + 1) * P)
                    pairs = ((cols_hi, rwhi), (cols_lo, rwhi), (cols_hi, rwlo))
                    for n, (c, w) in enumerate(pairs):
                        mm = pe.matmul(z_tile(2, b, t), c[:, k, ts], w[:, 3, k, :],
                                       start=k == 0 and n == 0 and t % 2 == 0,
                                       stop=k == DC - 1 and n == 2, skip_group_check=True)
                mm.then_inc(z_done, 1)

            def logits_of(b):
                pe.wait_ge(gate_split, 1)
                pe.wait_ge(cols_l, DC * TURNS[3, b] + DC)
                cs = slice(b * T, (b + 1) * T)
                for k in range(DC):
                    mm = three_passes(ps[0:RW, 4 + 2 * b, :], gate_hi[:, k, :], gate_lo[:, k, :],
                                      cols_hi[:, k, cs], cols_lo[:, k, cs], k == 0, k == DC - 1)
                mm.then_inc(logit_cols, 1)

            def logit_rows(b):
                pe.wait_ge(logit_copied, b + 1)
                for t in range(TPB):
                    mm = pe.transpose(ps[:, 5 + 2 * b, t * RW:(t + 1) * RW],
                                      logits_t[:, t * P:(t + 1) * P], ident[0:RW, 0:RW])
                mm.then_inc(route_mm, 1)

            def route_columns(b):
                pe.wait_ge(route_rows, b + 1)
                for t in range(TPB):
                    mm = pe.transpose(
                        ps[:, 5 + 2 * b, 0:T // 2].bitcast(BF16)[:, t * P:(t + 1) * P],
                        cb[:, t, :], identb[:, :])
                mm.then_inc(route_t, 1)

            def expert_up(v, r, b, chunk):
                u = v + HC * B
                cs = slice(b * T, (b + 1) * T)
                pe.wait_ge(m_lo_ready, v + 1)
                for w in range(2):
                    if w == 0:
                        pe.wait_ge(mul_done, u - 1)
                    else:
                        pe.wait_ge(silu_done, u)
                    for k in range(DC):
                        c = w * D + k * P
                        mm = three_passes(ps[:, (3 * r + w) % 4, :],
                                          mslot_hi[:, r, c:c + P], mslot_lo[:, r, c:c + P],
                                          cols_hi[:, k, cs], cols_lo[:, k, cs],
                                          k == 0, k == DC - 1)
                    mm.then_inc(up_u if w else up_g, 1)
                need(pe, t_done, v)
                if isinstance(v, int) and v == 0:
                    route_columns(0)
                if isinstance(chunk, int) and chunk == 0:
                    pe.wait_ge(route_cols, b + 1)
                pe.matmul(ps[:, (3 * r + 2) % 4, :], select_sb[:, bass.ds(chunk * P, P)],
                          ct[:, cs], start=True, stop=True).then_inc(bc_full, 1)

            def expert_down(v, r, b, start=False):
                par = r % 2
                down(3, b, v + HC * B, par, mslot_hi[:, r, 2 * D:3 * D],
                     mslot_lo[:, r, 2 * D:3 * D], start).then_inc(down_done, 1)

            mlp_up(0)
            out_product(1)
            pe.wait_ge(w2_lo_done, 2)
            for u in range(1, B * HC):
                if u == HC:
                    pe.wait_ge(cols_l, DC * TURNS[1, 1] + DC)
                mlp_up(u)
                if u == B * HC - 1:
                    mix_out(0)
                if u == 10:
                    pe.wait_ge(rows_ready, 3 * TPB)
                    transposes(2, 0, rows_tile(0))
                mlp_down(u - 1)
                if u == 5:
                    pe.wait_ge(rows_ready, 2 * TPB)
                    transposes(1, 1, rows_tile(1))
                if u == 12:
                    keys(0)
                if u == 13:
                    values(0)
                if u == 14:
                    receptances(0)
            mlp_down(B * HC - 1)
            pe.wait_ge(rows_ready, 4 * TPB)
            transposes(3, 0, rows_tile(0))
            logits_of(0)
            logit_rows(0)
            pe.wait_ge(rows_ready, 5 * TPB)
            transposes(2, 1, rows_tile(1))
            pe.wait_ge(s_select, 16)

            expert_up(0, 0, 0, 0)
            for v in range(1, MC):
                expert_up(v, v % 4, 0, v)
                expert_down(v - 1, (v - 1) % 4, 0, start=v == 1)
                if v == 2:
                    keys(1)
                if v == 3:
                    values(1)
                if v == SCAN_AT + 2:
                    receptances(1)
                if v == SCAN_AT + 10:
                    mix_out(1)
                if v == COL_AT:
                    pe.wait_ge(rows_ready, 6 * TPB)
                    transposes(3, 1, rows_tile(1))
                if v == COL_AT + 1:
                    logits_of(1)
                if v == COL_AT + 2:
                    logit_rows(1)
                if v == ROUTE_AT + 4:
                    route_columns(1)
            pe.wait_ge(cols_l, DC * TURNS[3, 1] + DC)
            for v in range(MC, MC + 2):
                expert_up(v, v % 4, 1, v - MC)
                expert_down(v - 1, (v - 1) % 4, 0 if v == MC else 1, start=v == MC + 1)
            with pe.Fori(0, (MC - 2) // 4) as i:
                for r in range(4):
                    q = (MC + 2 + r) % 4
                    expert_up(i * 4 + (MC + 2 + r), q, 1, i * 4 + (2 + r))
                    expert_down(i * 4 + (MC + 1 + r), (q + 3) % 4, 1)
            expert_down(2 * MC - 1, (2 * MC - 1) % 4, 1)


def kernel(**inputs):
    import numpy as _np
    import concourse.bacc as _bacc
    from concourse import mybir as _mybir
    from concourse.bass_utils import run_bass_kernel_spmd as _run

    a = {n: _np.asarray(v) for n, v in inputs.items()}

    def turned(w):
        return _np.ascontiguousarray(w.T)

    def by_part(w, heads):
        return _np.ascontiguousarray(
            w.reshape(D, heads, HD).transpose(0, 2, 1).reshape(D, heads * HD))

    def chunked(experts, shared):
        flat = _np.concatenate([
            experts.transpose(1, 0, 2).reshape(D, E * F), shared,
            _np.zeros((D, MC * P - E * F - SF), shared.dtype)], axis=1)
        return flat.reshape(DC, P, MC, P).transpose(2, 1, 0, 3).reshape(MC, P, D)

    place = _np.arange(P)
    had = _np.ones((1, 1), _np.float32)
    while had.shape[0] < P:
        had = _np.block([[had, had], [had, -had]])
    hide = _np.where(place[None, :] > place[:, None], _np.float32(MASKED), _np.float32(0))
    consts = _np.concatenate([
        _np.eye(P), hide, had, _np.tile(_np.arange(E), (P, 1))], axis=1)
    feature = _np.arange(MC * P)
    select = _np.zeros((P, MC * P), _np.float32)
    for part in range(3):
        of_expert = feature < E * F
        select[part * E + feature[of_expert] // F, feature[of_expert]] = 1.0
        select[3 * E + part, E * F:E * F + SF] = 1.0

    moe = _np.concatenate([
        chunked(a["L1_ffn_wg"], a["L1_ffn_sg"]), chunked(a["L1_ffn_wu"], a["L1_ffn_su"]),
        _np.concatenate([
            a["L1_ffn_wd"].reshape(E * F, D), a["L1_ffn_sd"],
            _np.zeros((MC * P - E * F - SF, D), _np.float32)]).reshape(MC, P, D)], axis=2)
    vecs = _np.stack([a["L1_attn_" + n] for n in ("tmr", "tmk", "tmv", "u", "w", "bk", "bv", "br")])
    arrays = {
        "x": a["L0_attn_x"].reshape(N, D),
        "consts": consts.astype(_np.float32),
        "wq": by_part(a["L0_attn_wq"].T, NKV * GQ), "wk": by_part(a["L0_attn_wk"].T, NKV),
        "wv": turned(a["L0_attn_wv"]), "wo": turned(a["L0_attn_wo"]),
        "w1": turned(a["L0_ffn_W1"]), "w3": turned(a["L0_ffn_W3"]), "w2": turned(a["L0_ffn_W2"]),
        "mix_w": _np.stack([a["L1_attn_W" + n].T for n in "kvro"]),
        "vecs": vecs.reshape(8, DC, P).transpose(2, 0, 1),
        "bo": a["L1_attn_bo"].reshape(1, D),
        "route_w": _np.concatenate([
            a["L1_ffn_gate_w"], a["L1_ffn_seg"], _np.zeros((D, RW - E - 1), _np.float32)], axis=1),
        "moe_w": moe,
        "select": select,
    }
    nc = _bacc.Bacc("TRN2", target_bir_lowering=False, num_devices=1)
    aps, named = [], {}
    for name, v in arrays.items():
        v = _np.ascontiguousarray(v)
        named[f"in_{name}"] = v
        aps.append(nc.dram_tensor(f"in_{name}", v.shape, _mybir.dt.from_np(v.dtype),
                                  kind="ExternalInput").ap())
    aps.append(nc.dram_tensor("out_x", (N, D), _mybir.dt.float32, kind="ExternalOutput").ap())
    sandwich_kernel(nc, *aps)
    r = _run(nc, [named], core_ids=[0])
    return r.results[0]["out_x"].reshape(B, T, D)
```
